# Optimizing a Trainium2 kernel written in Bass

```python
import numpy as np
import jax
import jax.numpy as jnp

def _softmax(x, axis=-1):
    return jax.nn.softmax(x, axis=axis)

def _gelu(x):
    return jax.nn.gelu(x, approximate=True)

def _silu(x):
    return jax.nn.silu(x)

def _sigmoid(x):
    return jax.nn.sigmoid(x)

def _layernorm(x, axis=-1, eps=1e-05):
    m = jnp.mean(x, axis=axis, keepdims=True)
    v = jnp.var(x, axis=axis, keepdims=True)
    return (x - m) / jnp.sqrt(v + eps)

def _scatter_add(tgt, idx, src, axis=0):
    return tgt.at[idx].add(src)

def _segment_sum(src, seg, n):
    return jax.ops.segment_sum(src, seg, n)
kernel_name = 'mk_vit_tower_cls_d2_tok_img512_r4_559c61'

def setup_inputs(seed: int=0):
    np.random.seed(seed)
    _w = jnp.asarray

    def _rec_inputs():
        import jax
        import jax.numpy as jnp
        _rk = jax.random.key(seed)
        x = -0.000477451 + 1.00034 * jax.random.normal(jax.random.fold_in(_rk, 1), (8, 32, 32, 29), jnp.float32)
        cls_tok = 0.02 * jax.random.normal(jax.random.fold_in(_rk, 5), (1, 1, 128), jnp.float32)
        return (x, cls_tok)
    x, cls_tok = _rec_inputs()

    def _L0_tok_setup():
        import jax, jax.numpy as jnp
        import numpy as np
        import math
        H, W_DIM, D_MODEL, B = (32, 32, 128, 128)
        F_TOTAL = 29
        SEQ_LEN = H * W_DIM

        def make_pe(seq_len: int, d_model: int) -> jnp.ndarray:
            position = np.arange(seq_len, dtype=np.float32)[:, None]
            div_term = np.exp(np.arange(0, d_model, 2, dtype=np.float32) * (-math.log(10000.0) / d_model))
            pe = np.zeros((seq_len, d_model), dtype=np.float32)
            pe[:, 0::2] = np.sin(position * div_term)
            pe[:, 1::2] = np.cos(position * div_term)
            return jnp.asarray(pe)
        key = jax.random.key(seed)
        k1, k2 = jax.random.split(key)
        state_tensor = jax.random.normal(k1, (B, H, W_DIM, F_TOTAL), dtype=jnp.float32)
        W = jax.random.normal(k2, (F_TOTAL, D_MODEL), dtype=jnp.float32) * 0.05
        return {'state_tensor': state_tensor, 'W': W}
    _L0_tok_all = _L0_tok_setup()
    _L0_tok_in = {k: v for k, v in _L0_tok_all.items() if k in ('W',)}
    del _L0_tok_all

    def _L0_attn_setup():
        import jax, jax.numpy as jnp
        import numpy as np
        B, S, D = (8, 256, 128)
        K, H = (64, 8)
        key = jax.random.key(seed)
        ks = jax.random.split(key, 8)
        s = lambda fan_in: 1.0 / np.sqrt(fan_in)
        return {'x': jax.random.normal(ks[0], (B, S, D), dtype=jnp.float32), 'Wq': jax.random.uniform(ks[1], (D, K * H), jnp.float32, -s(D), s(D)), 'Wk': jax.random.uniform(ks[2], (D, K * H), jnp.float32, -s(D), s(D)), 'Wv': jax.random.uniform(ks[3], (D, D * H), jnp.float32, -s(D), s(D)), 'Wo': jax.random.uniform(ks[4], (D * H, D), jnp.float32, -s(D * H), s(D * H)), 'bo': jax.random.uniform(ks[5], (D,), jnp.float32, -s(D * H), s(D * H)), 'gamma': jnp.ones((D,), jnp.float32), 'beta': jnp.zeros((D,), jnp.float32)}
    _L0_attn_all = _L0_attn_setup()
    _L0_attn_in = {k: v for k, v in _L0_attn_all.items() if k in ('Wq', 'Wk', 'Wv', 'Wo', 'bo', 'gamma', 'beta')}
    del _L0_attn_all

    def _L0_ffn_setup():
        import jax, jax.numpy as jnp
        import numpy as np
        N_DIM = 128
        HEADS = 8
        NUM_EXPERTS = 16384
        NUM_KEYS = 64
        DIM_KEY = 64
        TOPK = 16
        SCALE = 0.02
        key = jax.random.key(seed)
        k0, k1, k2, k3, k4 = jax.random.split(key, 5)
        x = jax.random.normal(k0, (1, 512, N_DIM), dtype=jnp.float32)
        W_q = jax.random.normal(k1, (N_DIM, 2 * HEADS * DIM_KEY), dtype=jnp.float32) * SCALE
        keys = jax.random.normal(k2, (HEADS, NUM_KEYS, 2, DIM_KEY), dtype=jnp.float32) * SCALE
        down_embed = jax.random.normal(k3, (NUM_EXPERTS, N_DIM), dtype=jnp.float32) * SCALE
        up_embed = jax.random.normal(k4, (NUM_EXPERTS, N_DIM), dtype=jnp.float32) * SCALE
        return {'x': x, 'W_q': W_q, 'keys': keys, 'down_embed': down_embed, 'up_embed': up_embed}
    _L0_ffn_all = _L0_ffn_setup()
    _L0_ffn_in = {k: v for k, v in _L0_ffn_all.items() if k in ('W_q', 'keys', 'down_embed', 'up_embed')}
    del _L0_ffn_all

    def _L1_attn_setup():
        import jax, jax.numpy as jnp
        import numpy as np
        SCALE = 64 ** 0.5
        key = jax.random.key(seed)
        kx, kw = jax.random.split(key)
        B, S, D, O = (8, 512, 128, 128)
        x = jax.random.normal(kx, (B, S, D), dtype=jnp.float32)
        kernel = jax.random.normal(kw, (3, D, O), dtype=jnp.float32) * 0.02
        return {'x': x, 'kernel': kernel}
    _L1_attn_all = _L1_attn_setup()
    _L1_attn_in = {k: v for k, v in _L1_attn_all.items() if k in ('kernel',)}
    del _L1_attn_all

    def _L1_ffn_setup():
        import jax, jax.numpy as jnp
        import numpy as np
        D_MODEL = 128
        N_HEADS = 8
        KV_OPTS = (8, 4, 1)
        D_K = D_MODEL // N_HEADS

        def gqa(x, wq, wk, wv, wo, n_kv):
            B, S, _ = x.shape
            groups = N_HEADS // n_kv
            q = (x @ wq).reshape(B, S, N_HEADS, D_K).transpose(0, 2, 1, 3)
            k = (x @ wk).reshape(B, S, n_kv, D_K).transpose(0, 2, 1, 3)
            v = (x @ wv).reshape(B, S, n_kv, D_K).transpose(0, 2, 1, 3)
            k = jnp.repeat(k, groups, axis=1)
            v = jnp.repeat(v, groups, axis=1)
            scores = jnp.einsum('bhqd,bhkd->bhqk', q, k) / jnp.sqrt(jnp.float32(D_K))
            attn = jax.nn.softmax(scores, axis=-1)
            out = jnp.einsum('bhqk,bhkd->bhqd', attn, v)
            out = out.transpose(0, 2, 1, 3).reshape(B, S, D_MODEL)
            return out @ wo
        key = jax.random.key(seed)
        ks = jax.random.split(key, 32)
        it = iter(ks)
        s = 0.02
        inp = {'x': jax.random.normal(next(it), (64, 256, D_MODEL), dtype=jnp.float32)}
        inp['r_w1'] = jax.random.normal(next(it), (D_MODEL, D_MODEL // 4), jnp.float32) * s
        inp['r_b1'] = jnp.zeros((D_MODEL // 4,), jnp.float32)
        inp['r_w2'] = jax.random.normal(next(it), (D_MODEL // 4, len(KV_OPTS)), jnp.float32) * s
        inp['r_b2'] = jnp.zeros((len(KV_OPTS),), jnp.float32)
        for i, nkv in enumerate(KV_OPTS):
            inp[f'wq{i}'] = jax.random.normal(next(it), (D_MODEL, D_MODEL), jnp.float32) * s
            inp[f'wk{i}'] = jax.random.normal(next(it), (D_MODEL, nkv * D_K), jnp.float32) * s
            inp[f'wv{i}'] = jax.random.normal(next(it), (D_MODEL, nkv * D_K), jnp.float32) * s
            inp[f'wo{i}'] = jax.random.normal(next(it), (D_MODEL, D_MODEL), jnp.float32) * s
        return inp
    _L1_ffn_all = _L1_ffn_setup()
    _L1_ffn_in = {k: v for k, v in _L1_ffn_all.items() if k in ('r_w1', 'r_b1', 'r_w2', 'r_b2', 'wq0', 'wk0', 'wv0', 'wo0', 'wq1', 'wk1', 'wv1', 'wo1', 'wq2', 'wk2', 'wv2', 'wo2')}
    del _L1_ffn_all
    return {'x': x, 'cls_tok': cls_tok, 'L0_tok_W': _L0_tok_in['W'], 'L0_attn_Wq': _L0_attn_in['Wq'], 'L0_attn_Wk': _L0_attn_in['Wk'], 'L0_attn_Wv': _L0_attn_in['Wv'], 'L0_attn_Wo': _L0_attn_in['Wo'], 'L0_attn_bo': _L0_attn_in['bo'], 'L0_attn_gamma': _L0_attn_in['gamma'], 'L0_attn_beta': _L0_attn_in['beta'], 'L0_ffn_W_q': _L0_ffn_in['W_q'], 'L0_ffn_keys': _L0_ffn_in['keys'], 'L0_ffn_down_embed': _L0_ffn_in['down_embed'], 'L0_ffn_up_embed': _L0_ffn_in['up_embed'], 'L1_attn_kernel': _L1_attn_in['kernel'], 'L1_ffn_r_w1': _L1_ffn_in['r_w1'], 'L1_ffn_r_b1': _L1_ffn_in['r_b1'], 'L1_ffn_r_w2': _L1_ffn_in['r_w2'], 'L1_ffn_r_b2': _L1_ffn_in['r_b2'], 'L1_ffn_wq0': _L1_ffn_in['wq0'], 'L1_ffn_wk0': _L1_ffn_in['wk0'], 'L1_ffn_wv0': _L1_ffn_in['wv0'], 'L1_ffn_wo0': _L1_ffn_in['wo0'], 'L1_ffn_wq1': _L1_ffn_in['wq1'], 'L1_ffn_wk1': _L1_ffn_in['wk1'], 'L1_ffn_wv1': _L1_ffn_in['wv1'], 'L1_ffn_wo1': _L1_ffn_in['wo1'], 'L1_ffn_wq2': _L1_ffn_in['wq2'], 'L1_ffn_wk2': _L1_ffn_in['wk2'], 'L1_ffn_wv2': _L1_ffn_in['wv2'], 'L1_ffn_wo2': _L1_ffn_in['wo2']}

def reference(x, cls_tok, L0_tok_W, L0_attn_Wq, L0_attn_Wk, L0_attn_Wv, L0_attn_Wo, L0_attn_bo, L0_attn_gamma, L0_attn_beta, L0_ffn_W_q, L0_ffn_keys, L0_ffn_down_embed, L0_ffn_up_embed, L1_attn_kernel, L1_ffn_r_w1, L1_ffn_r_b1, L1_ffn_r_w2, L1_ffn_r_b2, L1_ffn_wq0, L1_ffn_wk0, L1_ffn_wv0, L1_ffn_wo0, L1_ffn_wq1, L1_ffn_wk1, L1_ffn_wv1, L1_ffn_wo1, L1_ffn_wq2, L1_ffn_wk2, L1_ffn_wv2, L1_ffn_wo2):
    import jax
    import jax.numpy as jnp

    def _L0_tok_ref(state_tensor, W):
        import jax, jax.numpy as jnp
        import numpy as np
        import math
        H, W_DIM, D_MODEL, B = (32, 32, 128, 128)
        F_TOTAL = 29
        SEQ_LEN = H * W_DIM

        def make_pe(seq_len: int, d_model: int) -> jnp.ndarray:
            position = np.arange(seq_len, dtype=np.float32)[:, None]
            div_term = np.exp(np.arange(0, d_model, 2, dtype=np.float32) * (-math.log(10000.0) / d_model))
            pe = np.zeros((seq_len, d_model), dtype=np.float32)
            pe[:, 0::2] = np.sin(position * div_term)
            pe[:, 1::2] = np.cos(position * div_term)
            return jnp.asarray(pe)
        b, h, w, f = state_tensor.shape
        s = h * w
        x = state_tensor.reshape(b, s, f)
        emb = jnp.einsum('bsf,fd->bsd', x, W)
        pe = make_pe(s * 2, W.shape[1])[:s]
        return emb + pe[None, :, :]

    def _L0_attn_ref(x, Wq, Wk, Wv, Wo, bo, gamma, beta):
        import jax, jax.numpy as jnp
        import numpy as np
        B, S, D = (8, 256, 128)
        K, H = (64, 8)
        b, s, d = x.shape
        q = (x @ Wq).reshape(b, s, H, K)
        k = (x @ Wk).reshape(b, s, H, K)
        v = (x @ Wv).reshape(b, s, H, D)
        scores = jnp.einsum('bqhk,bshk->hbqs', q, k) / np.sqrt(K).astype(np.float32)
        scores = jnp.where(scores == 0, jnp.float32(-1000000000.0), scores)
        att = jax.nn.softmax(scores, axis=-1)
        o = jnp.einsum('hbqs,bshd->bqhd', att, v).reshape(b, s, H * D)
        o = o @ Wo + bo
        y = o + x
        mu = jnp.mean(y, axis=-1, keepdims=True)
        var = jnp.mean(jnp.square(y - mu), axis=-1, keepdims=True)
        return (y - mu) * jax.lax.rsqrt(var + 1e-06) * gamma + beta

    def _L0_ffn_ref(x, W_q, keys, down_embed, up_embed):
        import jax, jax.numpy as jnp
        import numpy as np
        N_DIM = 128
        HEADS = 8
        NUM_EXPERTS = 16384
        NUM_KEYS = 64
        DIM_KEY = 64
        TOPK = 16
        SCALE = 0.02
        b, n, d = x.shape
        q = (x @ W_q).reshape(b, n, 2, HEADS, DIM_KEY).transpose(2, 0, 1, 3, 4)
        sim = jnp.einsum('pbnhd,hkpd->pbnhk', q, keys)
        sx, ix = jax.lax.top_k(sim[0], TOPK)
        sy, iy = jax.lax.top_k(sim[1], TOPK)
        all_scores = (sx[..., :, None] + sy[..., None, :]).reshape(b, n, HEADS, TOPK * TOPK)
        scores, pk_idx = jax.lax.top_k(all_scores, TOPK)
        w_down = down_embed[pk_idx]
        w_up = up_embed[pk_idx]
        h = jnp.einsum('bnd,bnhkd->bnhk', x, w_down)
        h = jax.nn.gelu(h, approximate=False)
        h = jax.nn.softmax(scores, axis=-1) * h
        return jnp.einsum('bnhk,bnhkd->bnd', h, w_up)

    def _L1_attn_ref(x, kernel):
        import jax, jax.numpy as jnp
        import numpy as np
        SCALE = 64 ** 0.5
        WQ = jnp.einsum('bsd,do->bso', x, kernel[0])
        WK = jnp.einsum('bsd,do->bso', x, kernel[1])
        WV = jnp.einsum('bsd,do->bso', x, kernel[2])
        QK = jnp.einsum('bso,bto->bst', WQ, WK)
        row_sums = jnp.sum(QK, axis=2)
        c0 = jnp.argmin(row_sums[0])
        A = jax.nn.softmax(QK / SCALE, axis=-1)
        row_mask = (jnp.arange(QK.shape[1]) == c0)[None, :, None]
        A = jnp.where(row_mask, jnp.zeros((), A.dtype), A)
        V = jnp.einsum('bst,bto->bso', A, WV)
        return V

    def _L1_ffn_ref(x, r_w1, r_b1, r_w2, r_b2, wq0, wk0, wv0, wo0, wq1, wk1, wv1, wo1, wq2, wk2, wv2, wo2):
        import jax, jax.numpy as jnp
        import numpy as np
        D_MODEL = 128
        N_HEADS = 8
        KV_OPTS = (8, 4, 1)
        D_K = D_MODEL // N_HEADS

        def gqa(x, wq, wk, wv, wo, n_kv):
            B, S, _ = x.shape
            groups = N_HEADS // n_kv
            q = (x @ wq).reshape(B, S, N_HEADS, D_K).transpose(0, 2, 1, 3)
            k = (x @ wk).reshape(B, S, n_kv, D_K).transpose(0, 2, 1, 3)
            v = (x @ wv).reshape(B, S, n_kv, D_K).transpose(0, 2, 1, 3)
            k = jnp.repeat(k, groups, axis=1)
            v = jnp.repeat(v, groups, axis=1)
            scores = jnp.einsum('bhqd,bhkd->bhqk', q, k) / jnp.sqrt(jnp.float32(D_K))
            attn = jax.nn.softmax(scores, axis=-1)
            out = jnp.einsum('bhqk,bhkd->bhqd', attn, v)
            out = out.transpose(0, 2, 1, 3).reshape(B, S, D_MODEL)
            return out @ wo
        routing_input = x.mean(axis=1)
        logits = jax.nn.relu(routing_input @ r_w1 + r_b1) @ r_w2 + r_b2
        sel = jnp.argmax(jax.nn.softmax(logits, axis=-1), axis=-1)
        params = [(wq0, wk0, wv0, wo0), (wq1, wk1, wv1, wo1), (wq2, wk2, wv2, wo2)]
        out = jnp.zeros_like(x)
        for i, nkv in enumerate(KV_OPTS):
            yi = gqa(x, *params[i], nkv)
            mask = (sel == i)[:, None, None]
            out = jnp.where(mask, yi, out)
        return out
    h = _L0_tok_ref(x, L0_tok_W)
    h = jnp.concatenate([jnp.broadcast_to(cls_tok, (h.shape[0], 1, h.shape[2])), h], axis=1)
    h = h + _L0_attn_ref(_layernorm(h, axis=-1), L0_attn_Wq, L0_attn_Wk, L0_attn_Wv, L0_attn_Wo, L0_attn_bo, L0_attn_gamma, L0_attn_beta)
    h = h + _L0_ffn_ref(_layernorm(h, axis=-1), L0_ffn_W_q, L0_ffn_keys, L0_ffn_down_embed, L0_ffn_up_embed)
    h = h + _L1_attn_ref(_layernorm(h, axis=-1), L1_attn_kernel)
    h = h + _L1_ffn_ref(_layernorm(h, axis=-1), L1_ffn_r_w1, L1_ffn_r_b1, L1_ffn_r_w2, L1_ffn_r_b2, L1_ffn_wq0, L1_ffn_wk0, L1_ffn_wv0, L1_ffn_wo0, L1_ffn_wq1, L1_ffn_wk1, L1_ffn_wv1, L1_ffn_wo1, L1_ffn_wq2, L1_ffn_wk2, L1_ffn_wv2, L1_ffn_wo2)
    return h

_drawn_inputs = setup_inputs


def setup_inputs(seed=0):
    import zlib

    import numpy as np

    out = dict(_drawn_inputs(seed))
    spreads = {'L0_attn_gamma': (1.0, 0.2),
     'L0_attn_beta': (0.0, 0.1),
     'L1_ffn_r_b1': (0.0, 0.1),
     'L1_ffn_r_b2': (0.0, 0.1)}
    factors = {'cls_tok': 2.802,
     'L0_attn_Wq': 6.747,
     'L0_attn_Wk': 6.945,
     'L0_attn_bo': 4.723,
     'L0_ffn_W_q': 8.0,
     'L0_ffn_keys': 8.0,
     'L0_ffn_down_embed': 8.0,
     'L0_ffn_up_embed': 8.0,
     'L1_ffn_wq1': 8.0,
     'L1_ffn_wk1': 8.0,
     'L1_ffn_wv1': 4.75,
     'L1_ffn_wo1': 4.34}
    for name, (base, spread) in spreads.items():
        noise = np.random.default_rng([zlib.crc32(name.encode()), seed]).standard_normal(out[name].shape)
        drawn = base * np.exp(spread * noise) if base else spread * noise
        out[name] = jnp.asarray(drawn.astype(out[name].dtype))
    for name, factor in factors.items():
        out[name] = (out[name] * factor).astype(out[name].dtype)
    return out
```

```python
import math
from contextlib import ExitStack

import numpy as np

import concourse.bass as bass
from concourse import mybir

FP32 = mybir.dt.float32
I32 = mybir.dt.int32
ALU = mybir.AluOpType
ACT = mybir.ActivationFunctionType
AX = mybir.AxisListType.X
ds = bass.ds

B = 8
SEQ = 1025
F = 29
D = 128
H0, K0 = 8, 64
NE_HEADS, NKEYS, DKEY, TOPK = 8, 64, 64, 16
H1, K1 = 8, 16
KV_OPTS = (8, 4, 1)
RH = D // 4

T = 114
NT = 9
SP = T * NT
CH = 342
NC = SP // CH
LAST = SEQ - (NT - 1) * T
BANK = 512

RUN = [TOPK // (i + 1) for i in range(TOPK)]
START = [sum(RUN[:i]) for i in range(TOPK)]
NCAND = sum(RUN)
SINGLES = next(i for i in range(TOPK) if RUN[i] == 1)
REMOVED = -3.0e38
TH = NT * NE_HEADS

UNITS = H0 * NT
CHUNKS = H0 * NC
RANK0 = 2048

LN_EPS = 1e-5
POST_EPS = 1e-6
MASKED = -1.0e9


def vit_kernel(nc, x, cls_tok, W, Wq, Wk, Wv, Wo, bo, gamma, beta, W_q, keys, down, up, qkv,
               r_w1, r_b1, r_w2, r_b2, wq, wk, wv, wo, pe, out):
    ctx = ExitStack()
    with ctx:
        def sb(name, shape, dt=FP32):
            return ctx.enter_context(nc.sbuf_tensor(name, shape, dt))

        def signal(name):
            return ctx.enter_context(nc.semaphore(name))

        ps = ctx.enter_context(nc.psum_tensor("ps", [128, 8 * BANK], FP32))

        def banks(first, n, p, w):
            return ps[0:p, first * BANK:(first + n) * BANK].rearrange("p (n w) -> p n w", n=n)[:, :, 0:w]

        ident = sb("ident", [128, 128])
        sum_row = sb("sum_row", [128, 128])
        ones_row = sb("ones_row", [128, 1])
        ones1 = sb("ones1", [1, 128])
        rank_i = sb("rank_i", [T, NT], I32)
        rank = sb("rank", [T, NT])
        base = sb("base", [T, NT, D])
        w_tok = sb("w_tok", [F, D])
        w_q0 = sb("w_q0", [D, H0 * K0])
        w_k0 = sb("w_k0", [D, H0 * K0])
        w_v0 = sb("w_v0", [D, H0 * D])
        w_o0 = sb("w_o0", [D, H0, D])
        bo_t = sb("bo_t", [T, D])
        gamma_t = sb("gamma_t", [T, D])
        beta_t = sb("beta_t", [T, D])
        w_sim = sb("w_sim", [D, 2 * NE_HEADS * NKEYS])
        w_down = sb("w_down", [D, NCAND])
        w_up = sb("w_up", [NCAND, D])
        w_a1 = sb("w_a1", [D, 3, D])
        rw1 = sb("rw1", [D, RH])
        rb1 = sb("rb1", [RH, 1])
        rw2 = sb("rw2", [RH, 3])
        rb2 = sb("rb2", [1, 3])
        QKV = 640
        w_all = sb("w_all", [D, 3, QKV])
        wo_all = sb("wo_all", [128, 3, 2, D])
        w_sel = sb("w_sel", [D, QKV])
        wo_sel = sb("wo_sel", [128, 2, D])

        xin = sb("xin", [T, NT, F])
        xinT = sb("xinT", [F, SP])
        h = sb("h", [T, NT, D])
        xn = sb("xn", [T, NT, D])
        xnT = sb("xnT", [D, SP])
        y = sb("y", [T, NT, D])
        stats = sb("stats", [T, NT, 6])
        mv = sb("mv", [T, NT, 2])
        rst = sb("rst", [T, 4, NT])
        big = sb("big", [128, 17424])
        ring = sb("ring", [T, 3, SP])
        mring = sb("mring", [T, 3, SP])
        small = sb("small", [128, 64])
        rowmax = sb("rowmax", [T, UNITS])
        rowsum = sb("rowsum", [T, UNITS])
        rrec = sb("rrec", [T, UNITS])
        stage = sb("stage", [128, 2048])
        pt = sb("pt", [T, 2, NT * CH])
        oT = sb("oT", [D, 2, CH])

        qT = big[:, 0:4 * SP].rearrange("p (n s) -> p n s", n=4)
        kT = big[:, 4 * SP:8 * SP].rearrange("p (n s) -> p n s", n=4)
        v0 = big[0:T, 8 * SP:8 * SP + NT * H0 * D].rearrange("p (t n) -> p t n", t=NT)
        NTOP = NT * 2 * NE_HEADS * TOPK
        o = 0
        top = big[0:T, o:o + NTOP].rearrange("p (t s h k) -> p t s h k", t=NT, s=2, h=NE_HEADS)
        o += NTOP
        cand = big[0:T, o:o + TH * NCAND].rearrange("p (g c) -> p g c", g=TH)
        o += TH * NCAND
        left = big[0:T, o:o + TH * NCAND].rearrange("p (g c) -> p g c", g=TH)
        o += TH * NCAND
        prob = big[0:T, o:o + TH * NCAND].rearrange("p (g c) -> p g c", g=TH)
        o += TH * NCAND
        best = big[0:T, o:o + TH * TOPK].rearrange("p (g k) -> p g k", g=TH)
        o += TH * TOPK
        simw = pt[:, 0, 0:2 * NE_HEADS * NKEYS].rearrange("p (g k) -> p g k", k=NKEYS)
        assert o <= 17424
        wexp = pt[:, 1, 0:NT * NCAND].rearrange("p (t c) -> p t c", t=NT)
        hexp = pt[:, 1, 512:512 + NT * NCAND].rearrange("p (t c) -> p t c", t=NT)
        wexpT = stage[0:NCAND, 0:SP]
        q1T = big[:, 0:SP]
        k1T = big[:, SP:2 * SP]
        v1 = big[0:T, 2 * SP:2 * SP + NT * D].rearrange("p (t n) -> p t n", t=NT)
        pt1 = pt[:, :, 0:SP].rearrange("p r (k q) -> p r k q", k=NT)
        q2T = big[:, 0:2 * SP].rearrange("p (g s) -> p g s", g=2)
        k2T = big[:, 2 * SP:4 * SP].rearrange("p (g s) -> p g s", g=2)
        v2 = big[0:T, 4 * SP:4 * SP + NT * 256].rearrange("p (t h c) -> p t h c", t=NT, h=H1)
        o = 4 * SP + NT * 256
        o2T = big[:, o:o + 2 * SP].rearrange("p (g s) -> p g s", g=2)
        o += 2 * SP
        m3 = big[0:T, o:o + 216].rearrange("p (g t c j) -> p g t c j", g=2, t=NT, c=NC)
        o += 216
        mpad = big[0:T, o:o + 2 * NT * 128].rearrange("p (g t m) -> p g t m", g=2, t=NT)
        o += 2 * NT * 128
        assert o <= 17424
        p2 = ring[:, :, 0:2 * CH].rearrange("p r (j q) -> p r j q", j=2)

        loaded = signal("loaded")
        cls_loaded = signal("cls_loaded")
        pool_setup = signal("pool_setup")
        dve_setup = signal("dve_setup")
        setup_T = signal("setup_T")
        setup_copied = signal("setup_copied")
        setup_sim = signal("setup_sim")
        setup_done = signal("setup_done")
        go_pool, go_act, go_dve, go_pe = (signal("go_" + e) for e in ("pool", "act", "dve", "pe"))
        x_loaded = signal("x_loaded")
        xT_ps = signal("xT_ps")
        xT_ready = signal("xT_ready")
        tok_ready = signal("tok_ready")
        xn_ready = signal("xn_ready")
        xnT_ps = signal("xnT_ps")
        xnT_ready = signal("xnT_ready")
        NPROJ = 8 + NT
        proj_ready = signal("proj_ready")
        proj_act = signal("proj_act")
        proj_dve = signal("proj_dve")
        score_ps = signal("score_ps")
        score_sb = signal("score_sb")
        fill_ready = signal("fill_ready")
        masked = signal("masked")
        prob_ready = signal("prob_ready")
        probT_ps = signal("probT_ps")
        probT_sb = signal("probT_sb")
        pv_done = signal("pv_done")
        oT_ready = signal("oT_ready")
        oproj_done = signal("oproj_done")
        y_added = signal("y_added")
        sim_ps = signal("sim_ps")
        sim_read = signal("sim_read")
        hexp_ps = signal("hexp_ps")
        gelu_done = signal("gelu_done")
        logit_ready = signal("logit_ready")
        cexp_done = signal("cexp_done")
        wexp_ready = signal("wexp_ready")
        wexpT_ps = signal("wexpT_ps")
        wexpT_sb = signal("wexpT_sb")
        eout_ps = signal("eout_ps")
        q1_ps = signal("q1_ps")
        q1_act = signal("q1_act")
        q1_dve = signal("q1_dve")
        ksum_ready = signal("ksum_ready")
        rs_ps = signal("rs_ps")
        rs_part = signal("rs_part")
        rs_all = signal("rs_all")
        s1_ps = signal("s1_ps")
        s1_max = signal("s1_max")
        p1_ready = signal("p1_ready")
        p1T_ps = signal("p1T_ps")
        p1T_sb = signal("p1T_sb")
        o1_ps = signal("o1_ps")
        o1_read = signal("o1_read")
        mean_ready = signal("mean_ready")
        r1_ps = signal("r1_ps")
        r1_ready = signal("r1_ready")
        r2_ps = signal("r2_ps")
        route_in = signal("route_in")
        route_exp = signal("route_exp")
        onehot = signal("onehot")
        onehot_ps = signal("onehot_ps")
        wsel_ready = signal("wsel_ready")
        q2_ps = signal("q2_ps")
        q2_act = signal("q2_act")
        q2_dve = signal("q2_dve")
        PASS1 = 2 * NT * NC
        s2_ps = signal("s2_ps")
        s2_max = signal("s2_max")
        m_ready = signal("m_ready")
        mT_ps = signal("mT_ps")
        q2_shift = signal("q2_shift")
        PAIRS = 2 * NC * NT * 2
        s3_ps = signal("s3_ps")
        p3_ready = signal("p3_ready")
        pv3_pair = signal("pv3_pair")
        o3_sb = signal("o3_sb")
        sum_ps = signal("sum_ps")
        o3_norm = signal("o3_norm")
        y2_ps = signal("y2_ps")
        round_done = signal("round_done")
        stored = signal("stored")
        dve_seq = signal("dve_seq")
        arrived = signal("arrived")
        in_round = (x_loaded, arrived)
        NLOAD = [0]

        block = ctx.enter_context(nc.Block())

        def end_round(eng, go):
            eng.drain().then_inc(arrived, 1)
            eng.wait_ge(go, 1)
            eng.sem_clear(go)

        @block.sync
        def _(sp):
            def load(dst, src):
                NLOAD[0] += 16
                sp.dma_start(dst, src).then_inc(loaded, 16)

            sp.dma_start(base[:], pe.rearrange("(t p) d -> p t d", p=T)).then_inc(cls_loaded, 16)
            load(w_tok[:], W)
            load(w_q0[:], Wq)
            load(w_k0[:], Wk)
            load(w_v0[:], Wv)
            load(w_o0[:], Wo.rearrange("(h d) n -> d h n", h=H0))
            for t, v in ((bo_t, bo), (gamma_t, gamma), (beta_t, beta)):
                load(t[:], bass.AP(v.tensor, 0, [[0, T], [1, D]]))
            for s in range(2):
                load(big[:, 0:1024].rearrange("p (h s d) -> p h s d", h=NE_HEADS, s=2)[:, :, s, :],
                     W_q[:, s * 512:(s + 1) * 512].rearrange("m (h d) -> m h d", h=NE_HEADS))
            load(stage[0:NKEYS, 0:1024].rearrange("k (h c) -> k h c", h=NE_HEADS),
                 keys.rearrange("h k s d -> k h (s d)"))
            for i in range(SINGLES):
                load(stage[START[i]:START[i] + RUN[i], 1024:1152], down[TOPK * i:TOPK * i + RUN[i], :])
                load(w_up[START[i]:START[i] + RUN[i], :], up[TOPK * i:TOPK * i + RUN[i], :])
            s0 = START[SINGLES]
            rest = slice(TOPK * SINGLES, TOPK * TOPK)
            load(stage[s0:NCAND, 1024:1152], down[rest, :].rearrange("(i k) d -> i k d", k=TOPK)[:, 0, :])
            load(w_up[s0:NCAND, :], up[rest, :].rearrange("(i k) d -> i k d", k=TOPK)[:, 0, :])
            load(w_a1[:], qkv.rearrange("c d o -> d c o"))
            load(rw1[:], r_w1)
            load(rb1[:], r_b1.rearrange("(n a) -> n a", a=1))
            load(rw2[:], r_w2)
            load(rb2[:], r_b2.rearrange("(a n) -> a n", a=1))
            sp.wait_ge(pool_setup, 1)
            for i, nkv in enumerate(KV_OPTS):
                load(w_all[:, i, 0:256].rearrange("p (h c) -> p h c", h=H1)[:, :, 0:K1],
                     wq[i].rearrange("m (h d) -> m h d", h=H1))
                for hh in range(H1):
                    kv = hh * nkv // H1
                    load(w_all[:, i, 256 + 32 * hh:256 + 32 * hh + K1], wk[i][:, kv * K1:(kv + 1) * K1])
                    load(w_all[:, i, 512 + K1 * hh:512 + K1 * (hh + 1)], wv[i][:, kv * K1:(kv + 1) * K1])
                    load(wo_all[32 * (hh % 4):32 * (hh % 4) + K1, i, hh // 4, :],
                         wo[i][hh * K1:(hh + 1) * K1, :])
            sp.wait_ge(cls_loaded, 16)
            sp.dma_start(base[0:1, 0, :], cls_tok[0, :, :]).then_inc(cls_loaded, 16)
            xs = x.rearrange("b h w f -> b (h w) f")
            with sp.Fori(0, B) as b:
                xb = xs[ds(b, 1), :, :].rearrange("b s f -> (b s) f")
                sp.dma_start(xin[1:T, 0, :], xb[0:T - 1, :]).then_inc(x_loaded, 16)
                sp.dma_start(xin[:, 1:NT - 1, :], xb[T - 1:T * (NT - 1) - 1, :]
                             .rearrange("(t p) f -> p t f", p=T)).then_inc(x_loaded, 16)
                sp.dma_start(xin[0:LAST, NT - 1, :], xb[T * (NT - 1) - 1:SEQ - 1, :]).then_inc(x_loaded, 16)
                sp.wait_ge(round_done, 1)
                ob = out[ds(b, 1), :, :].rearrange("b s d -> (b s) d")
                sp.dma_start(ob[0:T * (NT - 1), :].rearrange("(t p) d -> p t d", p=T),
                             y[:, 0:NT - 1, :]).then_inc(stored, 16)
                sp.dma_start(ob[T * (NT - 1):SEQ, :], y[0:LAST, NT - 1, :]).then_inc(stored, 16)
                sp.wait_ge(stored, 32)
                sp.wait_ge(arrived, 4)
                sp.sem_clear(range(in_round[0].num, in_round[-1].num + 1))
                for go in (go_pool, go_act, go_dve, go_pe):
                    sp.sem_inc(go, 1)

        NL = NLOAD[0]

        @block.gpsimd
        def _(pool):
            nc.gpsimd.memset(w_all[:], 0.0)
            nc.gpsimd.memset(wo_all[:], 0.0)
            nc.gpsimd.memset(xin[:], 0.0)
            nc.gpsimd.memset(ident[:], 0.0)
            nc.gpsimd.memset(sum_row[:], 0.0)
            nc.gpsimd.memset(ones1[:], 1.0)
            nc.gpsimd.memset(mring[:], 0.0).then_inc(pool_setup, 1)
            pool.wait_ge(pool_setup, 1)
            nc.gpsimd.affine_select(out=ident[:], in_=ident[:], compare_op=ALU.not_equal, fill=1.0,
                                    base=0, pattern=[[-1, 128]], channel_multiplier=1)
            nc.gpsimd.affine_select(out=sum_row[:].rearrange("p (j c) -> p j c", c=32),
                                    in_=sum_row[:].rearrange("p (j c) -> p j c", c=32),
                                    compare_op=ALU.not_equal, fill=1.0, base=-K1,
                                    pattern=[[-32, 4], [0, 32]], channel_multiplier=1)
            nc.gpsimd.iota(rank_i[:], pattern=[[-T, NT]], base=RANK0,
                           channel_multiplier=-1).then_inc(pool_setup, 1)

            with pool.Fori(0, B) as b:
                for u in range(UNITS):
                    pool.wait_ge(score_sb, u + 1)
                    if u >= 3:
                        pool.wait_ge(probT_ps, u - 2)
                    nc.gpsimd.tensor_scalar(mring[:, u % 3, 0:SEQ], ring[:, u % 3, 0:SEQ], 0.0,
                                            MASKED * math.sqrt(K0), ALU.is_equal,
                                            ALU.mult).then_inc(fill_ready, 1)
                for k in range(2):
                    pool.wait_ge(rs_part, k + 1)
                    nc.gpsimd.partition_all_reduce(small[0:T, 4 + k:5 + k], small[0:T, 2 + k:3 + k], T,
                                                   bass.bass_isa.ReduceOp.max).then_inc(rs_all, 1)
                end_round(pool, go_pool)

        @block.scalar
        def _(act):
            def copy(dst, src):
                return nc.scalar.activation(dst, src, ACT.Copy)

            with act.Fori(0, B) as b:
                def normed_T(k):
                    act.wait_ge(xnT_ps, k + 1)
                    copy(xnT[:].rearrange("p (c w) -> p c w", c=NC), banks(0, 3, D, CH)).then_inc(xnT_ready, 1)
                act.wait_ge(xT_ps, 1)
                copy(xinT[:].rearrange("p (c w) -> p c w", c=NC), banks(0, 3, F, CH)).then_inc(xT_ready, 1)
                normed_T(0)
                for i in range(0, NPROJ, 2):
                    act.wait_ge(proj_ready, i + 1)
                    if i < 8:
                        dst = (qT if i < 4 else kT)[:, i % 4, :].rearrange("p (c w) -> p c w", c=NC)
                        copy(dst, banks(0, 3, D, CH)).then_inc(proj_act, 1)
                    else:
                        copy(v0[:, i - 8, :], ps[0:T, 0:2 * BANK]).then_inc(proj_act, 1)
                for s in range(UNITS + 8):
                    if s < UNITS:
                        act.wait_ge(score_ps, s + 1)
                        if s >= 3:
                            act.wait_ge(masked, s - 2)
                        copy(ring[:, s % 3, :].rearrange("p (c w) -> p c w", c=NC),
                             banks(0, 3, T, CH)).then_inc(score_sb, 1)
                    u = s - 1
                    if 0 <= u < UNITS:
                        act.wait_ge(masked, u + 1)
                        nc.scalar.activation(mring[:, u % 3, 0:SEQ], mring[:, u % 3, 0:SEQ], ACT.Exp,
                                             bias=rowmax[:, u:u + 1], scale=-1.0,
                                             accum_out=rowsum[:, u:u + 1]).then_inc(prob_ready, 1)
                    c = (s - 7) // 3
                    if (s - 7) % 3 == 0 and 0 <= c < CHUNKS:
                        act.wait_ge(pv_done, c + 1)
                        if c >= 2:
                            act.wait_ge(oproj_done, c - 1)
                        copy(oT[:, c % 2, :], ps[:, 6 * BANK:6 * BANK + CH]).then_inc(oT_ready, 1)
                normed_T(1)
                act.wait_ge(hexp_ps, 1)
                nc.scalar.activation(hexp, ps[0:T, 6 * BANK:6 * BANK + NT * NCAND].rearrange(
                    "p (t c) -> p t c", t=NT), ACT.Gelu).then_inc(gelu_done, 1)
                act.wait_ge(logit_ready, 1)
                nc.scalar.activation(prob, prob, ACT.Exp).then_inc(cexp_done, 1)
                act.wait_ge(wexpT_ps, 1)
                copy(wexpT.rearrange("p (c w) -> p c w", c=NC), banks(0, 3, NCAND, CH)).then_inc(wexpT_sb, 1)
                normed_T(2)
                act.wait_ge(q1_ps, 1)
                nc.scalar.activation(q1T.rearrange("p (c w) -> p c w", c=NC), banks(0, 3, D, CH),
                                     ACT.Copy, scale=0.125).then_inc(q1_act, 1)
                for t in range(NT):
                    act.wait_ge(s1_max, t + 1)
                    if t >= 2:
                        act.wait_ge(p1T_ps, t - 1)
                    nc.scalar.activation(mring[:, t % 2, 0:SEQ], ps[0:T, 0:SEQ], ACT.Exp,
                                         bias=rowmax[:, t:t + 1], scale=1.0,
                                         accum_out=rowsum[:, t:t + 1]).then_inc(p1_ready, 1)
                normed_T(3)
                act.wait_ge(route_in, 1)
                nc.scalar.activation(small[0:1, 16:19], small[0:1, 13:16], ACT.Exp,
                                     accum_out=small[0:1, 19:20]).then_inc(route_exp, 1)
                for g in range(2):
                    act.wait_ge(q2_ps, 2 * g + 1)
                    nc.scalar.activation(q2T[:, g, :].rearrange("p (c w) -> p c w", c=NC),
                                         banks(0, 3, D, CH), ACT.Copy, scale=0.25).then_inc(q2_act, 1)
                n = 0
                for gc in range(2 * NC):
                    for kt in range(NT):
                        kk = LAST if kt == NT - 1 else T
                        for j in range(2):
                            act.wait_ge(s3_ps, n + 1)
                            if n >= 3:
                                act.wait_ge(pv3_pair, n - 2)
                            nc.scalar.activation(p2[0:kk, n % 3, :, :], banks(2 * (n % 3), 2, kk, CH),
                                                 ACT.Exp).then_inc(p3_ready, 1)
                            n += 1
                end_round(act, go_act)

        @block.vector
        def _(dve):
            dve.wait_ge(pool_setup, 2)
            nc.vector.tensor_copy(rank[:], rank_i[:])
            nc.vector.memset(small[:, 0:1], 1.0)
            nc.vector.memset(small[:, 1:2], 0.0)
            nc.vector.reduce_max(ones_row[:], sum_row[:].rearrange("p (j c) -> p j c", c=32)[:, :, 0],
                                 axis=AX).then_inc(dve_setup, 1)
            dve.wait_ge(dve_setup, 1)
            dve.wait_ge(setup_T, 1)
            nc.vector.tensor_copy(big[:, 2048:3072], ps[:, 0:1024])
            nc.vector.tensor_copy(big[:, 3072:3584], ps[:, 1024:1536])
            nc.vector.tensor_copy(w_down[:], ps[:, 1536:1536 + NCAND]).then_inc(setup_copied, 1)
            dve.wait_ge(setup_sim, 1)
            nc.vector.tensor_copy(w_sim[:], ps[:, 4 * BANK:6 * BANK]).then_inc(setup_done, 1)

            with dve.Fori(0, B) as b:
                done = [0]

                def link(ins):
                    done[0] += 1
                    ins.then_inc(dve_seq, 1)
                    dve.wait_ge(dve_seq, done[0])

                def rstd_of(src, eps):
                    for t in range(NT):
                        last = nc.vector.bn_stats(stats[:, t, :], src[:, t, :])
                    link(last)
                    for t in range(NT):
                        last = nc.vector.bn_aggr(mv[:, t, :], stats[:, t, :])
                    link(last)
                    r, a, c, v = (rst[:, i, :] for i in range(4))
                    link(nc.vector.tensor_scalar_add(v, mv[:, :, 1], eps))
                    link(nc.vector.tensor_scalar(r.bitcast(I32), v.bitcast(I32), -0.5, 1597463007.0,
                                                 ALU.mult, ALU.add))
                    for _ in range(3):
                        link(nc.vector.tensor_tensor(a, r, r, ALU.mult))
                        link(nc.vector.scalar_tensor_tensor(c, a, -0.5, v, ALU.mult, ALU.mult))
                        link(nc.vector.scalar_tensor_tensor(r, c, 1.5, r, ALU.add, ALU.mult))

                def normalise(dst, src):
                    for t in range(NT):
                        last = nc.vector.tensor_scalar(dst[:, t, :], src[:, t, :], mv[:, t, 0:1],
                                                       rst[:, 0, t:t + 1], ALU.subtract, ALU.mult)
                    return last

                def over_tiles(v):
                    return v[:].rearrange("p (a n) -> p a n", a=1).broadcast_to([T, NT, D])

                def wide(v):
                    return v[:].rearrange("p (c j) d -> p c (j d)", c=NC)

                dve.wait_ge(tok_ready, 1)
                dve.wait_ge(cls_loaded, 32)
                link(nc.vector.tensor_tensor(wide(h), banks(3, 3, T, 3 * D), wide(base), ALU.add))
                rstd_of(h, LN_EPS)
                normalise(xn, h).then_inc(xn_ready, 1)
                dve.wait_ge(xn_ready, 1)
                nc.vector.tensor_tensor(y[:], xn[:], over_tiles(bo_t), ALU.add)
                for i in range(1, NPROJ, 2):
                    dve.wait_ge(proj_ready, i + 1)
                    if i < 8:
                        dst = (qT if i < 4 else kT)[:, i % 4, :].rearrange("p (c w) -> p c w", c=NC)
                        nc.vector.tensor_copy(dst, banks(3, 3, D, CH)).then_inc(proj_dve, 1)
                    else:
                        nc.vector.tensor_copy(v0[:, i - 8, :],
                                              ps[0:T, 3 * BANK:5 * BANK]).then_inc(proj_dve, 1)

                for s in range(UNITS + 11):
                    if s < UNITS:
                        dve.wait_ge(fill_ready, s + 1)
                        nc.vector.tensor_tensor_reduce(
                            out=mring[:, s % 3, 0:SEQ], in0=ring[:, s % 3, 0:SEQ], in1=mring[:, s % 3, 0:SEQ],
                            scale=-1.0 / math.sqrt(K0), scalar=3.0e38, op0=ALU.add, op1=ALU.min,
                            accum_out=rowmax[:, s:s + 1]).then_inc(masked, 1)
                    u = s - 2
                    if 0 <= u < UNITS:
                        c, j = u // 3, u % 3
                        dve.wait_ge(probT_ps, u + 1)
                        if j == 0 and c >= 2:
                            dve.wait_ge(pv_done, c - 1)
                        dst = pt[:, c % 2, :].rearrange("p (i k q) -> p i k q", i=NC, k=3)
                        nc.vector.tensor_copy(dst[:, :, :, T * j:T * (j + 1)],
                                              banks(3, 3, T, CH).rearrange("p i (k q) -> p i k q", k=3)
                                              ).then_inc(probT_sb, 1)
                    c = (s - 9) // 3
                    if (s - 9) % 3 == 0 and 0 <= c < CHUNKS:
                        link(nc.vector.reciprocal(rrec[:, 3 * c:3 * c + 3], rowsum[:, 3 * c:3 * c + 3]))
                        dve.wait_ge(oproj_done, c + 1)
                        for j in range(3):
                            t = (3 * c + j) % NT
                            last = nc.vector.scalar_tensor_tensor(
                                y[:, t, :], ps[0:T, 7 * BANK + j * D:7 * BANK + (j + 1) * D],
                                rrec[:, 3 * c + j:3 * c + j + 1], y[:, t, :], ALU.mult, ALU.add)
                        last.then_inc(y_added, 1)
                dve.wait_ge(y_added, CHUNKS)
                rstd_of(y, POST_EPS)
                link(normalise(y, y))
                link(nc.vector.tensor_tensor(y[:], y[:], over_tiles(gamma_t), ALU.mult))
                link(nc.vector.tensor_tensor(y[:], y[:], over_tiles(beta_t), ALU.add))
                link(nc.vector.tensor_tensor(h[:], h[:], y[:], ALU.add))

                rstd_of(h, LN_EPS)
                normalise(xn, h).then_inc(xn_ready, 1)
                for t in range(NT):
                    dve.wait_ge(sim_ps, t + 1)
                    side = 3 * (t % 2)
                    sims = ps[0:T, side * BANK:(side + 2) * BANK].rearrange("p (g k) -> p g k", k=NKEYS)
                    tt = top[:, t, :, :, :].rearrange("p s h k -> p (s h) k")
                    for g in range(2 * NE_HEADS):
                        last = nc.vector.max(tt[:, g, 0:8], sims[:, g, :])
                    link(last)
                    for g in range(2 * NE_HEADS):
                        last = nc.vector.match_replace(simw[:, g, :], tt[:, g, 0:8], sims[:, g, :], REMOVED)
                    last.then_inc(sim_read, 1)
                    dve.wait_ge(sim_read, t + 1)
                    for g in range(2 * NE_HEADS):
                        last = nc.vector.max(tt[:, g, 8:16], simw[:, g, :])
                link(last)
                cand4 = cand.rearrange("p (t h) c -> p t h c", t=NT)
                sx, sy = top[:, :, 0, :, :], top[:, :, 1, :, :]
                for i in range(SINGLES):
                    n = RUN[i]
                    nc.vector.tensor_tensor(cand4[:, :, :, START[i]:START[i] + n],
                                            sx[:, :, :, i:i + 1].broadcast_to([T, NT, NE_HEADS, n]),
                                            sy[:, :, :, 0:n], ALU.add)
                n = TOPK - SINGLES
                link(nc.vector.tensor_tensor(cand4[:, :, :, START[SINGLES]:NCAND], sx[:, :, :, SINGLES:TOPK],
                                             sy[:, :, :, 0:1].broadcast_to([T, NT, NE_HEADS, n]), ALU.add))
                for half in range(2):
                    src = cand if half == 0 else left
                    for g in range(TH):
                        last = nc.vector.max(best[:, g, 8 * half:8 * half + 8], src[:, g, :])
                    link(last)
                    for g in range(TH):
                        last = nc.vector.match_replace(left[:, g, :], best[:, g, 8 * half:8 * half + 8],
                                                       src[:, g, :], REMOVED)
                    link(last)
                nc.vector.tensor_tensor(prob, cand, cand[:, :, 0:1].broadcast_to([T, TH, NCAND]),
                                        ALU.subtract).then_inc(logit_ready, 1)
                dve.wait_ge(cexp_done, 1)
                link(nc.vector.scalar_tensor_tensor(prob, left, REMOVED, prob, ALU.is_equal, ALU.mult))
                link(nc.vector.reduce_sum(rowsum[:, 0:TH], prob, axis=AX))
                link(nc.vector.reciprocal(rrec[:, 0:TH], rowsum[:, 0:TH]))
                link(nc.vector.tensor_tensor(prob, prob, rrec[:, 0:TH].rearrange("p (g a) -> p g a", a=1)
                                             .broadcast_to([T, TH, NCAND]), ALU.mult))
                link(nc.vector.reduce_sum(wexp, prob.rearrange("p (t h) c -> p t c h", t=NT), axis=AX))
                dve.wait_ge(gelu_done, 1)
                nc.vector.tensor_tensor(wexp, wexp, hexp, ALU.mult).then_inc(wexp_ready, 1)
                dve.wait_ge(eout_ps, 1)
                link(nc.vector.tensor_tensor(wide(h), banks(3, 3, T, 3 * D), wide(h), ALU.add))

                rstd_of(h, LN_EPS)
                normalise(xn, h).then_inc(xn_ready, 1)
                dve.wait_ge(q1_ps, 2)
                nc.vector.tensor_copy(k1T.rearrange("p (c w) -> p c w", c=NC), banks(3, 3, D, CH)).then_inc(q1_dve, 1)
                dve.wait_ge(q1_dve, 1)
                nc.vector.reduce_sum(small[:, 6:7], k1T[:, 0:SEQ], axis=AX).then_inc(ksum_ready, 1)
                dve.wait_ge(q1_ps, 3)
                nc.vector.tensor_copy(v1.rearrange("p (c j) d -> p c (j d)", c=NC),
                                      banks(0, 3, T, 3 * D)).then_inc(q1_dve, 1)
                dve.wait_ge(rs_ps, 1)
                rs, eq = small[0:T, 20:20 + NT], small[0:T, 30:30 + NT]
                link(nc.vector.memset(rs, -3.0e38))
                nc.vector.tensor_scalar(rs[:, 0:NT - 1], ps[0:T, 6 * BANK:6 * BANK + NT - 1], -1.0, None, ALU.mult)
                link(nc.vector.tensor_scalar(rs[0:LAST, NT - 1:NT], ps[0:LAST, 6 * BANK + NT - 1:6 * BANK + NT],
                                             -1.0, None, ALU.mult))
                nc.vector.reduce_max(small[0:T, 2:3], rs, axis=AX).then_inc(rs_part, 1)
                dve.wait_ge(rs_all, 1)
                link(nc.vector.scalar_tensor_tensor(eq, rs, small[0:T, 4:5], rank[:], ALU.is_equal, ALU.mult))
                nc.vector.reduce_max(small[0:T, 3:4], eq, axis=AX).then_inc(rs_part, 1)
                dve.wait_ge(rs_all, 2)
                link(nc.vector.tensor_tensor(small[0:T, 7:8], small[0:T, 5:6], small[0:T, 1:2], ALU.subtract))
                link(nc.vector.scalar_tensor_tensor(small[0:T, 1:2], small[0:T, 7:8], small[0:T, 0:1],
                                                    small[0:T, 1:2], ALU.mult, ALU.add))
                nc.vector.memset(small[0:T, 0:1], 0.0)
                keep = small[0:T, 40:40 + NT]
                link(nc.vector.tensor_scalar(keep, rank[:], small[0:T, 1:2], None, ALU.not_equal))
                for s in range(NT + 2):
                    if s < NT:
                        dve.wait_ge(s1_ps, s + 1)
                        nc.vector.tensor_reduce(rowmax[:, s:s + 1], ps[0:T, 0:SEQ], axis=AX, op=ALU.max,
                                                negate=True).then_inc(s1_max, 1)
                    u = s - 1
                    if 0 <= u < NT:
                        dve.wait_ge(p1T_ps, u + 1)
                        if u >= 2:
                            dve.wait_ge(o1_ps, u - 1)
                        nc.vector.tensor_copy(pt1[:, u % 2, :, :].rearrange("p (i k) q -> p i (k q)", i=NC),
                                              banks(3, 3, T, CH)).then_inc(p1T_sb, 1)
                    u = s - 2
                    if 0 <= u < NT:
                        link(nc.vector.reciprocal(rrec[:, u:u + 1], rowsum[:, u:u + 1]))
                        link(nc.vector.tensor_tensor(rrec[:, u:u + 1], rrec[:, u:u + 1], keep[:, u:u + 1], ALU.mult))
                        dve.wait_ge(o1_ps, u + 1)
                        nc.vector.scalar_tensor_tensor(
                            h[:, u, :], ps[0:T, (6 + u % 2) * BANK:(6 + u % 2) * BANK + D], rrec[:, u:u + 1],
                            h[:, u, :], ALU.mult, ALU.add).then_inc(o1_read, 1)
                dve.wait_ge(o1_read, NT)

                rstd_of(h, LN_EPS)
                normalise(xn, h).then_inc(xn_ready, 1)
                dve.wait_ge(xnT_ready, 4)
                link(nc.vector.reduce_sum(small[:, 8:9], xnT[:, 0:SEQ], axis=AX))
                nc.vector.tensor_scalar(small[:, 9:10], small[:, 8:9], 1.0 / SEQ, None, ALU.mult).then_inc(mean_ready, 1)
                dve.wait_ge(r1_ps, 1)
                nc.vector.tensor_scalar(small[0:RH, 10:11], ps[0:RH, 6 * BANK:6 * BANK + 1], rb1[:], 0.0,
                                        ALU.add, ALU.max).then_inc(r1_ready, 1)
                dve.wait_ge(r2_ps, 1)
                lg, ex, oh = small[0:1, 13:16], small[0:1, 16:19], small[0:1, 50:53]
                link(nc.vector.tensor_tensor(lg, ps[0:1, 7 * BANK:7 * BANK + 3], rb2[:], ALU.add))
                link(nc.vector.reduce_max(small[0:1, 12:13], lg, axis=AX))
                nc.vector.tensor_scalar(lg, lg, small[0:1, 12:13], None, ALU.subtract).then_inc(route_in, 1)
                dve.wait_ge(route_exp, 1)
                link(nc.vector.reciprocal(small[0:1, 11:12], small[0:1, 19:20]))
                link(nc.vector.tensor_scalar(lg, ex, small[0:1, 11:12], None, ALU.mult))
                link(nc.vector.reduce_max(small[0:1, 12:13], lg, axis=AX))
                link(nc.vector.tensor_scalar(oh, lg, small[0:1, 12:13], None, ALU.is_equal))
                link(nc.vector.tensor_tensor(small[0:1, 54:55], oh[:, 0:1], oh[:, 1:2], ALU.mult))
                link(nc.vector.tensor_tensor(oh[:, 1:2], oh[:, 1:2], small[0:1, 54:55], ALU.subtract))
                link(nc.vector.tensor_tensor(small[0:1, 55:56], oh[:, 0:1], oh[:, 1:2], ALU.add))
                nc.vector.tensor_scalar(oh[:, 2:3], small[0:1, 55:56], -1.0, 1.0, ALU.mult,
                                        ALU.add).then_inc(onehot, 1)
                dve.wait_ge(onehot_ps, 1)
                link(nc.vector.tensor_copy(small[:, 57:60], ps[:, 6 * BANK:6 * BANK + 3]))
                wf = [(w_sel[:], w_all), (wo_sel[:].rearrange("p g n -> p (g n)"), wo_all)]
                for i in range(3):
                    for dst, src in wf:
                        w = src[:, i, :] if src is w_all else src[:, i, :, :].rearrange("p g n -> p (g n)")
                        s = small[:, 57 + i:58 + i]
                        if i == 0:
                            last = nc.vector.tensor_scalar(dst, w, s, None, ALU.mult)
                        else:
                            last = nc.vector.scalar_tensor_tensor(dst, w, s, dst, ALU.mult, ALU.add)
                    if i < 2:
                        link(last)
                last.then_inc(wsel_ready, 1)
                link(nc.vector.memset(v2, 0.0))
                link(nc.vector.memset(mpad, 0.0))
                link(nc.vector.memset(v2[:, :, :, K1:K1 + 1], 1.0))
                for g in range(2):
                    dve.wait_ge(q2_ps, 2 * g + 2)
                    nc.vector.tensor_scalar(k2T[:, g, :].rearrange("p (c w) -> p c w", c=NC), banks(3, 3, D, CH),
                                            ones_row[:], None, ALU.add).then_inc(q2_dve, 1)
                dve.wait_ge(q2_ps, 5)
                for c in range(NC):
                    last = nc.vector.tensor_copy(
                        v2[:, 3 * c:3 * c + 3, :, 0:K1],
                        ps[0:T, c * BANK:c * BANK + 3 * D].rearrange("p (t h c) -> p t h c", t=3, h=H1))
                last.then_inc(q2_dve, 1)
                n = 0
                for g in range(2):
                    for t in range(NT):
                        for c in range(NC):
                            w = CH - (c == NC - 1)
                            dve.wait_ge(s2_ps, n + 1)
                            nc.vector.reduce_max(m3[:, g, t, c, :], banks(4 * (n % 2), 4, T, w),
                                                 axis=AX).then_inc(s2_max, 1)
                            n += 1
                    dve.wait_ge(s2_max, n)
                    nc.vector.tensor_reduce(mpad[:, g, :, :].rearrange("p t (j c) -> p t j c", c=32)[:, :, :, K1],
                                            m3[:, g, :, :, :].rearrange("p t c j -> p t j c"), axis=AX,
                                            op=ALU.max, negate=True).then_inc(m_ready, 1)
                for g in range(2):
                    dve.wait_ge(mT_ps, g + 1)
                    nc.vector.tensor_tensor(q2T[:, g, :].rearrange("p (c w) -> p c w", c=NC), banks(3 * g, 3, D, CH),
                                            q2T[:, g, :].rearrange("p (c w) -> p c w", c=NC),
                                            ALU.add).then_inc(q2_shift, 1)
                for n in range(2 * NC):
                    g, c = n // NC, n % NC
                    dve.wait_ge(pv3_pair, (n + 1) * 2 * NT)
                    nc.vector.tensor_copy(o2T[:, g, CH * c:CH * (c + 1)],
                                          ps[:, 6 * BANK:6 * BANK + CH]).then_inc(o3_sb, 1)
                    dve.wait_ge(sum_ps, n + 1)
                    link(nc.vector.reciprocal(stage[:, 0:CH], ps[:, 7 * BANK:7 * BANK + CH]))
                    nc.vector.tensor_tensor(o2T[:, g, CH * c:CH * (c + 1)], o2T[:, g, CH * c:CH * (c + 1)],
                                            stage[:, 0:CH], ALU.mult).then_inc(o3_norm, 1)
                dve.wait_ge(y2_ps, 1)
                nc.vector.tensor_tensor(wide(y), banks(0, 3, T, 3 * D), wide(h), ALU.add).then_inc(round_done, 1)
                end_round(dve, go_dve)

        @block.tensor
        def _(pe_):
            def mm(out_, lhsT, rhs, start=True, stop=True):
                return nc.tensor.matmul(out_, lhsT, rhs, start=start, stop=stop)

            pe_.wait_ge(pool_setup, 2)
            pe_.wait_ge(loaded, NL)
            for hh in range(NE_HEADS):
                nc.tensor.transpose(ps[:, hh * 128:(hh + 1) * 128], big[:, hh * 128:(hh + 1) * 128], ident[:])
                nc.tensor.transpose(ps[:, 1024 + hh * 64:1024 + (hh + 1) * 64],
                                    stage[0:NKEYS, hh * 128:(hh + 1) * 128], ident[0:NKEYS, 0:NKEYS])
            nc.tensor.transpose(ps[:, 1536:1536 + NCAND], stage[0:NCAND, 1024:1152],
                                ident[0:NCAND, 0:NCAND]).then_inc(setup_T, 1)
            pe_.wait_ge(setup_copied, 1)
            for hh in range(NE_HEADS):
                for s in range(2):
                    r = slice(64 * s, 64 * s + 64)
                    last = mm(ps[:, (4 + s) * BANK + hh * 64:(4 + s) * BANK + (hh + 1) * 64],
                              big[r, 2048 + hh * 128:2048 + (hh + 1) * 128], big[r, 3072 + hh * 64:3072 + (hh + 1) * 64])
            last.then_inc(setup_sim, 1)
            pe_.wait_ge(setup_done, 1)

            with pe_.Fori(0, B) as b:
                def three_chunks(first, lhsT, rhs):
                    for c in range(NC):
                        last = mm(ps[0:lhsT.shape[1], (first + c) * BANK:(first + c) * BANK + CH], lhsT,
                                  rhs[:, CH * c:CH * (c + 1)])
                    return last

                def tokens_T(src, width):
                    for t in range(NT):
                        at = (t // 3) * BANK + (t % 3) * T
                        last = nc.tensor.transpose(ps[0:width, at:at + T], src[:, t, :], ident[0:T, 0:T])
                    return last

                def by_token(first, xT_, rhs):
                    for t in range(NT):
                        at = (first + t // 3) * BANK + (t % 3) * D
                        last = mm(ps[0:T, at:at + D], xT_[:, T * t:T * (t + 1)], rhs)
                    return last

                def normed_T(k):
                    pe_.wait_ge(xn_ready, k + 1)
                    tokens_T(xn, D).then_inc(xnT_ps, 1)
                    pe_.wait_ge(xnT_ready, k + 1)

                pe_.wait_ge(x_loaded, 48)
                tokens_T(xin, F).then_inc(xT_ps, 1)
                pe_.wait_ge(xT_ready, 1)
                by_token(3, xinT, w_tok[:]).then_inc(tok_ready, 1)
                normed_T(0)
                for i in range(NPROJ):
                    side = 3 * (i % 2)
                    if i >= 2:
                        s_, n_ = (proj_act, i // 2) if i % 2 == 0 else (proj_dve, i // 2)
                        pe_.wait_ge(s_, n_)
                    if i < 8:
                        w = (w_q0 if i < 4 else w_k0)[:, D * (i % 4):D * (i % 4 + 1)]
                        three_chunks(side, w, xnT).then_inc(proj_ready, 1)
                    else:
                        for n in range(2):
                            last = mm(ps[0:T, (side + n) * BANK:(side + n + 1) * BANK],
                                      xnT[:, T * (i - 8):T * (i - 7)], w_v0[:, n * BANK:(n + 1) * BANK])
                        last.then_inc(proj_ready, 1)
                pe_.wait_ge(proj_act, (NPROJ + 1) // 2)
                pe_.wait_ge(proj_dve, NPROJ // 2)
                for s in range(UNITS + 9):
                    if s < UNITS:
                        hh, t = s // NT, s % NT
                        r = slice(64 * (hh % 2), 64 * (hh % 2) + 64)
                        if s >= 1:
                            pe_.wait_ge(score_sb, s)
                        three_chunks(0, qT[r, hh // 2, T * t:T * (t + 1)], kT[r, hh // 2, :]).then_inc(score_ps, 1)
                    c, j = (s - 5) // 3, (s - 5) % 3
                    if 0 <= c < CHUNKS:
                        if j == 0:
                            pe_.wait_ge(probT_sb, 3 * c + 3)
                            if c >= 1:
                                pe_.wait_ge(oT_ready, c)
                        for kt in range(3 * j, 3 * j + 3):
                            last = mm(ps[:, 6 * BANK:6 * BANK + CH], v0[:, kt, D * (c // 3):D * (c // 3 + 1)],
                                      pt[:, c % 2, CH * kt:CH * (kt + 1)], start=(kt == 0), stop=(kt == NT - 1))
                        if j == 2:
                            last.then_inc(pv_done, 1)
                    c = (s - 8) // 3
                    if (s - 8) % 3 == 0 and 0 <= c < CHUNKS:
                        pe_.wait_ge(oT_ready, c + 1)
                        if c >= 1:
                            pe_.wait_ge(y_added, c)
                        for j in range(3):
                            last = mm(ps[0:T, 7 * BANK + j * D:7 * BANK + (j + 1) * D],
                                      oT[:, c % 2, T * j:T * (j + 1)], w_o0[:, c // 3, :])
                        last.then_inc(oproj_done, 1)
                    u = s - 2
                    if 0 <= u < UNITS:
                        pe_.wait_ge(prob_ready, u + 1)
                        if u >= 1:
                            pe_.wait_ge(probT_sb, u)
                        for kt in range(NT):
                            at = (3 + kt // 3) * BANK + (kt % 3) * T
                            last = nc.tensor.transpose(ps[0:T, at:at + T], mring[:, u % 3, T * kt:T * (kt + 1)],
                                                       ident[0:T, 0:T])
                        last.then_inc(probT_ps, 1)
                normed_T(1)
                for t in range(NT):
                    at = 6 * BANK + t * NCAND
                    last = mm(ps[0:T, at:at + NCAND], xnT[:, T * t:T * (t + 1)], w_down[:])
                last.then_inc(hexp_ps, 1)
                for t in range(NT):
                    if t >= 2:
                        pe_.wait_ge(sim_read, t - 1)
                    for n in range(2):
                        at = (3 * (t % 2) + n) * BANK
                        last = mm(ps[0:T, at:at + BANK], xnT[:, T * t:T * (t + 1)], w_sim[:, n * BANK:(n + 1) * BANK])
                    last.then_inc(sim_ps, 1)
                pe_.wait_ge(wexp_ready, 1)
                tokens_T(wexp, NCAND).then_inc(wexpT_ps, 1)
                pe_.wait_ge(wexpT_sb, 1)
                by_token(3, wexpT, w_up[:]).then_inc(eout_ps, 1)
                normed_T(2)
                three_chunks(0, w_a1[:, 0, :], xnT).then_inc(q1_ps, 1)
                three_chunks(3, w_a1[:, 1, :], xnT).then_inc(q1_ps, 1)
                pe_.wait_ge(q1_act, 1)
                by_token(0, xnT, w_a1[:, 2, :]).then_inc(q1_ps, 1)
                pe_.wait_ge(ksum_ready, 1)
                for t in range(NT):
                    last = mm(ps[0:T, 6 * BANK + t:6 * BANK + t + 1], q1T[:, T * t:T * (t + 1)], small[:, 6:7])
                last.then_inc(rs_ps, 1)
                pe_.wait_ge(q1_dve, 2)
                pe_.wait_ge(rs_part, 1)
                for s in range(NT + 2):
                    if s < NT:
                        if s >= 1:
                            pe_.wait_ge(p1_ready, s)
                        for c0, c1 in ((0, 512), (512, 1024), (1024, SEQ)):
                            last = mm(ps[0:T, c0:c1], q1T[:, T * s:T * (s + 1)], k1T[:, c0:c1])
                        last.then_inc(s1_ps, 1)
                    u = s - 1
                    if 0 <= u < NT:
                        pe_.wait_ge(p1_ready, u + 1)
                        if u >= 1:
                            pe_.wait_ge(p1T_sb, u)
                        for kt in range(NT):
                            at = (3 + kt // 3) * BANK + (kt % 3) * T
                            last = nc.tensor.transpose(ps[0:T, at:at + T], mring[:, u % 2, T * kt:T * (kt + 1)],
                                                       ident[0:T, 0:T])
                        last.then_inc(p1T_ps, 1)
                    u = s - 2
                    if 0 <= u < NT:
                        pe_.wait_ge(p1T_sb, u + 1)
                        if u >= 2:
                            pe_.wait_ge(o1_read, u - 1)
                        for kt in range(NT):
                            at = (6 + u % 2) * BANK
                            last = mm(ps[0:T, at:at + D], pt1[:, u % 2, kt, :], v1[:, kt, :],
                                      start=(kt == 0), stop=(kt == NT - 1))
                        last.then_inc(o1_ps, 1)
                normed_T(3)
                pe_.wait_ge(mean_ready, 1)
                mm(ps[0:RH, 6 * BANK:6 * BANK + 1], rw1[:], small[:, 9:10]).then_inc(r1_ps, 1)
                pe_.wait_ge(r1_ready, 1)
                mm(ps[0:1, 7 * BANK:7 * BANK + 3], small[0:RH, 10:11], rw2[:]).then_inc(r2_ps, 1)
                pe_.wait_ge(onehot, 1)
                mm(ps[:, 6 * BANK:6 * BANK + 3], ones1[:], small[0:1, 50:53]).then_inc(onehot_ps, 1)
                pe_.wait_ge(wsel_ready, 1)
                for g in range(2):
                    if g:
                        pe_.wait_ge(q2_act, g)
                    three_chunks(0, w_sel[:, D * g:D * (g + 1)], xnT).then_inc(q2_ps, 1)
                    if g:
                        pe_.wait_ge(q2_dve, g)
                    three_chunks(3, w_sel[:, 256 + D * g:256 + D * (g + 1)], xnT).then_inc(q2_ps, 1)
                pe_.wait_ge(q2_act, 2)
                by_token(0, xnT, w_sel[:, 512:640]).then_inc(q2_ps, 1)
                pe_.wait_ge(q2_dve, 3)
                n = 0
                for g in range(2):
                    for t in range(NT):
                        for c in range(NC):
                            w = CH - (c == NC - 1)
                            if n >= 2:
                                pe_.wait_ge(s2_max, n - 1)
                            for j in range(4):
                                r = slice(32 * j, 32 * j + 32)
                                at = (4 * (n % 2) + j) * BANK
                                last = mm(ps[0:T, at:at + w], q2T[r, g, T * t:T * (t + 1)],
                                          k2T[r, g, CH * c:CH * c + w])
                            last.then_inc(s2_ps, 1)
                            n += 1
                pe_.wait_ge(s2_max, PASS1)
                for g in range(2):
                    pe_.wait_ge(m_ready, g + 1)
                    for t in range(NT):
                        at = (3 * g + t // 3) * BANK + (t % 3) * T
                        last = nc.tensor.transpose(ps[:, at:at + T], mpad[:, g, t, :], ident[0:T, 0:T])
                    last.then_inc(mT_ps, 1)
                pe_.wait_ge(q2_shift, 2)

                def values(n):
                    gc, kt, jj = n // (2 * NT), n // 2 % NT, n % 2
                    g = gc // NC
                    kk = LAST if kt == NT - 1 else T
                    pe_.wait_ge(p3_ready, n + 1)
                    if kt == 0 and jj == 0 and gc >= 1:
                        pe_.wait_ge(o3_sb, gc)
                    for i in range(2):
                        j = 2 * jj + i
                        last = mm(ps[32 * j:32 * j + 32, 6 * BANK:6 * BANK + CH], v2[0:kk, kt, 4 * g + j, :],
                                  p2[0:kk, n % 3, i, :], start=(kt == 0), stop=(kt == NT - 1))
                    last.then_inc(pv3_pair, 1)

                def sums(gc):
                    g, c = gc // NC, gc % NC
                    pe_.wait_ge(o3_sb, gc + 1)
                    if gc >= 1:
                        pe_.wait_ge(o3_norm, gc)
                    mm(ps[:, 7 * BANK:7 * BANK + CH], sum_row[:], o2T[:, g, CH * c:CH * (c + 1)]).then_inc(sum_ps, 1)

                for n in range(PAIRS + 2):
                    if n < PAIRS:
                        gc, kt, jj = n // (2 * NT), n // 2 % NT, n % 2
                        g, c = gc // NC, gc % NC
                        kk = LAST if kt == NT - 1 else T
                        if n >= 3:
                            pe_.wait_ge(p3_ready, n - 2)
                        for i in range(2):
                            j = 2 * jj + i
                            r = slice(32 * j, 32 * j + 32)
                            at = (2 * (n % 3) + i) * BANK
                            last = mm(ps[0:kk, at:at + CH], k2T[r, g, T * kt:T * kt + kk],
                                      q2T[r, g, CH * c:CH * (c + 1)])
                        last.then_inc(s3_ps, 1)
                    if n >= 2:
                        values(n - 2)
                    if n >= 2 + 2 * NT and (n - 2) % (2 * NT) == 2:
                        sums((n - 2) // (2 * NT) - 1)
                sums(2 * NC - 1)
                pe_.wait_ge(o3_norm, 2 * NC)
                for t in range(NT):
                    at = (t // 3) * BANK + (t % 3) * D
                    for g in range(2):
                        last = mm(ps[0:T, at:at + D], o2T[:, g, T * t:T * (t + 1)], wo_sel[:, g, :],
                                  start=(g == 0), stop=(g == 1))
                last.then_inc(y2_ps, 1)
                end_round(pe_, go_pe)


_INS = ['x', 'cls_tok', 'L0_tok_W', 'L0_attn_Wq', 'L0_attn_Wk', 'L0_attn_Wv', 'L0_attn_Wo', 'L0_attn_bo',
        'L0_attn_gamma', 'L0_attn_beta', 'L0_ffn_W_q', 'L0_ffn_keys', 'L0_ffn_down_embed', 'L0_ffn_up_embed',
        'L1_attn_kernel', 'L1_ffn_r_w1', 'L1_ffn_r_b1', 'L1_ffn_r_w2', 'L1_ffn_r_b2', 'L1_ffn_wq0', 'L1_ffn_wk0',
        'L1_ffn_wv0', 'L1_ffn_wo0', 'L1_ffn_wq1', 'L1_ffn_wk1', 'L1_ffn_wv1', 'L1_ffn_wo1', 'L1_ffn_wq2',
        'L1_ffn_wk2', 'L1_ffn_wv2', 'L1_ffn_wo2']


def position_table():
    position = np.arange(2 * (SEQ - 1), dtype=np.float32)[:, None]
    div_term = np.exp(np.arange(0, D, 2, dtype=np.float32) * (-math.log(10000.0) / D))
    pe = np.zeros((2 * (SEQ - 1), D), dtype=np.float32)
    pe[:, 0::2] = np.sin(position * div_term)
    pe[:, 1::2] = np.cos(position * div_term)
    table = np.zeros((SP, D), np.float32)
    table[1:SEQ] = pe[:SEQ - 1]
    return table


def kernel(**inputs):
    import concourse.bacc as bacc
    from concourse.bass_utils import run_bass_kernel_spmd

    nc = bacc.Bacc("TRN2", target_bir_lowering=False, num_devices=1)
    arrays, aps = {}, {}
    for name in _INS + ['position_table']:
        a = position_table() if name == 'position_table' else np.ascontiguousarray(inputs[name])
        arrays[f"in_{name}"] = a
        aps[name] = nc.dram_tensor(f"in_{name}", a.shape, mybir.dt.from_np(a.dtype), kind="ExternalInput").ap()
    out = nc.dram_tensor("out", (B, SEQ, D), FP32, kind="ExternalOutput").ap()
    a = [aps[n] for n in _INS]
    last = a[19:]
    vit_kernel(nc, *a[:19], [last[0], last[4], last[8]], [last[1], last[5], last[9]],
               [last[2], last[6], last[10]], [last[3], last[7], last[11]], aps['position_table'], out)
    r = run_bass_kernel_spmd(nc, [arrays], core_ids=[0])
    return r.results[0]["out"]
```

```python
import math
from contextlib import ExitStack

import numpy as np

import concourse.bass as bass
from concourse import mybir

FP32 = mybir.dt.float32
I32 = mybir.dt.int32
FR = mybir.dt.float32r
ALU = mybir.AluOpType
ACT = mybir.ActivationFunctionType
AX = mybir.AxisListType.X
ds = bass.ds

B = 8
SEQ = 1025
F = 29
D = 128
H0, K0 = 8, 64
NE_HEADS, NKEYS, DKEY, TOPK = 8, 64, 64, 16
H1, K1 = 8, 16
KV_OPTS = (8, 4, 1)
RH = D // 4

T = 114
NT = 9
SP = T * NT
CH = 342
NC = SP // CH
LAST = SEQ - (NT - 1) * T
BANK = 512

RUN = [TOPK // (i + 1) for i in range(TOPK)]
START = [sum(RUN[:i]) for i in range(TOPK)]
NCAND = sum(RUN)
SINGLES = next(i for i in range(TOPK) if RUN[i] == 1)
REMOVED = -3.0e38
TH = NT * NE_HEADS

UNITS = H0 * NT
CHUNKS = H0 * NC
RANK0 = 2048

LN_EPS = 1e-5
POST_EPS = 1e-6
MASKED = -1.0e9


def lookahead_jobs():
    jobs = [(-1, 0, kind, 0, c) for kind in "qkv" for c in range(NC)]
    for s in range(UNITS + 9):
        head, r = s // NT, s % NT
        if s >= 8 and (s - 8) % 3 == 0 and (s - 8) // 3 < CHUNKS:
            jobs.append((s, 0, "o", (s - 8) // 3 // NC, (s - 8) // 3))
        if head + 1 < H0:
            if r % 3 != 2:
                n = 2 * (r // 3) + r % 3
                jobs.append((s, 0, "qk"[n // 3], head + 1, n % 3))
            if r in (5, 6, 7):
                jobs.append((s, 1, "v", head + 1, r - 5))
    return jobs


JOBS = lookahead_jobs()


def jobs_at(slot, place):
    return [i for i, job in enumerate(JOBS) if job[:2] == (slot, place)]


def splits_before(i):
    return sum(job[2] != "o" for job in JOBS[:i])


def splits_through(kind, head):
    return splits_before(max(i for i, job in enumerate(JOBS) if job[2:4] == (kind, head))) + 1


def job_bank(i):
    return i % 8 if i < 3 * NC else 7


def vit_kernel(nc, x, cls_tok, W, Wq, Wk, Wv, Wo, bo, gamma, beta, W_q, keys, down, up, qkv,
               r_w1, r_b1, r_w2, r_b2, wq, wk, wv, wo, pe, out):
    ctx = ExitStack()
    with ctx:
        def sb(name, shape, dt=FP32):
            return ctx.enter_context(nc.sbuf_tensor(name, shape, dt))

        def signal(name):
            return ctx.enter_context(nc.semaphore(name))

        ps = ctx.enter_context(nc.psum_tensor("ps", [128, 8 * BANK], FP32))

        def banks(first, n, p, w):
            return ps[0:p, first * BANK:(first + n) * BANK].rearrange("p (n w) -> p n w", n=n)[:, :, 0:w]

        ident = sb("ident", [128, 128])
        sum_row = sb("sum_row", [128, 128])
        marks = sb("marks", [128, 3, 2, K1])
        mark = sb("mark", [128, 3])
        q_sign = sb("q_sign", [128, 1])
        k_sign = sb("k_sign", [128, 1])
        ones1 = sb("ones1", [1, 128])
        rank_i = sb("rank_i", [T, NT], I32)
        rank = sb("rank", [T, NT])
        base = sb("base", [T, NT, D])
        w_tok = sb("w_tok", [F, D])
        w_q0 = sb("w_q0", [D, H0, 2 * K0])
        w_k0 = sb("w_k0", [D, H0, 2 * K0])
        w_v0 = sb("w_v0", [D, H0 * D])
        w_o0 = sb("w_o0", [D, H0, D])
        bo_t = sb("bo_t", [T, D])
        gamma_t = sb("gamma_t", [T, D])
        beta_t = sb("beta_t", [T, D])
        w_sim = sb("w_sim", [D, 2 * NE_HEADS * NKEYS])
        w_down = sb("w_down", [D, NCAND])
        w_up = sb("w_up", [NCAND, D])
        w_a1 = sb("w_a1", [D, 3, D])
        rw1 = sb("rw1", [D, RH])
        rb1 = sb("rb1", [RH, 1])
        rw2 = sb("rw2", [RH, 3])
        rb2 = sb("rb2", [1, 3])
        w_all = sb("w_all", [D, 3, 3 * D])
        wo_all = sb("wo_all", [128, 3, 2, D])
        w_sel = sb("w_sel", [D, 3 * D])
        w_thrice = sb("w_thrice", [D, 2, H1, 4, K1])
        wo_sel = sb("wo_sel", [128, 2, D])

        xin = sb("xin", [T, NT, F])
        xinT = sb("xinT", [F, SP])
        h = sb("h", [T, NT, D])
        xn = sb("xn", [T, NT, D])
        xnT = sb("xnT", [D, SP])
        y = sb("y", [T, NT, D])
        stats = sb("stats", [T, NT, 6])
        mv = sb("mv", [T, NT, 2])
        rst = sb("rst", [T, 4, NT])
        ring = sb("ring", [T, 3, SP])
        mring = sb("mring", [T, 3, SP])
        small = sb("small", [128, 64])
        rowmax = sb("rowmax", [T, UNITS])
        rowsum = sb("rowsum", [T, UNITS])
        rrec = sb("rrec", [T, UNITS])
        stage = sb("stage", [128, 2048])
        oT = sb("oT", [D, 2, CH])
        WIDE = 17424
        arena_words = WIDE + 2 * NT * CH + 4
        arena = nc.lookup_mloc(sb("arena", [128, arena_words])).addr

        def place(name, word, shape, dt=FP32):
            word = (word + 7) // 8 * 8
            words = (math.prod(shape[1:]) + 7) // 8 * 8
            assert word + words <= arena_words
            return nc.alloc_sbuf_tensor_at(name, shape, dt, offset=arena + 4 * word), word + words

        big, o = place("big", 0, [128, WIDE])
        pt, o = place("pt", o, [T, 2, NT * CH])

        q_parts, o = place("q_parts", 0, [128, 2, SP], FR)
        k_high, o = place("k_high", o, [128, 2, SP], FR)
        k_rest, o = place("k_rest", o, [128, 2, SP], FR)
        v_high, o = place("v_high", o, [T, 2, NT, D], FR)
        v_rest, o = place("v_rest", o, [T, 2, NT, D], FR)
        pt_high, o = place("pt_high", o, [T, 2, NT * CH], FR)
        pt_rest, o = place("pt_rest", o, [T, 2, NT * CH], FR)
        NTOP = NT * 2 * NE_HEADS * TOPK
        o = 0
        top = big[0:T, o:o + NTOP].rearrange("p (t s h k) -> p t s h k", t=NT, s=2, h=NE_HEADS)
        o += NTOP
        cand = big[0:T, o:o + TH * NCAND].rearrange("p (g c) -> p g c", g=TH)
        o += TH * NCAND
        left = big[0:T, o:o + TH * NCAND].rearrange("p (g c) -> p g c", g=TH)
        o += TH * NCAND
        prob = big[0:T, o:o + TH * NCAND].rearrange("p (g c) -> p g c", g=TH)
        o += TH * NCAND
        best = big[0:T, o:o + TH * TOPK].rearrange("p (g k) -> p g k", g=TH)
        o += TH * TOPK
        simw = pt[:, 0, 0:2 * NE_HEADS * NKEYS].rearrange("p (g k) -> p g k", k=NKEYS)
        assert o <= 17424
        wexp = pt[:, 1, 0:NT * NCAND].rearrange("p (t c) -> p t c", t=NT)
        hexp = pt[:, 1, 512:512 + NT * NCAND].rearrange("p (t c) -> p t c", t=NT)
        wexpT = stage[0:NCAND, 0:SP]
        q1T = big[:, 0:SP]
        k1T = big[:, SP:2 * SP]
        v1 = big[0:T, 2 * SP:2 * SP + NT * D].rearrange("p (t n) -> p t n", t=NT)
        pt1 = pt[:, :, 0:SP].rearrange("p r (k q) -> p r k q", k=NT)
        o = 0
        v2 = big[0:T, o:o + NT * 256].rearrange("p (t h c) -> p t h c", t=NT, h=H1)
        o += NT * 256
        o2T = big[:, o:o + 2 * SP].rearrange("p (g s) -> p g s", g=2)
        o += 2 * SP
        mpad = big[0:T, o:o + 4 * NT * 128].rearrange("p (g t m) -> p g t m", g=4, t=NT)
        o += 4 * NT * 128
        p2 = big[0:T, o:o + 8 * CH].rearrange("p (r j q) -> p r j q", r=4, j=2)
        o += 8 * CH
        q4, o = place("q4", o, [128, 4, SP], FR)
        k4, o = place("k4", o, [128, 4, SP], FR)
        qk_high, o = place("qk_high", o, [128, 2, SP], FR)
        max_high = sb("max_high", [T, UNITS], FR)

        loaded = signal("loaded")
        cls_loaded = signal("cls_loaded")
        pool_setup = signal("pool_setup")
        dve_setup = signal("dve_setup")
        setup_T = signal("setup_T")
        setup_copied = signal("setup_copied")
        setup_sim = signal("setup_sim")
        setup_done = signal("setup_done")
        go_pool, go_act, go_dve, go_pe = (signal("go_" + e) for e in ("pool", "act", "dve", "pe"))
        x_loaded = signal("x_loaded")
        xT_ps = signal("xT_ps")
        xT_ready = signal("xT_ready")
        tok_ready = signal("tok_ready")
        xn_ready = signal("xn_ready")
        xnT_ps = signal("xnT_ps")
        xnT_ready = signal("xnT_ready")
        job_ps = signal("job_ps")
        high_done = signal("high_done")
        rest_done = signal("rest_done")
        score_ps = signal("score_ps")
        score_sb = signal("score_sb")
        masked = signal("masked")
        prob_ready = signal("prob_ready")
        probT_ps = signal("probT_ps")
        probT_high = signal("probT_high")
        probT_sb = signal("probT_sb")
        pv_done = signal("pv_done")
        oT_ready = signal("oT_ready")
        oproj_done = signal("oproj_done")
        y_added = signal("y_added")
        sim_ps = signal("sim_ps")
        sim_read = signal("sim_read")
        hexp_ps = signal("hexp_ps")
        gelu_done = signal("gelu_done")
        logit_ready = signal("logit_ready")
        cexp_done = signal("cexp_done")
        wexp_ready = signal("wexp_ready")
        wexpT_ps = signal("wexpT_ps")
        wexpT_sb = signal("wexpT_sb")
        eout_ps = signal("eout_ps")
        q1_ps = signal("q1_ps")
        q1_act = signal("q1_act")
        q1_dve = signal("q1_dve")
        ksum_ready = signal("ksum_ready")
        rs_ps = signal("rs_ps")
        rs_part = signal("rs_part")
        rs_all = signal("rs_all")
        s1_ps = signal("s1_ps")
        s1_max = signal("s1_max")
        p1_ready = signal("p1_ready")
        p1T_ps = signal("p1T_ps")
        p1T_sb = signal("p1T_sb")
        o1_ps = signal("o1_ps")
        o1_read = signal("o1_read")
        mean_ready = signal("mean_ready")
        r1_ps = signal("r1_ps")
        r1_ready = signal("r1_ready")
        r2_ps = signal("r2_ps")
        route_in = signal("route_in")
        route_exp = signal("route_exp")
        onehot = signal("onehot")
        onehot_ps = signal("onehot_ps")
        wsel_ready = signal("wsel_ready")
        q2_ps = signal("q2_ps")
        q2_act = signal("q2_act")
        q2_dve = signal("q2_dve")
        PASS1 = 4 * NT * 2
        s2_ps = signal("s2_ps")
        s2_max = signal("s2_max")
        m_ready = signal("m_ready")
        mT_ps = signal("mT_ps")
        q2_shift = signal("q2_shift")
        QUADS = 2 * NC * NT
        s3_ps = signal("s3_ps")
        p3_ready = signal("p3_ready")
        pv3_quad = signal("pv3_quad")
        pads_zero = signal("pads_zero")
        o3_sb = signal("o3_sb")
        sum_ps = signal("sum_ps")
        o3_norm = signal("o3_norm")
        y2_ps = signal("y2_ps")
        round_done = signal("round_done")
        stored = signal("stored")
        dve_seq = signal("dve_seq")
        arrived = signal("arrived")
        in_round = (x_loaded, arrived)
        NLOAD = [0]

        block = ctx.enter_context(nc.Block())

        def end_round(eng, go):
            eng.drain().then_inc(arrived, 1)
            eng.wait_ge(go, 1)
            eng.sem_clear(go)

        @block.sync
        def _(sp):
            def load(dst, src):
                NLOAD[0] += 16
                sp.dma_start(dst, src).then_inc(loaded, 16)

            sp.dma_start(base[:], pe.rearrange("(t p) d -> p t d", p=T)).then_inc(cls_loaded, 16)
            load(w_tok[:], W)
            for twice in range(2):
                for dst, src in ((w_q0, Wq), (w_k0, Wk)):
                    load(dst[:, :, K0 * twice:K0 * (twice + 1)], src.rearrange("m (h d) -> m h d", h=H0))
            load(w_v0[:], Wv)
            load(w_o0[:], Wo.rearrange("(h d) n -> d h n", h=H0))
            for t, v in ((bo_t, bo), (gamma_t, gamma), (beta_t, beta)):
                load(t[:], bass.AP(v.tensor, 0, [[0, T], [1, D]]))
            for s in range(2):
                load(big[:, 0:1024].rearrange("p (h s d) -> p h s d", h=NE_HEADS, s=2)[:, :, s, :],
                     W_q[:, s * 512:(s + 1) * 512].rearrange("m (h d) -> m h d", h=NE_HEADS))
            load(stage[0:NKEYS, 0:1024].rearrange("k (h c) -> k h c", h=NE_HEADS),
                 keys.rearrange("h k s d -> k h (s d)"))
            for i in range(SINGLES):
                load(stage[START[i]:START[i] + RUN[i], 1024:1152], down[TOPK * i:TOPK * i + RUN[i], :])
                load(w_up[START[i]:START[i] + RUN[i], :], up[TOPK * i:TOPK * i + RUN[i], :])
            s0 = START[SINGLES]
            rest = slice(TOPK * SINGLES, TOPK * TOPK)
            load(stage[s0:NCAND, 1024:1152], down[rest, :].rearrange("(i k) d -> i k d", k=TOPK)[:, 0, :])
            load(w_up[s0:NCAND, :], up[rest, :].rearrange("(i k) d -> i k d", k=TOPK)[:, 0, :])
            load(w_a1[:], qkv.rearrange("c d o -> d c o"))
            load(rw1[:], r_w1)
            load(rb1[:], r_b1.rearrange("(n a) -> n a", a=1))
            load(rw2[:], r_w2)
            load(rb2[:], r_b2.rearrange("(a n) -> a n", a=1))
            sp.wait_ge(pool_setup, 1)
            for i, nkv in enumerate(KV_OPTS):
                load(w_all[:, i, 0:D], wq[i])
                for hh in range(H1):
                    kv = hh * nkv // H1
                    for first, w in ((D, wk), (2 * D, wv)):
                        load(w_all[:, i, first + K1 * hh:first + K1 * (hh + 1)], w[i][:, kv * K1:(kv + 1) * K1])
                    load(wo_all[32 * (hh % 4):32 * (hh % 4) + K1, i, hh // 4, :],
                         wo[i][hh * K1:(hh + 1) * K1, :])
            sp.wait_ge(cls_loaded, 16)
            sp.dma_start(base[0:1, 0, :], cls_tok[0, :, :]).then_inc(cls_loaded, 16)
            xs = x.rearrange("b h w f -> b (h w) f")
            with sp.Fori(0, B) as b:
                xb = xs[ds(b, 1), :, :].rearrange("b s f -> (b s) f")
                sp.dma_start(xin[1:T, 0, :], xb[0:T - 1, :]).then_inc(x_loaded, 16)
                sp.dma_start(xin[:, 1:NT - 1, :], xb[T - 1:T * (NT - 1) - 1, :]
                             .rearrange("(t p) f -> p t f", p=T)).then_inc(x_loaded, 16)
                sp.dma_start(xin[0:LAST, NT - 1, :], xb[T * (NT - 1) - 1:SEQ - 1, :]).then_inc(x_loaded, 16)
                sp.wait_ge(round_done, 1)
                ob = out[ds(b, 1), :, :].rearrange("b s d -> (b s) d")
                sp.dma_start(ob[0:T * (NT - 1), :].rearrange("(t p) d -> p t d", p=T),
                             y[:, 0:NT - 1, :]).then_inc(stored, 16)
                sp.dma_start(ob[T * (NT - 1):SEQ, :], y[0:LAST, NT - 1, :]).then_inc(stored, 16)
                sp.wait_ge(stored, 32)
                sp.wait_ge(arrived, 4)
                sp.sem_clear(range(in_round[0].num, in_round[-1].num + 1))
                for go in (go_pool, go_act, go_dve, go_pe):
                    sp.sem_inc(go, 1)

        NL = NLOAD[0]

        @block.gpsimd
        def _(pool):
            nc.gpsimd.memset(w_thrice[:], 0.0)
            nc.gpsimd.memset(marks[:], 0.0)
            nc.gpsimd.memset(wo_all[:], 0.0)
            nc.gpsimd.memset(xin[:], 0.0)
            nc.gpsimd.memset(ident[:], 0.0)
            nc.gpsimd.memset(sum_row[:], 0.0)
            nc.gpsimd.memset(ones1[:], 1.0)
            nc.gpsimd.memset(mring[:], 0.0).then_inc(pool_setup, 1)
            pool.wait_ge(pool_setup, 1)
            nc.gpsimd.affine_select(out=ident[:], in_=ident[:], compare_op=ALU.not_equal, fill=1.0,
                                    base=0, pattern=[[-1, 128]], channel_multiplier=1)
            nc.gpsimd.affine_select(out=sum_row[:].rearrange("p (j c) -> p j c", c=32),
                                    in_=sum_row[:].rearrange("p (j c) -> p j c", c=32),
                                    compare_op=ALU.not_equal, fill=1.0, base=-K1,
                                    pattern=[[-32, 4], [0, 32]], channel_multiplier=1)
            for n, (first, width) in enumerate(((2 * K1, K1), (K1, K1), (3 * K1, 2))):
                nc.gpsimd.affine_select(out=marks[:, n, :, 0:width], in_=marks[:, n, :, 0:width],
                                        compare_op=ALU.not_equal, fill=1.0, base=-first,
                                        pattern=[[-64, 2], [-1, width]], channel_multiplier=1)
            nc.gpsimd.iota(rank_i[:], pattern=[[-T, NT]], base=RANK0,
                           channel_multiplier=-1).then_inc(pool_setup, 1)

            with pool.Fori(0, B) as b:
                for k in range(2):
                    pool.wait_ge(rs_part, k + 1)
                    nc.gpsimd.partition_all_reduce(small[0:T, 4 + k:5 + k], small[0:T, 2 + k:3 + k], T,
                                                   bass.bass_isa.ReduceOp.max).then_inc(rs_all, 1)
                pool.wait_ge(xn_ready, 4)
                nc.gpsimd.memset(v2, 0.0)
                nc.gpsimd.memset(mpad, 0.0).then_inc(pads_zero, 1)
                pool.wait_ge(pads_zero, 1)
                nc.gpsimd.memset(v2[:, :, :, K1:K1 + 1], 1.0).then_inc(pads_zero, 1)
                end_round(pool, go_pool)

        @block.scalar
        def _(act):
            def copy(dst, src):
                return nc.scalar.activation(dst, src, ACT.Copy)

            with act.Fori(0, B) as b:
                def normed_T(k):
                    act.wait_ge(xnT_ps, k + 1)
                    copy(xnT[:].rearrange("p (c w) -> p c w", c=NC), banks(0, 3, D, CH)).then_inc(xnT_ready, 1)
                act.wait_ge(xT_ps, 1)
                copy(xinT[:].rearrange("p (c w) -> p c w", c=NC), banks(0, 3, F, CH)).then_inc(xT_ready, 1)
                normed_T(0)

                def high_part(i):
                    _, _, kind, head, c = JOBS[i]
                    act.wait_ge(job_ps, splits_before(i) + 1)
                    bank = ps[:, job_bank(i) * BANK:(job_bank(i) + 1) * BANK]
                    if kind == "v":
                        copy(v_high[:, head % 2, 3 * c:3 * c + 3, :].rearrange("p t d -> p (t d)"),
                             bank[0:T, 0:3 * D]).then_inc(high_done, 1)
                    else:
                        dst = q_parts if kind == "q" else k_high
                        copy(dst[:, head % 2, CH * c:CH * (c + 1)], bank[:, 0:CH]).then_inc(high_done, 1)

                for i in jobs_at(-1, 0):
                    high_part(i)
                for s in range(UNITS + 9):
                    if s < UNITS:
                        act.wait_ge(score_ps, s + 1)
                        if s >= 3:
                            act.wait_ge(masked, s - 2)
                        copy(ring[:, s % 3, :].rearrange("p (c w) -> p c w", c=NC),
                             banks(0, 3, T, CH)).then_inc(score_sb, 1)
                    for i in jobs_at(s, 0):
                        if JOBS[i][2] != "o":
                            high_part(i)
                    u = s - 1
                    if 0 <= u < UNITS:
                        act.wait_ge(masked, u + 1)
                        nc.scalar.activation(mring[:, u % 3, 0:SEQ], mring[:, u % 3, 0:SEQ], ACT.Exp,
                                             bias=rowmax[:, u:u + 1], scale=-1.0,
                                             accum_out=rowsum[:, u:u + 1]).then_inc(prob_ready, 1)
                    c = (s - 7) // 3
                    if (s - 7) % 3 == 0 and 0 <= c < CHUNKS:
                        act.wait_ge(pv_done, c + 1)
                        if c >= 2:
                            act.wait_ge(oproj_done, c - 1)
                        copy(oT[:, c % 2, :], ps[:, 6 * BANK:6 * BANK + CH]).then_inc(oT_ready, 1)
                    for i in jobs_at(s, 1):
                        high_part(i)
                    u = s - 2
                    if 0 <= u < UNITS:
                        c, j = u // 3, u % 3
                        act.wait_ge(probT_ps, u + 1)
                        if j == 0 and c >= 2:
                            act.wait_ge(pv_done, c - 1)
                        dst = pt_high[:, c % 2, :].rearrange("p (i k q) -> p i k q", i=NC, k=3)
                        copy(dst[:, :, :, T * j:T * (j + 1)],
                             banks(3, 3, T, CH).rearrange("p i (k q) -> p i k q", k=3)).then_inc(probT_high, 1)
                normed_T(1)
                act.wait_ge(hexp_ps, 1)
                nc.scalar.activation(hexp, ps[0:T, 6 * BANK:6 * BANK + NT * NCAND].rearrange(
                    "p (t c) -> p t c", t=NT), ACT.Gelu).then_inc(gelu_done, 1)
                act.wait_ge(logit_ready, 1)
                nc.scalar.activation(prob, prob, ACT.Exp).then_inc(cexp_done, 1)
                act.wait_ge(wexpT_ps, 1)
                copy(wexpT.rearrange("p (c w) -> p c w", c=NC), banks(0, 3, NCAND, CH)).then_inc(wexpT_sb, 1)
                normed_T(2)
                act.wait_ge(q1_ps, 1)
                nc.scalar.activation(q1T.rearrange("p (c w) -> p c w", c=NC), banks(0, 3, D, CH),
                                     ACT.Copy, scale=0.125).then_inc(q1_act, 1)
                for t in range(NT):
                    act.wait_ge(s1_max, t + 1)
                    if t >= 2:
                        act.wait_ge(p1T_ps, t - 1)
                    nc.scalar.activation(mring[:, t % 2, 0:SEQ], ps[0:T, 0:SEQ], ACT.Exp,
                                         bias=rowmax[:, t:t + 1], scale=1.0,
                                         accum_out=rowsum[:, t:t + 1]).then_inc(p1_ready, 1)
                normed_T(3)
                act.wait_ge(route_in, 1)
                nc.scalar.activation(small[0:1, 16:19], small[0:1, 13:16], ACT.Exp,
                                     accum_out=small[0:1, 19:20]).then_inc(route_exp, 1)
                for i in range(8):
                    act.wait_ge(q2_ps, i + 1)
                    if i >= 2:
                        act.wait_ge(q2_dve, i - 1)
                    dst = qk_high[:, i % 2, :].rearrange("p (c w) -> p c w", c=NC)
                    if i % 2 == 0:
                        copy(dst, banks(0, 3, D, CH)).then_inc(q2_act, 1)
                    else:
                        nc.scalar.activation(dst, banks(3, 3, D, CH), ACT.Identity,
                                             bias=mark[:, 2:3], scale=1.0).then_inc(q2_act, 1)
                for n in range(2 * QUADS):
                    kk = LAST if n // 2 % NT == NT - 1 else T
                    act.wait_ge(s3_ps, n + 1)
                    if n >= 4:
                        act.wait_ge(pv3_quad, n // 2 - 1)
                    nc.scalar.activation(p2[0:kk, n % 4, :, :], banks(2 * (n % 3), 2, kk, CH),
                                         ACT.Exp).then_inc(p3_ready, 1)
                end_round(act, go_act)

        @block.vector
        def _(dve):
            dve.wait_ge(pool_setup, 2)
            nc.vector.tensor_copy(rank[:], rank_i[:])
            nc.vector.memset(small[:, 0:1], 1.0)
            nc.vector.memset(small[:, 1:2], 0.0)
            nc.vector.reduce_max(mark[:], marks[:].rearrange("p n j c -> p n (j c)"),
                                 axis=AX).then_inc(dve_setup, 1)
            dve.wait_ge(dve_setup, 1)
            nc.vector.tensor_scalar(q_sign[:], mark[:, 0:1], -1.0, None, ALU.mult)
            nc.vector.tensor_tensor(k_sign[:], mark[:, 2:3], mark[:, 1:2], ALU.subtract).then_inc(dve_setup, 1)
            dve.wait_ge(dve_setup, 2)
            dve.wait_ge(setup_T, 1)
            nc.vector.tensor_copy(big[:, 2048:3072], ps[:, 0:1024])
            nc.vector.tensor_copy(big[:, 3072:3584], ps[:, 1024:1536])
            nc.vector.tensor_copy(w_down[:], ps[:, 1536:1536 + NCAND]).then_inc(setup_copied, 1)
            dve.wait_ge(setup_sim, 1)
            nc.vector.tensor_copy(w_sim[:], ps[:, 4 * BANK:6 * BANK]).then_inc(setup_done, 1)

            with dve.Fori(0, B) as b:
                done = [0]

                def link(ins):
                    done[0] += 1
                    ins.then_inc(dve_seq, 1)
                    dve.wait_ge(dve_seq, done[0])

                def rstd_of(src, eps):
                    for t in range(NT):
                        last = nc.vector.bn_stats(stats[:, t, :], src[:, t, :])
                    link(last)
                    for t in range(NT):
                        last = nc.vector.bn_aggr(mv[:, t, :], stats[:, t, :])
                    link(last)
                    r, a, c, v = (rst[:, i, :] for i in range(4))
                    link(nc.vector.tensor_scalar_add(v, mv[:, :, 1], eps))
                    link(nc.vector.tensor_scalar(r.bitcast(I32), v.bitcast(I32), -0.5, 1597463007.0,
                                                 ALU.mult, ALU.add))
                    for _ in range(3):
                        link(nc.vector.tensor_tensor(a, r, r, ALU.mult))
                        link(nc.vector.scalar_tensor_tensor(c, a, -0.5, v, ALU.mult, ALU.mult))
                        link(nc.vector.scalar_tensor_tensor(r, c, 1.5, r, ALU.add, ALU.mult))

                def normalise(dst, src):
                    for t in range(NT):
                        last = nc.vector.tensor_scalar(dst[:, t, :], src[:, t, :], mv[:, t, 0:1],
                                                       rst[:, 0, t:t + 1], ALU.subtract, ALU.mult)
                    return last

                def over_tiles(v):
                    return v[:].rearrange("p (a n) -> p a n", a=1).broadcast_to([T, NT, D])

                def wide(v):
                    return v[:].rearrange("p (c j) d -> p c (j d)", c=NC)

                dve.wait_ge(tok_ready, 1)
                dve.wait_ge(cls_loaded, 32)
                link(nc.vector.tensor_tensor(wide(h), banks(3, 3, T, 3 * D), wide(base), ALU.add))
                rstd_of(h, LN_EPS)
                normalise(xn, h).then_inc(xn_ready, 1)
                dve.wait_ge(xn_ready, 1)
                nc.vector.tensor_tensor(y[:], xn[:], over_tiles(bo_t), ALU.add)

                def rest(i):
                    _, _, kind, head, c = JOBS[i]
                    dve.wait_ge(high_done, splits_before(i) + 1)
                    bank = ps[:, job_bank(i) * BANK:(job_bank(i) + 1) * BANK]
                    if kind == "v":
                        src = v_high[:, head % 2, 3 * c:3 * c + 3, :].rearrange("p t d -> p (t d)")
                        dst = v_rest[:, head % 2, 3 * c:3 * c + 3, :].rearrange("p t d -> p (t d)")
                        whole = bank[0:T, 0:3 * D]
                    else:
                        part = slice(CH * c, CH * (c + 1))
                        rows = slice(K0, 2 * K0) if kind == "q" else slice(0, 2 * K0)
                        src = (q_parts if kind == "q" else k_high)[rows, head % 2, part]
                        dst = (q_parts if kind == "q" else k_rest)[rows, head % 2, part]
                        whole = bank[rows, 0:CH]
                    nc.vector.tensor_tensor(dst, whole, src.bitcast(FP32), ALU.subtract).then_inc(rest_done, 1)

                for i in jobs_at(-1, 0):
                    rest(i)
                for s in range(UNITS + 9):
                    for i in jobs_at(s, 0):
                        if JOBS[i][2] != "o":
                            rest(i)
                    c = (s - 8) // 3
                    if (s - 8) % 3 == 0 and 0 <= c < CHUNKS:
                        link(nc.vector.reciprocal(rrec[:, 3 * c:3 * c + 3], rowsum[:, 3 * c:3 * c + 3]))
                        dve.wait_ge(oproj_done, c + 1)
                        for j in range(3):
                            t = (3 * c + j) % NT
                            last = nc.vector.scalar_tensor_tensor(
                                y[:, t, :], ps[0:T, 7 * BANK + j * D:7 * BANK + (j + 1) * D],
                                rrec[:, 3 * c + j:3 * c + j + 1], y[:, t, :], ALU.mult, ALU.add)
                        last.then_inc(y_added, 1)
                    if s < UNITS:
                        dve.wait_ge(score_sb, s + 1)
                        if s >= 3:
                            dve.wait_ge(probT_ps, s - 2)
                        link(nc.vector.tensor_scalar(mring[:, s % 3, 0:SEQ], ring[:, s % 3, 0:SEQ], 0.0,
                                                     MASKED * math.sqrt(K0), ALU.is_equal, ALU.mult))
                        nc.vector.tensor_tensor_reduce(
                            out=mring[:, s % 3, 0:SEQ], in0=ring[:, s % 3, 0:SEQ], in1=mring[:, s % 3, 0:SEQ],
                            scale=-1.0 / math.sqrt(K0), scalar=3.0e38, op0=ALU.add, op1=ALU.min,
                            accum_out=rowmax[:, s:s + 1]).then_inc(masked, 1)
                    for i in jobs_at(s, 1):
                        rest(i)
                    u = s - 2
                    if 0 <= u < UNITS:
                        c, j = u // 3, u % 3
                        dve.wait_ge(probT_high, u + 1)
                        part = (slice(0, T), slice(None), slice(None), slice(T * j, T * (j + 1)))
                        high = pt_high[:, c % 2, :].bitcast(FP32).rearrange("p (i k q) -> p i k q", i=NC, k=3)
                        dst = pt_rest[:, c % 2, :].rearrange("p (i k q) -> p i k q", i=NC, k=3)
                        nc.vector.tensor_tensor(dst[part],
                                                banks(3, 3, T, CH).rearrange("p i (k q) -> p i k q", k=3),
                                                high[part], ALU.subtract).then_inc(probT_sb, 1)
                dve.wait_ge(y_added, CHUNKS)
                rstd_of(y, POST_EPS)
                link(normalise(y, y))
                link(nc.vector.tensor_tensor(y[:], y[:], over_tiles(gamma_t), ALU.mult))
                link(nc.vector.tensor_tensor(y[:], y[:], over_tiles(beta_t), ALU.add))
                link(nc.vector.tensor_tensor(h[:], h[:], y[:], ALU.add))

                rstd_of(h, LN_EPS)
                normalise(xn, h).then_inc(xn_ready, 1)
                for t in range(NT):
                    dve.wait_ge(sim_ps, t + 1)
                    side = 3 * (t % 2)
                    sims = ps[0:T, side * BANK:(side + 2) * BANK].rearrange("p (g k) -> p g k", k=NKEYS)
                    tt = top[:, t, :, :, :].rearrange("p s h k -> p (s h) k")
                    for g in range(2 * NE_HEADS):
                        last = nc.vector.max(tt[:, g, 0:8], sims[:, g, :])
                    link(last)
                    for g in range(2 * NE_HEADS):
                        last = nc.vector.match_replace(simw[:, g, :], tt[:, g, 0:8], sims[:, g, :], REMOVED)
                    last.then_inc(sim_read, 1)
                    dve.wait_ge(sim_read, t + 1)
                    for g in range(2 * NE_HEADS):
                        last = nc.vector.max(tt[:, g, 8:16], simw[:, g, :])
                link(last)
                cand4 = cand.rearrange("p (t h) c -> p t h c", t=NT)
                sx, sy = top[:, :, 0, :, :], top[:, :, 1, :, :]
                for i in range(SINGLES):
                    n = RUN[i]
                    nc.vector.tensor_tensor(cand4[:, :, :, START[i]:START[i] + n],
                                            sx[:, :, :, i:i + 1].broadcast_to([T, NT, NE_HEADS, n]),
                                            sy[:, :, :, 0:n], ALU.add)
                n = TOPK - SINGLES
                link(nc.vector.tensor_tensor(cand4[:, :, :, START[SINGLES]:NCAND], sx[:, :, :, SINGLES:TOPK],
                                             sy[:, :, :, 0:1].broadcast_to([T, NT, NE_HEADS, n]), ALU.add))
                for half in range(2):
                    src = cand if half == 0 else left
                    for g in range(TH):
                        last = nc.vector.max(best[:, g, 8 * half:8 * half + 8], src[:, g, :])
                    link(last)
                    for g in range(TH):
                        last = nc.vector.match_replace(left[:, g, :], best[:, g, 8 * half:8 * half + 8],
                                                       src[:, g, :], REMOVED)
                    link(last)
                nc.vector.tensor_tensor(prob, cand, cand[:, :, 0:1].broadcast_to([T, TH, NCAND]),
                                        ALU.subtract).then_inc(logit_ready, 1)
                dve.wait_ge(cexp_done, 1)
                link(nc.vector.scalar_tensor_tensor(prob, left, REMOVED, prob, ALU.is_equal, ALU.mult))
                link(nc.vector.reduce_sum(rowsum[:, 0:TH], prob, axis=AX))
                link(nc.vector.reciprocal(rrec[:, 0:TH], rowsum[:, 0:TH]))
                link(nc.vector.tensor_tensor(prob, prob, rrec[:, 0:TH].rearrange("p (g a) -> p g a", a=1)
                                             .broadcast_to([T, TH, NCAND]), ALU.mult))
                link(nc.vector.reduce_sum(wexp, prob.rearrange("p (t h) c -> p t c h", t=NT), axis=AX))
                dve.wait_ge(gelu_done, 1)
                nc.vector.tensor_tensor(wexp, wexp, hexp, ALU.mult).then_inc(wexp_ready, 1)
                dve.wait_ge(eout_ps, 1)
                link(nc.vector.tensor_tensor(wide(h), banks(3, 3, T, 3 * D), wide(h), ALU.add))

                rstd_of(h, LN_EPS)
                normalise(xn, h).then_inc(xn_ready, 1)
                dve.wait_ge(q1_ps, 2)
                nc.vector.tensor_copy(k1T.rearrange("p (c w) -> p c w", c=NC), banks(3, 3, D, CH)).then_inc(q1_dve, 1)
                dve.wait_ge(q1_dve, 1)
                nc.vector.reduce_sum(small[:, 6:7], k1T[:, 0:SEQ], axis=AX).then_inc(ksum_ready, 1)
                dve.wait_ge(q1_ps, 3)
                nc.vector.tensor_copy(v1.rearrange("p (c j) d -> p c (j d)", c=NC),
                                      banks(0, 3, T, 3 * D)).then_inc(q1_dve, 1)
                dve.wait_ge(rs_ps, 1)
                rs, eq = small[0:T, 20:20 + NT], small[0:T, 30:30 + NT]
                link(nc.vector.memset(rs, -3.0e38))
                nc.vector.tensor_scalar(rs[:, 0:NT - 1], ps[0:T, 6 * BANK:6 * BANK + NT - 1], -1.0, None, ALU.mult)
                link(nc.vector.tensor_scalar(rs[0:LAST, NT - 1:NT], ps[0:LAST, 6 * BANK + NT - 1:6 * BANK + NT],
                                             -1.0, None, ALU.mult))
                nc.vector.reduce_max(small[0:T, 2:3], rs, axis=AX).then_inc(rs_part, 1)
                dve.wait_ge(rs_all, 1)
                link(nc.vector.scalar_tensor_tensor(eq, rs, small[0:T, 4:5], rank[:], ALU.is_equal, ALU.mult))
                nc.vector.reduce_max(small[0:T, 3:4], eq, axis=AX).then_inc(rs_part, 1)
                dve.wait_ge(rs_all, 2)
                link(nc.vector.tensor_tensor(small[0:T, 7:8], small[0:T, 5:6], small[0:T, 1:2], ALU.subtract))
                link(nc.vector.scalar_tensor_tensor(small[0:T, 1:2], small[0:T, 7:8], small[0:T, 0:1],
                                                    small[0:T, 1:2], ALU.mult, ALU.add))
                nc.vector.memset(small[0:T, 0:1], 0.0)
                keep = small[0:T, 40:40 + NT]
                link(nc.vector.tensor_scalar(keep, rank[:], small[0:T, 1:2], None, ALU.not_equal))
                for s in range(NT + 2):
                    if s < NT:
                        dve.wait_ge(s1_ps, s + 1)
                        nc.vector.tensor_reduce(rowmax[:, s:s + 1], ps[0:T, 0:SEQ], axis=AX, op=ALU.max,
                                                negate=True).then_inc(s1_max, 1)
                    u = s - 1
                    if 0 <= u < NT:
                        dve.wait_ge(p1T_ps, u + 1)
                        if u >= 2:
                            dve.wait_ge(o1_ps, u - 1)
                        nc.vector.tensor_copy(pt1[:, u % 2, :, :].rearrange("p (i k) q -> p i (k q)", i=NC),
                                              banks(3, 3, T, CH)).then_inc(p1T_sb, 1)
                    u = s - 2
                    if 0 <= u < NT:
                        link(nc.vector.reciprocal(rrec[:, u:u + 1], rowsum[:, u:u + 1]))
                        link(nc.vector.tensor_tensor(rrec[:, u:u + 1], rrec[:, u:u + 1], keep[:, u:u + 1], ALU.mult))
                        dve.wait_ge(o1_ps, u + 1)
                        nc.vector.scalar_tensor_tensor(
                            h[:, u, :], ps[0:T, (6 + u % 2) * BANK:(6 + u % 2) * BANK + D], rrec[:, u:u + 1],
                            h[:, u, :], ALU.mult, ALU.add).then_inc(o1_read, 1)
                dve.wait_ge(o1_read, NT)

                rstd_of(h, LN_EPS)
                normalise(xn, h).then_inc(xn_ready, 1)
                dve.wait_ge(xnT_ready, 4)
                link(nc.vector.reduce_sum(small[:, 8:9], xnT[:, 0:SEQ], axis=AX))
                nc.vector.tensor_scalar(small[:, 9:10], small[:, 8:9], 1.0 / SEQ, None, ALU.mult).then_inc(mean_ready, 1)
                dve.wait_ge(r1_ps, 1)
                nc.vector.tensor_scalar(small[0:RH, 10:11], ps[0:RH, 6 * BANK:6 * BANK + 1], rb1[:], 0.0,
                                        ALU.add, ALU.max).then_inc(r1_ready, 1)
                dve.wait_ge(r2_ps, 1)
                lg, ex, oh = small[0:1, 13:16], small[0:1, 16:19], small[0:1, 50:53]
                link(nc.vector.tensor_tensor(lg, ps[0:1, 7 * BANK:7 * BANK + 3], rb2[:], ALU.add))
                link(nc.vector.reduce_max(small[0:1, 12:13], lg, axis=AX))
                nc.vector.tensor_scalar(lg, lg, small[0:1, 12:13], None, ALU.subtract).then_inc(route_in, 1)
                dve.wait_ge(route_exp, 1)
                link(nc.vector.reciprocal(small[0:1, 11:12], small[0:1, 19:20]))
                link(nc.vector.tensor_scalar(lg, ex, small[0:1, 11:12], None, ALU.mult))
                link(nc.vector.reduce_max(small[0:1, 12:13], lg, axis=AX))
                link(nc.vector.tensor_scalar(oh, lg, small[0:1, 12:13], None, ALU.is_equal))
                link(nc.vector.tensor_tensor(small[0:1, 54:55], oh[:, 0:1], oh[:, 1:2], ALU.mult))
                link(nc.vector.tensor_tensor(oh[:, 1:2], oh[:, 1:2], small[0:1, 54:55], ALU.subtract))
                link(nc.vector.tensor_tensor(small[0:1, 55:56], oh[:, 0:1], oh[:, 1:2], ALU.add))
                nc.vector.tensor_scalar(oh[:, 2:3], small[0:1, 55:56], -1.0, 1.0, ALU.mult,
                                        ALU.add).then_inc(onehot, 1)
                dve.wait_ge(onehot_ps, 1)
                link(nc.vector.tensor_copy(small[:, 57:60], ps[:, 6 * BANK:6 * BANK + 3]))
                wf = [(w_sel[:], w_all), (wo_sel[:].rearrange("p g n -> p (g n)"), wo_all)]
                for i in range(3):
                    for dst, src in wf:
                        w = src[:, i, :] if src is w_all else src[:, i, :, :].rearrange("p g n -> p (g n)")
                        s = small[:, 57 + i:58 + i]
                        if i == 0:
                            last = nc.vector.tensor_scalar(dst, w, s, None, ALU.mult)
                        else:
                            last = nc.vector.scalar_tensor_tensor(dst, w, s, dst, ALU.mult, ALU.add)
                    link(last)
                for n, scale in enumerate((1.0 / math.sqrt(K1), 1.0)):
                    src = w_sel[:, D * n:D * (n + 1)].rearrange("p (h a c) -> p h a c", h=H1, a=1)
                    last = nc.vector.tensor_scalar(w_thrice[:, n, :, 0:3, :], src.broadcast_to([D, H1, 3, K1]),
                                                   scale, None, ALU.mult)
                last.then_inc(wsel_ready, 1)
                for i in range(8):
                    dve.wait_ge(q2_act, i + 1)
                    dst = (q4 if i % 2 == 0 else k4)[:, i // 2, :].rearrange("p (c w) -> p c w", c=NC)
                    nc.vector.scalar_tensor_tensor(
                        dst, qk_high[:, i % 2, :].bitcast(FP32).rearrange("p (c w) -> p c w", c=NC),
                        (q_sign if i % 2 == 0 else k_sign)[:], banks(3 * (i % 2), 3, D, CH),
                        ALU.mult, ALU.add).then_inc(q2_dve, 1)
                dve.wait_ge(pads_zero, 2)
                dve.wait_ge(q2_ps, 9)
                for c in range(NC):
                    last = nc.vector.tensor_copy(
                        v2[:, 3 * c:3 * c + 3, :, 0:K1],
                        ps[0:T, c * BANK:c * BANK + 3 * D].rearrange("p (t h c) -> p t h c", t=3, h=H1))
                last.then_inc(q2_dve, 1)
                for n in range(PASS1):
                    dve.wait_ge(s2_ps, n + 1)
                    side = 4 * BANK * (n % 2)
                    nc.vector.tensor_reduce(rowmax[:, n:n + 1], ps[0:T, side:side + SEQ], axis=AX, op=ALU.max,
                                            negate=True).then_inc(s2_max, 1)
                dve.wait_ge(s2_max, PASS1)
                link(nc.vector.tensor_copy(max_high[:], rowmax[:]))
                heads = mpad.rearrange("p g t (j m) -> p (g t j) m", j=2)
                nc.vector.tensor_copy(heads[:, :, 3 * K1], max_high[:].bitcast(FP32))
                nc.vector.tensor_tensor(heads[:, :, 3 * K1 + 1], rowmax[:], max_high[:].bitcast(FP32),
                                        ALU.subtract).then_inc(m_ready, 1)
                for g in range(4):
                    dve.wait_ge(mT_ps, g + 1)
                    nc.vector.tensor_tensor(q4[:, g, :].rearrange("p (c w) -> p c w", c=NC),
                                            banks(3 * (g % 2), 3, D, CH),
                                            q4[:, g, :].bitcast(FP32).rearrange("p (c w) -> p c w", c=NC),
                                            ALU.add).then_inc(q2_shift, 1)
                for n in range(2 * NC):
                    g, c = n // NC, n % NC
                    dve.wait_ge(pv3_quad, (n + 1) * NT)
                    nc.vector.tensor_copy(o2T[:, g, CH * c:CH * (c + 1)],
                                          ps[:, 6 * BANK:6 * BANK + CH]).then_inc(o3_sb, 1)
                    dve.wait_ge(sum_ps, n + 1)
                    link(nc.vector.reciprocal(stage[:, 0:CH], ps[:, 7 * BANK:7 * BANK + CH]))
                    nc.vector.tensor_tensor(o2T[:, g, CH * c:CH * (c + 1)], o2T[:, g, CH * c:CH * (c + 1)],
                                            stage[:, 0:CH], ALU.mult).then_inc(o3_norm, 1)
                dve.wait_ge(y2_ps, 1)
                nc.vector.tensor_tensor(wide(y), banks(0, 3, T, 3 * D), wide(h), ALU.add).then_inc(round_done, 1)
                end_round(dve, go_dve)

        @block.tensor
        def _(pe_):
            def mm(out_, lhsT, rhs, start=True, stop=True):
                return nc.tensor.matmul(out_, lhsT, rhs, start=start, stop=stop)

            pe_.wait_ge(pool_setup, 2)
            pe_.wait_ge(loaded, NL)
            for hh in range(NE_HEADS):
                nc.tensor.transpose(ps[:, hh * 128:(hh + 1) * 128], big[:, hh * 128:(hh + 1) * 128], ident[:])
                nc.tensor.transpose(ps[:, 1024 + hh * 64:1024 + (hh + 1) * 64],
                                    stage[0:NKEYS, hh * 128:(hh + 1) * 128], ident[0:NKEYS, 0:NKEYS])
            nc.tensor.transpose(ps[:, 1536:1536 + NCAND], stage[0:NCAND, 1024:1152],
                                ident[0:NCAND, 0:NCAND]).then_inc(setup_T, 1)
            pe_.wait_ge(setup_copied, 1)
            for hh in range(NE_HEADS):
                for s in range(2):
                    r = slice(64 * s, 64 * s + 64)
                    last = mm(ps[:, (4 + s) * BANK + hh * 64:(4 + s) * BANK + (hh + 1) * 64],
                              big[r, 2048 + hh * 128:2048 + (hh + 1) * 128], big[r, 3072 + hh * 64:3072 + (hh + 1) * 64])
            last.then_inc(setup_sim, 1)
            pe_.wait_ge(setup_done, 1)

            with pe_.Fori(0, B) as b:
                def three_chunks(first, lhsT, rhs):
                    for c in range(NC):
                        last = mm(ps[0:lhsT.shape[1], (first + c) * BANK:(first + c) * BANK + CH], lhsT,
                                  rhs[:, CH * c:CH * (c + 1)])
                    return last

                def tokens_T(src, width):
                    for t in range(NT):
                        at = (t // 3) * BANK + (t % 3) * T
                        last = nc.tensor.transpose(ps[0:width, at:at + T], src[:, t, :], ident[0:T, 0:T])
                    return last

                def by_token(first, xT_, rhs):
                    for t in range(NT):
                        at = (first + t // 3) * BANK + (t % 3) * D
                        last = mm(ps[0:T, at:at + D], xT_[:, T * t:T * (t + 1)], rhs)
                    return last

                def normed_T(k):
                    pe_.wait_ge(xn_ready, k + 1)
                    tokens_T(xn, D).then_inc(xnT_ps, 1)
                    pe_.wait_ge(xnT_ready, k + 1)

                pe_.wait_ge(x_loaded, 48)
                tokens_T(xin, F).then_inc(xT_ps, 1)
                pe_.wait_ge(xT_ready, 1)
                by_token(3, xinT, w_tok[:]).then_inc(tok_ready, 1)
                normed_T(0)

                def job(i):
                    _, _, kind, head, c = JOBS[i]
                    if kind == "o":
                        pe_.wait_ge(oT_ready, c + 1)
                    before = i - 8 if i < 3 * NC else i - 1
                    if before >= 0:
                        if JOBS[before][2] == "o":
                            pe_.wait_ge(y_added, JOBS[before][4] + 1)
                        else:
                            pe_.wait_ge(rest_done, splits_before(before) + 1)
                    bank = ps[:, job_bank(i) * BANK:(job_bank(i) + 1) * BANK]
                    for j in range(3 if kind in "ov" else 0):
                        dst = bank[0:T, j * D:(j + 1) * D]
                        if kind == "v":
                            t = 3 * c + j
                            last = mm(dst, xnT[:, T * t:T * (t + 1)], w_v0[:, D * head:D * (head + 1)])
                        else:
                            last = mm(dst, oT[:, c % 2, T * j:T * (j + 1)], w_o0[:, head, :])
                    if kind in "qk":
                        w = w_q0 if kind == "q" else w_k0
                        last = mm(bank[:, 0:CH], w[:, head, :], xnT[:, CH * c:CH * (c + 1)])
                    last.then_inc(oproj_done if kind == "o" else job_ps, 1)

                for i in jobs_at(-1, 0):
                    job(i)
                pe_.wait_ge(rest_done, 3 * NC)
                for s in range(UNITS + 9):
                    if s < UNITS:
                        head, t = s // NT, s % NT
                        if s >= 1:
                            pe_.wait_ge(score_sb, s)
                        if t == 0 and head:
                            pe_.wait_ge(rest_done, splits_through("k", head))
                        for n, k_part in enumerate((k_high, k_rest)):
                            for c in range(NC):
                                last = mm(ps[0:T, c * BANK:c * BANK + CH], q_parts[:, head % 2, T * t:T * (t + 1)],
                                          k_part[:, head % 2, CH * c:CH * (c + 1)], start=(n == 0), stop=(n == 1))
                        last.then_inc(score_ps, 1)
                    for i in jobs_at(s, 0):
                        job(i)
                    c, j = (s - 5) // 3, (s - 5) % 3
                    if 0 <= c < CHUNKS:
                        if j == 0:
                            pe_.wait_ge(probT_sb, 3 * c + 3)
                            if c >= 1:
                                pe_.wait_ge(oT_ready, c)
                            if c % NC == 0:
                                pe_.wait_ge(rest_done, splits_through("v", c // NC))
                        par = (c // NC) % 2
                        for kt in range(3 * j, 3 * j + 3):
                            for n, (vp, pp) in enumerate(((v_high, pt_high), (v_high, pt_rest), (v_rest, pt_high))):
                                last = mm(ps[:, 6 * BANK:6 * BANK + CH], vp[:, par, kt, :],
                                          pp[:, c % 2, CH * kt:CH * (kt + 1)], start=(kt == 0 and n == 0),
                                          stop=(kt == NT - 1 and n == 2))
                        if j == 2:
                            last.then_inc(pv_done, 1)
                    for i in jobs_at(s, 1):
                        job(i)
                    u = s - 2
                    if 0 <= u < UNITS:
                        pe_.wait_ge(prob_ready, u + 1)
                        if u >= 1:
                            pe_.wait_ge(probT_sb, u)
                        for kt in range(NT):
                            at = (3 + kt // 3) * BANK + (kt % 3) * T
                            last = nc.tensor.transpose(ps[0:T, at:at + T], mring[:, u % 3, T * kt:T * (kt + 1)],
                                                       ident[0:T, 0:T])
                        last.then_inc(probT_ps, 1)
                normed_T(1)
                for t in range(NT):
                    at = 6 * BANK + t * NCAND
                    last = mm(ps[0:T, at:at + NCAND], xnT[:, T * t:T * (t + 1)], w_down[:])
                last.then_inc(hexp_ps, 1)
                for t in range(NT):
                    if t >= 2:
                        pe_.wait_ge(sim_read, t - 1)
                    for n in range(2):
                        at = (3 * (t % 2) + n) * BANK
                        last = mm(ps[0:T, at:at + BANK], xnT[:, T * t:T * (t + 1)], w_sim[:, n * BANK:(n + 1) * BANK])
                    last.then_inc(sim_ps, 1)
                pe_.wait_ge(wexp_ready, 1)
                tokens_T(wexp, NCAND).then_inc(wexpT_ps, 1)
                pe_.wait_ge(wexpT_sb, 1)
                by_token(3, wexpT, w_up[:]).then_inc(eout_ps, 1)
                normed_T(2)
                three_chunks(0, w_a1[:, 0, :], xnT).then_inc(q1_ps, 1)
                three_chunks(3, w_a1[:, 1, :], xnT).then_inc(q1_ps, 1)
                pe_.wait_ge(q1_act, 1)
                by_token(0, xnT, w_a1[:, 2, :]).then_inc(q1_ps, 1)
                pe_.wait_ge(ksum_ready, 1)
                for t in range(NT):
                    last = mm(ps[0:T, 6 * BANK + t:6 * BANK + t + 1], q1T[:, T * t:T * (t + 1)], small[:, 6:7])
                last.then_inc(rs_ps, 1)
                pe_.wait_ge(q1_dve, 2)
                pe_.wait_ge(rs_part, 1)
                for s in range(NT + 2):
                    if s < NT:
                        if s >= 1:
                            pe_.wait_ge(p1_ready, s)
                        for c0, c1 in ((0, 512), (512, 1024), (1024, SEQ)):
                            last = mm(ps[0:T, c0:c1], q1T[:, T * s:T * (s + 1)], k1T[:, c0:c1])
                        last.then_inc(s1_ps, 1)
                    u = s - 1
                    if 0 <= u < NT:
                        pe_.wait_ge(p1_ready, u + 1)
                        if u >= 1:
                            pe_.wait_ge(p1T_sb, u)
                        for kt in range(NT):
                            at = (3 + kt // 3) * BANK + (kt % 3) * T
                            last = nc.tensor.transpose(ps[0:T, at:at + T], mring[:, u % 2, T * kt:T * (kt + 1)],
                                                       ident[0:T, 0:T])
                        last.then_inc(p1T_ps, 1)
                    u = s - 2
                    if 0 <= u < NT:
                        pe_.wait_ge(p1T_sb, u + 1)
                        if u >= 2:
                            pe_.wait_ge(o1_read, u - 1)
                        for kt in range(NT):
                            at = (6 + u % 2) * BANK
                            last = mm(ps[0:T, at:at + D], pt1[:, u % 2, kt, :], v1[:, kt, :],
                                      start=(kt == 0), stop=(kt == NT - 1))
                        last.then_inc(o1_ps, 1)
                normed_T(3)
                pe_.wait_ge(mean_ready, 1)
                mm(ps[0:RH, 6 * BANK:6 * BANK + 1], rw1[:], small[:, 9:10]).then_inc(r1_ps, 1)
                pe_.wait_ge(r1_ready, 1)
                mm(ps[0:1, 7 * BANK:7 * BANK + 3], small[0:RH, 10:11], rw2[:]).then_inc(r2_ps, 1)
                pe_.wait_ge(onehot, 1)
                mm(ps[:, 6 * BANK:6 * BANK + 3], ones1[:], small[0:1, 50:53]).then_inc(onehot_ps, 1)
                pe_.wait_ge(wsel_ready, 1)
                for i in range(8):
                    if i >= 2:
                        pe_.wait_ge(q2_dve, i - 1)
                    w = w_thrice[:, i % 2, i // 2 * 2:i // 2 * 2 + 2, :, :].rearrange("p h r c -> p (h r c)")
                    three_chunks(3 * (i % 2), w, xnT).then_inc(q2_ps, 1)
                pe_.wait_ge(q2_dve, 7)
                by_token(0, xnT, w_sel[:, 2 * D:3 * D]).then_inc(q2_ps, 1)
                pe_.wait_ge(q2_dve, 9)
                for n in range(PASS1):
                    g, t, j = n // (2 * NT), n // 2 % NT, n % 2
                    r = slice(64 * j, 64 * j + 64)
                    side = 4 * BANK * (n % 2)
                    if n >= 2:
                        pe_.wait_ge(s2_max, n - 1)
                    for c0, w in ((0, BANK), (BANK, BANK), (2 * BANK, SP - 2 * BANK)):
                        last = mm(ps[0:T, side + c0:side + c0 + w], q4[r, g, T * t:T * (t + 1)],
                                  k4[r, g, c0:c0 + w])
                    last.then_inc(s2_ps, 1)
                pe_.wait_ge(s2_max, PASS1)
                pe_.wait_ge(m_ready, 1)
                for g in range(4):
                    if g >= 2:
                        pe_.wait_ge(q2_shift, g - 1)
                    for t in range(NT):
                        at = (3 * (g % 2) + t // 3) * BANK + (t % 3) * T
                        last = nc.tensor.transpose(ps[:, at:at + T], mpad[:, g, t, :], ident[0:T, 0:T])
                    last.then_inc(mT_ps, 1)
                pe_.wait_ge(q2_shift, 4)

                def values(m):
                    gc, kt = m // NT, m % NT
                    kk = LAST if kt == NT - 1 else T
                    pe_.wait_ge(p3_ready, 2 * m + 2)
                    if kt == 0 and gc >= 1:
                        pe_.wait_ge(o3_sb, gc)
                    for j in range(4):
                        last = mm(ps[32 * j:32 * j + 32, 6 * BANK:6 * BANK + CH],
                                  v2[0:kk, kt, 4 * (gc // NC) + j, :], p2[0:kk, 2 * (m % 2) + j // 2, j % 2, :],
                                  start=(kt == 0), stop=(kt == NT - 1))
                    last.then_inc(pv3_quad, 1)

                def sums(gc):
                    g, c = gc // NC, gc % NC
                    pe_.wait_ge(o3_sb, gc + 1)
                    if gc >= 1:
                        pe_.wait_ge(o3_norm, gc)
                    mm(ps[:, 7 * BANK:7 * BANK + CH], sum_row[:], o2T[:, g, CH * c:CH * (c + 1)]).then_inc(sum_ps, 1)

                for m in range(QUADS + 1):
                    if m < QUADS:
                        gc, kt = m // NT, m % NT
                        c = gc % NC
                        kk = LAST if kt == NT - 1 else T
                        for n in (2 * m, 2 * m + 1):
                            if n >= 3:
                                pe_.wait_ge(p3_ready, n - 2)
                            for j in range(2):
                                r = slice(64 * j, 64 * j + 64)
                                g = 2 * (gc // NC) + n % 2
                                at = (2 * (n % 3) + j) * BANK
                                last = mm(ps[0:kk, at:at + CH], k4[r, g, T * kt:T * kt + kk],
                                          q4[r, g, CH * c:CH * (c + 1)])
                            last.then_inc(s3_ps, 1)
                    if m >= 1:
                        values(m - 1)
                    if m > NT and (m - 1) % NT == 1:
                        sums((m - 1) // NT - 1)
                sums(2 * NC - 1)
                pe_.wait_ge(o3_norm, 2 * NC)
                for t in range(NT):
                    at = (t // 3) * BANK + (t % 3) * D
                    for g in range(2):
                        last = mm(ps[0:T, at:at + D], o2T[:, g, T * t:T * (t + 1)], wo_sel[:, g, :],
                                  start=(g == 0), stop=(g == 1))
                last.then_inc(y2_ps, 1)
                end_round(pe_, go_pe)


_INS = ['x', 'cls_tok', 'L0_tok_W', 'L0_attn_Wq', 'L0_attn_Wk', 'L0_attn_Wv', 'L0_attn_Wo', 'L0_attn_bo',
        'L0_attn_gamma', 'L0_attn_beta', 'L0_ffn_W_q', 'L0_ffn_keys', 'L0_ffn_down_embed', 'L0_ffn_up_embed',
        'L1_attn_kernel', 'L1_ffn_r_w1', 'L1_ffn_r_b1', 'L1_ffn_r_w2', 'L1_ffn_r_b2', 'L1_ffn_wq0', 'L1_ffn_wk0',
        'L1_ffn_wv0', 'L1_ffn_wo0', 'L1_ffn_wq1', 'L1_ffn_wk1', 'L1_ffn_wv1', 'L1_ffn_wo1', 'L1_ffn_wq2',
        'L1_ffn_wk2', 'L1_ffn_wv2', 'L1_ffn_wo2']


def position_table():
    position = np.arange(2 * (SEQ - 1), dtype=np.float32)[:, None]
    div_term = np.exp(np.arange(0, D, 2, dtype=np.float32) * (-math.log(10000.0) / D))
    pe = np.zeros((2 * (SEQ - 1), D), dtype=np.float32)
    pe[:, 0::2] = np.sin(position * div_term)
    pe[:, 1::2] = np.cos(position * div_term)
    table = np.zeros((SP, D), np.float32)
    table[1:SEQ] = pe[:SEQ - 1]
    return table


def kernel(**inputs):
    import concourse.bacc as bacc
    from concourse.bass_utils import run_bass_kernel_spmd

    nc = bacc.Bacc("TRN2", target_bir_lowering=False, num_devices=1)
    arrays, aps = {}, {}
    for name in _INS + ['position_table']:
        a = position_table() if name == 'position_table' else np.ascontiguousarray(inputs[name])
        arrays[f"in_{name}"] = a
        aps[name] = nc.dram_tensor(f"in_{name}", a.shape, mybir.dt.from_np(a.dtype), kind="ExternalInput").ap()
    out = nc.dram_tensor("out", (B, SEQ, D), FP32, kind="ExternalOutput").ap()
    a = [aps[n] for n in _INS]
    last = a[19:]
    vit_kernel(nc, *a[:19], [last[0], last[4], last[8]], [last[1], last[5], last[9]],
               [last[2], last[6], last[10]], [last[3], last[7], last[11]], aps['position_table'], out)
    r = run_bass_kernel_spmd(nc, [arrays], core_ids=[0])
    return r.results[0]["out"]
```

```python
import math
from contextlib import ExitStack

import numpy as np

import concourse.bass as bass
from concourse import mybir

FP32 = mybir.dt.float32
I32 = mybir.dt.int32
FR = mybir.dt.float32r
ALU = mybir.AluOpType
ACT = mybir.ActivationFunctionType
AX = mybir.AxisListType.X
ds = bass.ds

B = 8
SEQ = 1025
F = 29
D = 128
H0, K0 = 8, 64
NE_HEADS, NKEYS, DKEY, TOPK = 8, 64, 64, 16
H1, K1 = 8, 16
KV_OPTS = (8, 4, 1)
RH = D // 4

T = 114
NT = 9
SP = T * NT
CH = 342
NC = SP // CH
LAST = SEQ - (NT - 1) * T
BANK = 512

RUN = [TOPK // (i + 1) for i in range(TOPK)]
START = [sum(RUN[:i]) for i in range(TOPK)]
NCAND = sum(RUN)
SINGLES = next(i for i in range(TOPK) if RUN[i] == 1)
REMOVED = -3.0e38
TH = NT * NE_HEADS

UNITS = H0 * NT
CHUNKS = H0 * NC
RANK0 = 2048

LN_EPS = 1e-5
POST_EPS = 1e-6
MASKED = -1.0e9


def lookahead_jobs():
    jobs = [(-1, 0, kind, 0, c) for kind in "qk" for c in range(NC)]
    for s in range(UNITS + 10):
        head, r = s // NT, s % NT
        if s >= 9 and (s - 9) % 3 == 0 and (s - 9) // 3 < CHUNKS:
            jobs.append((s, 0, "o", (s - 9) // 3 // NC, (s - 9) // 3))
        if head + 1 < H0:
            if r % 3 != 0:
                n = 2 * (r // 3) + r % 3 - 1
                jobs.append((s, 0, "qk"[n // 3], head + 1, n % 3))
            if r in (6, 7, 8):
                jobs.append((s, 1, "v", head + 1, r - 6))
        if s < NC:
            jobs.append((s, 1, "v", 0, s))
    return jobs


JOBS = lookahead_jobs()


def jobs_at(slot, place):
    return [i for i, job in enumerate(JOBS) if job[:2] == (slot, place)]


def splits_before(i):
    return sum(job[2] != "o" for job in JOBS[:i])


def splits_through(kind, head):
    return splits_before(max(i for i, job in enumerate(JOBS) if job[2:4] == (kind, head))) + 1


def job_bank(i):
    return i if i < 2 * NC else 7


def vit_kernel(nc, x, cls_tok, W, Wq, Wk, Wv, Wo, bo, gamma, beta, W_q, keys, down, up, qkv,
               r_w1, r_b1, r_w2, r_b2, wq, wk, wv, wo, pe, out):
    ctx = ExitStack()
    with ctx:
        def sb(name, shape, dt=FP32):
            return ctx.enter_context(nc.sbuf_tensor(name, shape, dt))

        def signal(name):
            return ctx.enter_context(nc.semaphore(name))

        ps = ctx.enter_context(nc.psum_tensor("ps", [128, 8 * BANK], FP32))

        def banks(first, n, p, w):
            return ps[0:p, first * BANK:(first + n) * BANK].rearrange("p (n w) -> p n w", n=n)[:, :, 0:w]

        ident = sb("ident", [128, 128])
        sum_row = sb("sum_row", [128, 128])
        marks = sb("marks", [128, 3, 2, K1])
        mark = sb("mark", [128, 3])
        q_sign = sb("q_sign", [128, 1])
        k_sign = sb("k_sign", [128, 1])
        ones1 = sb("ones1", [1, 128])
        rank_i = sb("rank_i", [T, NT], I32)
        rank = sb("rank", [T, NT])
        base = sb("base", [T, NT, D])
        w_tok = sb("w_tok", [F, D])
        w_q0 = sb("w_q0", [D, H0, 2 * K0])
        w_k0 = sb("w_k0", [D, H0, 2 * K0])
        w_v0 = sb("w_v0", [D, H0 * D])
        w_o0 = sb("w_o0", [D, H0, D])
        bo_t = sb("bo_t", [T, D])
        gamma_t = sb("gamma_t", [T, D])
        beta_t = sb("beta_t", [T, D])
        w_sim = sb("w_sim", [D, 2 * NE_HEADS * NKEYS])
        w_down = sb("w_down", [D, NCAND])
        w_up = sb("w_up", [NCAND, D])
        w_a1 = sb("w_a1", [D, 3, D])
        rw1 = sb("rw1", [D, RH])
        rb1 = sb("rb1", [RH, 1])
        rw2 = sb("rw2", [RH, 3])
        rb2 = sb("rb2", [1, 3])
        w_all = sb("w_all", [D, 3, 3 * D])
        wo_all = sb("wo_all", [128, 3, 2, D])
        w_sel = sb("w_sel", [D, 3 * D])
        w_thrice = sb("w_thrice", [D, 2, H1, 4, K1])
        wo_sel = sb("wo_sel", [128, 2, D])

        xin = sb("xin", [T, NT, F])
        xinT = sb("xinT", [F, SP])
        h = sb("h", [T, NT, D])
        h_new = sb("h_new", [T, NT, D])
        xn = sb("xn", [T, NT, D])
        xnT = sb("xnT", [D, SP])
        y = sb("y", [T, NT, D])
        stats = sb("stats", [T, NT, 6])
        mv = sb("mv", [T, NT, 2])
        rst = sb("rst", [T, 4, NT])
        ring = sb("ring", [T, 3, SP])
        mring = sb("mring", [T, 3, SP])
        small = sb("small", [128, 64])
        rowmax = sb("rowmax", [T, UNITS])
        rowsum = sb("rowsum", [T, UNITS])
        rrec = sb("rrec", [T, UNITS])
        stage = sb("stage", [128, 2048])
        oT = sb("oT", [D, 2, CH])
        WIDE = 17424
        arena_words = WIDE + 2 * NT * CH + 4
        arena = nc.lookup_mloc(sb("arena", [128, arena_words])).addr

        def place(name, word, shape, dt=FP32):
            word = (word + 7) // 8 * 8
            words = (math.prod(shape[1:]) + 7) // 8 * 8
            assert word + words <= arena_words
            return nc.alloc_sbuf_tensor_at(name, shape, dt, offset=arena + 4 * word), word + words

        big, o = place("big", 0, [128, WIDE])

        q_parts, o = place("q_parts", 0, [128, 2, SP], FR)
        k_high, o = place("k_high", o, [128, 2, SP], FR)
        k_rest, o = place("k_rest", o, [128, 2, SP], FR)
        v_high, o = place("v_high", o, [T, 2, NT, D], FR)
        v_rest, o = place("v_rest", o, [T, 2, NT, D], FR)
        pt_high, o = place("pt_high", o, [T, 2, NT * CH], FR)
        pt_rest, o = place("pt_rest", o, [T, 2, NT * CH], FR)
        q1T = big[:, 0:SP]
        k1T = big[:, SP:2 * SP]
        v1 = big[0:T, 2 * SP:2 * SP + NT * D].rearrange("p (t n) -> p t n", t=NT)
        o = 2 * SP + NT * D
        pt1 = big[0:T, o:o + 2 * SP].rearrange("p (r k q) -> p r k q", r=2, k=NT)
        o = 0
        v2 = big[0:T, o:o + NT * 256].rearrange("p (t h c) -> p t h c", t=NT, h=H1)
        o += NT * 256
        o2T = big[:, o:o + 2 * SP].rearrange("p (g s) -> p g s", g=2)
        o += 2 * SP
        p2 = big[0:T, o:o + 8 * CH].rearrange("p (r j q) -> p r j q", r=4, j=2)
        o += 8 * CH
        q4, o = place("q4", o, [128, 4, SP], FR)
        k4, o = place("k4", o, [128, 4, SP], FR)
        free_later = o
        qk_high, o = place("qk_high", o, [128, 2, SP], FR)
        mpad, o = place("mpad", o, [T, 4, NT, 128])
        xnT_look, o = place("xnT_look", o, [D, SP])
        hexp, o = place("hexp", o, [T, NT, NCAND])
        top, o = place("top", free_later, [T, 2, 2, NE_HEADS, TOPK])
        simw, o = place("simw", o, [T, 2 * NE_HEADS, NKEYS])
        cand, o = place("cand", o, [T, 2, NE_HEADS, NCAND])
        left, o = place("left", o, [T, 2, NE_HEADS, NCAND])
        prob, o = place("prob", o, [T, 4, NE_HEADS, NCAND])
        best, o = place("best", o, [T, 2, NE_HEADS, TOPK])
        wexp, o = place("wexp", o, [T, NT, NCAND])
        wexpT = stage[0:NCAND, 0:SP]
        max_high = sb("max_high", [T, UNITS], FR)

        loaded = signal("loaded")
        cls_loaded = signal("cls_loaded")
        pool_setup = signal("pool_setup")
        dve_setup = signal("dve_setup")
        setup_T = signal("setup_T")
        setup_copied = signal("setup_copied")
        setup_sim = signal("setup_sim")
        setup_done = signal("setup_done")
        go_pool, go_act, go_dve, go_pe = (signal("go_" + e) for e in ("pool", "act", "dve", "pe"))
        x_loaded = signal("x_loaded")
        stored = signal("stored")
        xT_ps = signal("xT_ps")
        xT_ready = signal("xT_ready")
        tok_ready = signal("tok_ready")
        tok_read = signal("tok_read")
        STAGES = ("first", "lookup", "second", "last")
        xn_ready = [signal(f"xn_ready_{stage_}") for stage_ in STAGES]
        xnT_ps = [signal(f"xnT_ps_{stage_}") for stage_ in STAGES]
        xnT_ready = [signal(f"xnT_ready_{stage_}") for stage_ in STAGES]
        job_ps = signal("job_ps")
        high_done = signal("high_done")
        rest_done = signal("rest_done")
        score_ps = signal("score_ps")
        score_sb = signal("score_sb")
        masked = signal("masked")
        prob_ready = signal("prob_ready")
        probT_ps = signal("probT_ps")
        probT_high = signal("probT_high")
        probT_sb = signal("probT_sb")
        pv_done = signal("pv_done")
        oT_ready = signal("oT_ready")
        oproj_done = signal("oproj_done")
        y_added = signal("y_added")
        sim_ps = signal("sim_ps")
        sim_read = signal("sim_read")
        top_ready = signal("top_ready")
        cand_ready = signal("cand_ready")
        marked = signal("marked")
        weighed = signal("weighed")
        wsum_ready = signal("wsum_ready")
        wnorm_ready = signal("wnorm_ready")
        pool_seq = signal("pool_seq")
        hexp_ps = signal("hexp_ps")
        gelu_done = signal("gelu_done")
        logit_ready = signal("logit_ready")
        cexp_done = signal("cexp_done")
        wexp_ready = signal("wexp_ready")
        wexpT_ps = signal("wexpT_ps")
        wexpT_sb = signal("wexpT_sb")
        eout_ps = signal("eout_ps")
        q1_ps = signal("q1_ps")
        q1_act = signal("q1_act")
        q1_dve = signal("q1_dve")
        ksum_ready = signal("ksum_ready")
        rs_ps = signal("rs_ps")
        rs_part = signal("rs_part")
        rs_all = signal("rs_all")
        s1_ps = signal("s1_ps")
        s1_max = signal("s1_max")
        p1_ready = signal("p1_ready")
        p1T_ps = signal("p1T_ps")
        p1T_sb = signal("p1T_sb")
        o1_ps = signal("o1_ps")
        o1_read = signal("o1_read")
        mean_ready = signal("mean_ready")
        r1_ps = signal("r1_ps")
        r1_ready = signal("r1_ready")
        r2_ps = signal("r2_ps")
        route_in = signal("route_in")
        route_exp = signal("route_exp")
        onehot = signal("onehot")
        onehot_ps = signal("onehot_ps")
        wsel_ready = signal("wsel_ready")
        q2_ps = signal("q2_ps")
        q2_act = signal("q2_act")
        q2_dve = signal("q2_dve")
        PASS1 = 4 * NT * 2
        s2_ps = signal("s2_ps")
        s2_max = signal("s2_max")
        m_ready = signal("m_ready")
        mT_ps = signal("mT_ps")
        q2_shift = signal("q2_shift")
        QUADS = 2 * NC * NT
        LOOK_STEP = QUADS // NT
        s3_ps = signal("s3_ps")
        p3_ready = signal("p3_ready")
        pv3_quad = signal("pv3_quad")
        pads_zero = signal("pads_zero")
        o3_sb = signal("o3_sb")
        sum_ps = signal("sum_ps")
        o3_norm = signal("o3_norm")
        y2_ps = signal("y2_ps")
        round_done = signal("round_done")
        dve_seq = signal("dve_seq")
        arrived = signal("arrived")
        in_round = (xT_ps, arrived)
        NLOAD = [0]

        block = ctx.enter_context(nc.Block())

        def end_round(eng, go):
            eng.drain().then_inc(arrived, 1)
            eng.wait_ge(go, 1)
            eng.sem_clear(go)

        @block.sync
        def _(sp):
            def load(dst, src):
                NLOAD[0] += 16
                sp.dma_start(dst, src).then_inc(loaded, 16)

            sp.dma_start(base[:], pe.rearrange("(t p) d -> p t d", p=T)).then_inc(cls_loaded, 16)
            load(w_tok[:], W)
            for twice in range(2):
                for dst, src in ((w_q0, Wq), (w_k0, Wk)):
                    load(dst[:, :, K0 * twice:K0 * (twice + 1)], src.rearrange("m (h d) -> m h d", h=H0))
            load(w_v0[:], Wv)
            load(w_o0[:], Wo.rearrange("(h d) n -> d h n", h=H0))
            for t, v in ((bo_t, bo), (gamma_t, gamma), (beta_t, beta)):
                load(t[:], bass.AP(v.tensor, 0, [[0, T], [1, D]]))
            for s in range(2):
                load(big[:, 0:1024].rearrange("p (h s d) -> p h s d", h=NE_HEADS, s=2)[:, :, s, :],
                     W_q[:, s * 512:(s + 1) * 512].rearrange("m (h d) -> m h d", h=NE_HEADS))
            load(stage[0:NKEYS, 0:1024].rearrange("k (h c) -> k h c", h=NE_HEADS),
                 keys.rearrange("h k s d -> k h (s d)"))
            for i in range(SINGLES):
                load(stage[START[i]:START[i] + RUN[i], 1024:1152], down[TOPK * i:TOPK * i + RUN[i], :])
                load(w_up[START[i]:START[i] + RUN[i], :], up[TOPK * i:TOPK * i + RUN[i], :])
            s0 = START[SINGLES]
            rest = slice(TOPK * SINGLES, TOPK * TOPK)
            load(stage[s0:NCAND, 1024:1152], down[rest, :].rearrange("(i k) d -> i k d", k=TOPK)[:, 0, :])
            load(w_up[s0:NCAND, :], up[rest, :].rearrange("(i k) d -> i k d", k=TOPK)[:, 0, :])
            load(w_a1[:], qkv.rearrange("c d o -> d c o"))
            load(rw1[:], r_w1)
            load(rb1[:], r_b1.rearrange("(n a) -> n a", a=1))
            load(rw2[:], r_w2)
            load(rb2[:], r_b2.rearrange("(a n) -> a n", a=1))
            sp.wait_ge(pool_setup, 1)
            for i, nkv in enumerate(KV_OPTS):
                load(w_all[:, i, 0:D], wq[i])
                for hh in range(H1):
                    kv = hh * nkv // H1
                    for first, w in ((D, wk), (2 * D, wv)):
                        load(w_all[:, i, first + K1 * hh:first + K1 * (hh + 1)], w[i][:, kv * K1:(kv + 1) * K1])
                    load(wo_all[32 * (hh % 4):32 * (hh % 4) + K1, i, hh // 4, :],
                         wo[i][hh * K1:(hh + 1) * K1, :])
            sp.wait_ge(cls_loaded, 16)
            sp.dma_start(base[0:1, 0, :], cls_tok[0, :, :]).then_inc(cls_loaded, 16)
            xs = x.rearrange("b h w f -> b (h w) f")
            def load_image(b):
                xb = xs[ds(b, 1), :, :].rearrange("b s f -> (b s) f")
                sp.dma_start(xin[1:T, 0, :], xb[0:T - 1, :]).then_inc(x_loaded, 16)
                sp.dma_start(xin[:, 1:NT - 1, :], xb[T - 1:T * (NT - 1) - 1, :]
                             .rearrange("(t p) f -> p t f", p=T)).then_inc(x_loaded, 16)
                sp.dma_start(xin[0:LAST, NT - 1, :], xb[T * (NT - 1) - 1:SEQ - 1, :]).then_inc(x_loaded, 16)

            def finish(b):
                sp.wait_ge(round_done, 1)
                ob = out[ds(b, 1), :, :].rearrange("b s d -> (b s) d")
                sp.dma_start(ob[0:T * (NT - 1), :].rearrange("(t p) d -> p t d", p=T),
                             y[:, 0:NT - 1, :]).then_inc(stored, 16)
                sp.dma_start(ob[T * (NT - 1):SEQ, :], y[0:LAST, NT - 1, :]).then_inc(stored, 16)

            def next_round():
                sp.wait_ge(arrived, 4)
                sp.sem_clear(range(in_round[0].num, in_round[-1].num + 1))
                for go in (go_pool, go_act, go_dve, go_pe):
                    sp.sem_inc(go, 1)

            sp.sem_inc(stored, 32)
            sp.wait_ge(pool_setup, 1)
            load_image(0)
            sp.wait_ge(xT_ps, 1)
            load_image(1)
            sp.wait_ge(xT_ps, 2)
            load_image(2)
            next_round()
            with sp.Fori(1, B - 2) as b:
                finish(b - 1)
                sp.wait_ge(xT_ps, 1)
                load_image(b + 2)
                next_round()
            finish(B - 3)
            sp.wait_ge(xT_ps, 1)
            load_image(B - 1)
            next_round()
            finish(B - 2)
            next_round()
            finish(B - 1)
            next_round()
            sp.wait_ge(stored, 32)

        NL = NLOAD[0]

        @block.gpsimd
        def _(pool):
            nc.gpsimd.memset(w_thrice[:], 0.0)
            nc.gpsimd.memset(marks[:], 0.0)
            nc.gpsimd.memset(wo_all[:], 0.0)
            nc.gpsimd.memset(xin[:], 0.0)
            nc.gpsimd.memset(ident[:], 0.0)
            nc.gpsimd.memset(sum_row[:], 0.0)
            nc.gpsimd.memset(ones1[:], 1.0)
            nc.gpsimd.memset(mring[:], 0.0).then_inc(pool_setup, 1)
            pool.wait_ge(pool_setup, 1)
            nc.gpsimd.affine_select(out=ident[:], in_=ident[:], compare_op=ALU.not_equal, fill=1.0,
                                    base=0, pattern=[[-1, 128]], channel_multiplier=1)
            nc.gpsimd.affine_select(out=sum_row[:].rearrange("p (j c) -> p j c", c=32),
                                    in_=sum_row[:].rearrange("p (j c) -> p j c", c=32),
                                    compare_op=ALU.not_equal, fill=1.0, base=-K1,
                                    pattern=[[-32, 4], [0, 32]], channel_multiplier=1)
            for n, (first, width) in enumerate(((2 * K1, K1), (K1, K1), (3 * K1, 2))):
                nc.gpsimd.affine_select(out=marks[:, n, :, 0:width], in_=marks[:, n, :, 0:width],
                                        compare_op=ALU.not_equal, fill=1.0, base=-first,
                                        pattern=[[-64, 2], [-1, width]], channel_multiplier=1)
            nc.gpsimd.iota(rank_i[:], pattern=[[-T, NT]], base=RANK0,
                           channel_multiplier=-1).then_inc(pool_setup, 1)

            def one_round(new, old):
                done = [0]

                def link(ins):
                    done[0] += 1
                    ins.then_inc(pool_seq, 1)
                    pool.wait_ge(pool_seq, done[0])

                if old:
                    for k in range(2):
                        pool.wait_ge(rs_part, k + 1)
                        nc.gpsimd.partition_all_reduce(small[0:T, 4 + k:5 + k], small[0:T, 2 + k:3 + k], T,
                                                       bass.bass_isa.ReduceOp.max).then_inc(rs_all, 1)
                    pool.wait_ge(xn_ready[3], 1)
                    nc.gpsimd.memset(v2, 0.0)
                    nc.gpsimd.memset(mpad[:], 0.0).then_inc(pads_zero, 1)
                    pool.wait_ge(pads_zero, 1)
                    nc.gpsimd.memset(v2[:, :, :, K1:K1 + 1], 1.0).then_inc(pads_zero, 1)
                for t in range(NT + 2 if new else 0):
                    if t < NT:
                        pool.wait_ge(top_ready, t + 1)
                        sums, logits = cand[:, t % 2, :, :], prob[:, t % 4, :, :]
                        sx, sy = top[:, t % 2, 0, :, :], top[:, t % 2, 1, :, :]
                        for i in range(SINGLES):
                            n = RUN[i]
                            nc.gpsimd.tensor_tensor(sums[:, :, START[i]:START[i] + n],
                                                    sx[:, :, i:i + 1].broadcast_to([T, NE_HEADS, n]),
                                                    sy[:, :, 0:n], ALU.add)
                        n = TOPK - SINGLES
                        nc.gpsimd.tensor_tensor(sums[:, :, START[SINGLES]:NCAND], sx[:, :, SINGLES:TOPK],
                                                sy[:, :, 0:1].broadcast_to([T, NE_HEADS, n]),
                                                ALU.add).then_inc(cand_ready, 1)
                        pool.wait_ge(cand_ready, t + 1)
                        nc.gpsimd.tensor_tensor(logits, sums, sums[:, :, 0:1].broadcast_to([T, NE_HEADS, NCAND]),
                                                ALU.subtract).then_inc(logit_ready, 1)
                    u = t - 1
                    if 0 <= u < NT:
                        pool.wait_ge(marked, u + 1)
                        pool.wait_ge(cexp_done, u + 1)
                        marks_, w = left[:, u % 2, :, :], prob[:, u % 4, :, :]
                        link(nc.gpsimd.tensor_scalar(marks_, marks_, REMOVED, None, ALU.is_equal))
                        nc.gpsimd.tensor_tensor(w, w, marks_, ALU.mult).then_inc(weighed, 1)
                    u = t - 2
                    if 0 <= u < NT:
                        pool.wait_ge(wsum_ready, u + 1)
                        w = prob[:, u % 4, :, :]
                        over = rrec[:, NE_HEADS * u:NE_HEADS * (u + 1)].rearrange("p (g a) -> p g a", a=1)
                        nc.gpsimd.tensor_tensor(w, w, over.broadcast_to([T, NE_HEADS, NCAND]),
                                                ALU.mult).then_inc(wnorm_ready, 1)
                end_round(pool, go_pool)

            one_round(True, False)
            with pool.Fori(1, B) as b:
                one_round(True, True)
            one_round(False, True)

        @block.scalar
        def _(act):
            def copy(dst, src):
                return nc.scalar.activation(dst, src, ACT.Copy)

            def one_round(new, old):
                def normed_T(k):
                    act.wait_ge(xnT_ps[k], 1)
                    copy((xnT_look if k == 1 else xnT)[:].rearrange("p (c w) -> p c w", c=NC),
                         banks(0 if k else 3, 3, D, CH)).then_inc(xnT_ready[k], 1)

                def patches(n):
                    act.wait_ge(xT_ps, n)
                    copy(xinT[:].rearrange("p (c w) -> p c w", c=NC), banks(0, 3, F, CH)).then_inc(xT_ready, 1)

                def result_chunk(gc):
                    g, c = gc // NC, gc % NC
                    act.wait_ge(pv3_quad, (gc + 1) * NT)
                    copy(o2T[:, g, CH * c:CH * (c + 1)], ps[:, 4 * BANK:4 * BANK + CH]).then_inc(o3_sb, 1)

                def look_exp(t):
                    act.wait_ge(logit_ready, t + 1)
                    nc.scalar.activation(prob[:, t % 4, :, :], prob[:, t % 4, :, :], ACT.Exp).then_inc(cexp_done, 1)

                def look_hidden():
                    act.wait_ge(hexp_ps, 1)
                    nc.scalar.activation(hexp[:], ps[0:T, 7 * BANK:7 * BANK + NT * NCAND].rearrange(
                        "p (t c) -> p t c", t=NT), ACT.Gelu).then_inc(gelu_done, 1)

                def first_half():
                    if not old:
                        patches(1)
                    normed_T(0)

                    def high_part(i):
                        _, _, kind, head, c = JOBS[i]
                        act.wait_ge(job_ps, splits_before(i) + 1)
                        bank = ps[:, job_bank(i) * BANK:(job_bank(i) + 1) * BANK]
                        if kind == "v":
                            copy(v_high[:, head % 2, 3 * c:3 * c + 3, :].rearrange("p t d -> p (t d)"),
                                 bank[0:T, 0:3 * D]).then_inc(high_done, 1)
                        else:
                            dst = q_parts if kind == "q" else k_high
                            copy(dst[:, head % 2, CH * c:CH * (c + 1)], bank[:, 0:CH]).then_inc(high_done, 1)

                    for i in jobs_at(-1, 0):
                        high_part(i)
                    for s in range(UNITS + 10):
                        if s < UNITS:
                            act.wait_ge(score_ps, s + 1)
                            if s >= 3:
                                act.wait_ge(masked, s - 2)
                            copy(ring[:, s % 3, :].rearrange("p (c w) -> p c w", c=NC),
                                 banks(0, 3, T, CH)).then_inc(score_sb, 1)
                        for i in jobs_at(s, 0):
                            if JOBS[i][2] != "o":
                                high_part(i)
                        u = s - 1
                        if 0 <= u < UNITS:
                            act.wait_ge(masked, u + 1)
                            nc.scalar.activation(mring[:, u % 3, 0:SEQ], mring[:, u % 3, 0:SEQ], ACT.Exp,
                                                 bias=rowmax[:, u:u + 1], scale=-1.0,
                                                 accum_out=rowsum[:, u:u + 1]).then_inc(prob_ready, 1)
                        c = (s - 8) // 3
                        if (s - 8) % 3 == 0 and 0 <= c < CHUNKS:
                            act.wait_ge(pv_done, c + 1)
                            if c >= 2:
                                act.wait_ge(oproj_done, c - 1)
                            copy(oT[:, c % 2, :], ps[:, 6 * BANK:6 * BANK + CH]).then_inc(oT_ready, 1)
                        for i in jobs_at(s, 1):
                            high_part(i)
                        u = s - 2
                        if 0 <= u < UNITS:
                            c, j = u // 3, u % 3
                            act.wait_ge(probT_ps, u + 1)
                            if j == 0 and c >= 2:
                                act.wait_ge(pv_done, c - 1)
                            dst = pt_high[:, c % 2, :].rearrange("p (i k q) -> p i k q", i=NC, k=3)
                            copy(dst[:, :, :, T * j:T * (j + 1)],
                                 banks(3, 3, T, CH).rearrange("p i (k q) -> p i k q", k=3)).then_inc(probT_high, 1)

                def second_half():
                    normed_T(2)
                    act.wait_ge(q1_ps, 1)
                    nc.scalar.activation(q1T.rearrange("p (c w) -> p c w", c=NC), banks(0, 3, D, CH),
                                         ACT.Copy, scale=0.125).then_inc(q1_act, 1)
                    act.wait_ge(q1_ps, 3)
                    copy(v1.rearrange("p (c j) d -> p c (j d)", c=NC), banks(0, 3, T, 3 * D)).then_inc(q1_act, 1)
                    for s in range(NT + 1):
                        if s < NT:
                            act.wait_ge(s1_max, s + 1)
                            if s >= 2:
                                act.wait_ge(p1T_ps, s - 1)
                            nc.scalar.activation(mring[:, s % 2, 0:SEQ], ps[0:T, 0:SEQ], ACT.Exp,
                                                 bias=rowmax[:, s:s + 1], scale=1.0,
                                                 accum_out=rowsum[:, s:s + 1]).then_inc(p1_ready, 1)
                        u = s - 1
                        if u >= 0:
                            act.wait_ge(p1T_ps, u + 1)
                            if u >= 2:
                                act.wait_ge(o1_ps, u - 1)
                            copy(pt1[:, u % 2, :, :].rearrange("p (i k) q -> p i (k q)", i=NC),
                                 banks(3, 3, T, CH)).then_inc(p1T_sb, 1)
                    if new:
                        normed_T(1)
                    normed_T(3)
                    act.wait_ge(route_in, 1)
                    nc.scalar.activation(small[0:1, 16:19], small[0:1, 13:16], ACT.Exp,
                                         accum_out=small[0:1, 19:20]).then_inc(route_exp, 1)
                    if new:
                        look_hidden()
                    for i in range(8):
                        act.wait_ge(q2_ps, i + 1)
                        if i >= 2:
                            act.wait_ge(q2_dve, i - 1)
                        dst = qk_high[:, i % 2, :].rearrange("p (c w) -> p c w", c=NC)
                        if i % 2 == 0:
                            copy(dst, banks(0, 3, D, CH)).then_inc(q2_act, 1)
                        else:
                            nc.scalar.activation(dst, banks(3, 3, D, CH), ACT.Identity,
                                                 bias=mark[:, 2:3], scale=1.0).then_inc(q2_act, 1)

                if new:
                    first_half()
                if old:
                    second_half()
                else:
                    normed_T(1)
                    look_hidden()
                for m in range(QUADS + LOOK_STEP):
                    if old and m < QUADS:
                        kk = LAST if m % NT == NT - 1 else T
                        for n in (2 * m, 2 * m + 1):
                            act.wait_ge(s3_ps, n + 1)
                            if n >= 4:
                                act.wait_ge(pv3_quad, n // 2 - 1)
                            nc.scalar.activation(p2[0:kk, n % 4, :, :], banks(2 * (n % 2), 2, kk, CH),
                                                 ACT.Exp).then_inc(p3_ready, 1)
                    if old and m > 0 and m % NT == 0 and m <= QUADS:
                        result_chunk(m // NT - 1)
                    if new and m > LOOK_STEP and m % LOOK_STEP == 2:
                        look_exp(m // LOOK_STEP - 1)
                if new:
                    patches(1 if old else 2)
                    act.wait_ge(wexpT_ps, 1)
                    copy(wexpT.rearrange("p (c w) -> p c w", c=NC), banks(3, 3, NCAND, CH)).then_inc(wexpT_sb, 1)
                end_round(act, go_act)

            one_round(True, False)
            with act.Fori(1, B) as b:
                one_round(True, True)
            one_round(False, True)

        @block.vector
        def _(dve):
            dve.wait_ge(pool_setup, 2)
            nc.vector.tensor_copy(rank[:], rank_i[:])
            nc.vector.memset(small[:, 0:1], 1.0)
            nc.vector.memset(small[:, 1:2], 0.0)
            nc.vector.reduce_max(mark[:], marks[:].rearrange("p n j c -> p n (j c)"),
                                 axis=AX).then_inc(dve_setup, 1)
            dve.wait_ge(dve_setup, 1)
            nc.vector.tensor_scalar(q_sign[:], mark[:, 0:1], -1.0, None, ALU.mult)
            nc.vector.tensor_tensor(k_sign[:], mark[:, 2:3], mark[:, 1:2], ALU.subtract).then_inc(dve_setup, 1)
            dve.wait_ge(dve_setup, 2)
            dve.wait_ge(setup_T, 1)
            nc.vector.tensor_copy(big[:, 2048:3072], ps[:, 0:1024])
            nc.vector.tensor_copy(big[:, 3072:3584], ps[:, 1024:1536])
            nc.vector.tensor_copy(w_down[:], ps[:, 1536:1536 + NCAND]).then_inc(setup_copied, 1)
            dve.wait_ge(setup_sim, 1)
            nc.vector.tensor_copy(w_sim[:], ps[:, 4 * BANK:6 * BANK]).then_inc(setup_done, 1)

            def one_round(new, old):
                done = [0]

                def link(ins):
                    done[0] += 1
                    ins.then_inc(dve_seq, 1)
                    dve.wait_ge(dve_seq, done[0])

                def stats_of(src):
                    for t in range(NT):
                        last = nc.vector.bn_stats(stats[:, t, :], src[:, t, :])
                    link(last)

                def rstd(eps):
                    for t in range(NT):
                        last = nc.vector.bn_aggr(mv[:, t, :], stats[:, t, :])
                    link(last)
                    r, a, c, v = (rst[:, i, :] for i in range(4))
                    link(nc.vector.tensor_scalar_add(v, mv[:, :, 1], eps))
                    link(nc.vector.tensor_scalar(r.bitcast(I32), v.bitcast(I32), -0.5, 1597463007.0,
                                                 ALU.mult, ALU.add))
                    for _ in range(3):
                        link(nc.vector.tensor_tensor(a, r, r, ALU.mult))
                        link(nc.vector.scalar_tensor_tensor(c, a, -0.5, v, ALU.mult, ALU.mult))
                        link(nc.vector.scalar_tensor_tensor(r, c, 1.5, r, ALU.add, ALU.mult))

                def rstd_of(src, eps):
                    stats_of(src)
                    rstd(eps)

                def normalise(dst, src):
                    for t in range(NT):
                        last = nc.vector.tensor_scalar(dst[:, t, :], src[:, t, :], mv[:, t, 0:1],
                                                       rst[:, 0, t:t + 1], ALU.subtract, ALU.mult)
                    return last

                def over_tiles(v):
                    return v[:].rearrange("p (a n) -> p a n", a=1).broadcast_to([T, NT, D])

                def wide(v):
                    return v[:].rearrange("p (c j) d -> p c (j d)", c=NC)

                def row_max(first, dst):
                    return nc.vector.tensor_reduce(dst, ps[0:T, first:first + SEQ], axis=AX, op=ALU.max, negate=True)

                def y_free():
                    dve.wait_ge(stored, 32)
                    dve.sem_clear(stored)

                def first_half():
                    if not old:
                        dve.wait_ge(tok_ready, 1)
                    dve.wait_ge(cls_loaded, 32)
                    nc.vector.tensor_tensor(wide(h_new), banks(0, 3, T, 3 * D), wide(base), ALU.add).then_inc(tok_read, 1)
                    if old:
                        y_free()
                    else:
                        dve.wait_ge(tok_read, 1)
                        rstd_of(h_new, LN_EPS)
                        normalise(xn, h_new).then_inc(xn_ready[0], 1)
                        dve.wait_ge(xn_ready[0], 1)
                    nc.vector.tensor_tensor(y[:], xn[:], over_tiles(bo_t), ALU.add)

                    def rest(i):
                        _, _, kind, head, c = JOBS[i]
                        dve.wait_ge(high_done, splits_before(i) + 1)
                        bank = ps[:, job_bank(i) * BANK:(job_bank(i) + 1) * BANK]
                        if kind == "v":
                            src = v_high[:, head % 2, 3 * c:3 * c + 3, :].rearrange("p t d -> p (t d)")
                            dst = v_rest[:, head % 2, 3 * c:3 * c + 3, :].rearrange("p t d -> p (t d)")
                            whole = bank[0:T, 0:3 * D]
                        else:
                            part = slice(CH * c, CH * (c + 1))
                            rows = slice(K0, 2 * K0) if kind == "q" else slice(0, 2 * K0)
                            src = (q_parts if kind == "q" else k_high)[rows, head % 2, part]
                            dst = (q_parts if kind == "q" else k_rest)[rows, head % 2, part]
                            whole = bank[rows, 0:CH]
                        nc.vector.tensor_tensor(dst, whole, src.bitcast(FP32), ALU.subtract).then_inc(rest_done, 1)

                    for i in jobs_at(-1, 0):
                        rest(i)
                    for s in range(UNITS + 10):
                        for i in jobs_at(s, 0):
                            if JOBS[i][2] != "o":
                                rest(i)
                        c = (s - 9) // 3
                        if (s - 9) % 3 == 0 and 0 <= c < CHUNKS:
                            link(nc.vector.reciprocal(rrec[:, 3 * c:3 * c + 3], rowsum[:, 3 * c:3 * c + 3]))
                            dve.wait_ge(oproj_done, c + 1)
                            for j in range(3):
                                t = (3 * c + j) % NT
                                last = nc.vector.scalar_tensor_tensor(
                                    y[:, t, :], ps[0:T, 7 * BANK + j * D:7 * BANK + (j + 1) * D],
                                    rrec[:, 3 * c + j:3 * c + j + 1], y[:, t, :], ALU.mult, ALU.add)
                            last.then_inc(y_added, 1)
                        if s < UNITS:
                            dve.wait_ge(score_sb, s + 1)
                            if s >= 3:
                                dve.wait_ge(probT_ps, s - 2)
                            link(nc.vector.tensor_scalar(mring[:, s % 3, 0:SEQ], ring[:, s % 3, 0:SEQ], 0.0,
                                                         MASKED * math.sqrt(K0), ALU.is_equal, ALU.mult))
                            nc.vector.tensor_tensor_reduce(
                                out=mring[:, s % 3, 0:SEQ], in0=ring[:, s % 3, 0:SEQ], in1=mring[:, s % 3, 0:SEQ],
                                scale=-1.0 / math.sqrt(K0), scalar=3.0e38, op0=ALU.add, op1=ALU.min,
                                accum_out=rowmax[:, s:s + 1]).then_inc(masked, 1)
                        for i in jobs_at(s, 1):
                            rest(i)
                        u = s - 2
                        if 0 <= u < UNITS:
                            c, j = u // 3, u % 3
                            dve.wait_ge(probT_high, u + 1)
                            part = (slice(0, T), slice(None), slice(None), slice(T * j, T * (j + 1)))
                            high = pt_high[:, c % 2, :].bitcast(FP32).rearrange("p (i k q) -> p i k q", i=NC, k=3)
                            dst = pt_rest[:, c % 2, :].rearrange("p (i k q) -> p i k q", i=NC, k=3)
                            nc.vector.tensor_tensor(dst[part],
                                                    banks(3, 3, T, CH).rearrange("p i (k q) -> p i k q", k=3),
                                                    high[part], ALU.subtract).then_inc(probT_sb, 1)
                        if old and s == UNITS:
                            stats_of(h)
                        elif old and s == UNITS + 1:
                            rstd(LN_EPS)
                        elif old and s == UNITS + 2:
                            normalise(xn, h).then_inc(xn_ready[2], 1)

                result_parts = (
                    lambda: (dve.wait_ge(y_added, CHUNKS), stats_of(y)),
                    lambda: rstd(POST_EPS),
                    lambda: link(normalise(y, y)),
                    lambda: (link(nc.vector.tensor_tensor(y[:], y[:], over_tiles(gamma_t), ALU.mult)),
                             link(nc.vector.tensor_tensor(y[:], y[:], over_tiles(beta_t), ALU.add))),
                    lambda: link(nc.vector.tensor_tensor(h_new[:], h_new[:], y[:], ALU.add)),
                    lambda: stats_of(h_new),
                    lambda: rstd(LN_EPS),
                    lambda: normalise(xn, h_new).then_inc(xn_ready[1], 1))

                def second_half():
                    if not new:
                        rstd_of(h, LN_EPS)
                        normalise(xn, h).then_inc(xn_ready[2], 1)
                    dve.wait_ge(q1_ps, 2)
                    nc.vector.tensor_copy(k1T.rearrange("p (c w) -> p c w", c=NC), banks(3, 3, D, CH)).then_inc(q1_dve, 1)
                    dve.wait_ge(q1_dve, 1)
                    nc.vector.reduce_sum(small[:, 6:7], k1T[:, 0:SEQ], axis=AX).then_inc(ksum_ready, 1)
                    keep = small[0:T, 40:40 + NT]
                    for s in range(NT + 2):
                        if s < NT:
                            dve.wait_ge(s1_ps, s + 1)
                            row_max(0, rowmax[:, s:s + 1]).then_inc(s1_max, 1)
                        if s == 1:
                            dve.wait_ge(rs_ps, 1)
                            rs, eq = small[0:T, 20:20 + NT], small[0:T, 30:30 + NT]
                            link(nc.vector.memset(rs, -3.0e38))
                            nc.vector.tensor_scalar(rs[:, 0:NT - 1], ps[0:T, 6 * BANK:6 * BANK + NT - 1], -1.0, None, ALU.mult)
                            link(nc.vector.tensor_scalar(rs[0:LAST, NT - 1:NT], ps[0:LAST, 6 * BANK + NT - 1:6 * BANK + NT],
                                                         -1.0, None, ALU.mult))
                            nc.vector.reduce_max(small[0:T, 2:3], rs, axis=AX).then_inc(rs_part, 1)
                            dve.wait_ge(rs_all, 1)
                            link(nc.vector.scalar_tensor_tensor(eq, rs, small[0:T, 4:5], rank[:], ALU.is_equal, ALU.mult))
                            nc.vector.reduce_max(small[0:T, 3:4], eq, axis=AX).then_inc(rs_part, 1)
                            dve.wait_ge(rs_all, 2)
                            link(nc.vector.tensor_tensor(small[0:T, 7:8], small[0:T, 5:6], small[0:T, 1:2], ALU.subtract))
                            link(nc.vector.scalar_tensor_tensor(small[0:T, 1:2], small[0:T, 7:8], small[0:T, 0:1],
                                                                small[0:T, 1:2], ALU.mult, ALU.add))
                            nc.vector.memset(small[0:T, 0:1], 0.0)
                            link(nc.vector.tensor_scalar(keep, rank[:], small[0:T, 1:2], None, ALU.not_equal))
                        u = s - 2
                        if 0 <= u < NT:
                            link(nc.vector.reciprocal(rrec[:, u:u + 1], rowsum[:, u:u + 1]))
                            link(nc.vector.tensor_tensor(rrec[:, u:u + 1], rrec[:, u:u + 1], keep[:, u:u + 1], ALU.mult))
                            dve.wait_ge(o1_ps, u + 1)
                            nc.vector.scalar_tensor_tensor(
                                h[:, u, :], ps[0:T, (6 + u % 2) * BANK:(6 + u % 2) * BANK + D], rrec[:, u:u + 1],
                                h[:, u, :], ALU.mult, ALU.add).then_inc(o1_read, 1)
                        if new and 0 <= u < len(result_parts):
                            if u == len(result_parts) - 1:
                                dve.wait_ge(xnT_ps[2], 1)
                            result_parts[u]()
                    dve.wait_ge(o1_read, NT)

                    rstd_of(h, LN_EPS)
                    if new:
                        dve.wait_ge(xnT_ps[1], 1)
                    normalise(xn, h).then_inc(xn_ready[3], 1)
                    dve.wait_ge(xnT_ready[3], 1)
                    link(nc.vector.reduce_sum(small[:, 8:9], xnT[:, 0:SEQ], axis=AX))
                    nc.vector.tensor_scalar(small[:, 9:10], small[:, 8:9], 1.0 / SEQ, None, ALU.mult).then_inc(mean_ready, 1)
                    dve.wait_ge(r1_ps, 1)
                    nc.vector.tensor_scalar(small[0:RH, 10:11], ps[0:RH, 6 * BANK:6 * BANK + 1], rb1[:], 0.0,
                                            ALU.add, ALU.max).then_inc(r1_ready, 1)
                    dve.wait_ge(r2_ps, 1)
                    lg, ex, oh = small[0:1, 13:16], small[0:1, 16:19], small[0:1, 50:53]
                    link(nc.vector.tensor_tensor(lg, ps[0:1, 7 * BANK:7 * BANK + 3], rb2[:], ALU.add))
                    link(nc.vector.reduce_max(small[0:1, 12:13], lg, axis=AX))
                    nc.vector.tensor_scalar(lg, lg, small[0:1, 12:13], None, ALU.subtract).then_inc(route_in, 1)
                    dve.wait_ge(route_exp, 1)
                    link(nc.vector.reciprocal(small[0:1, 11:12], small[0:1, 19:20]))
                    link(nc.vector.tensor_scalar(lg, ex, small[0:1, 11:12], None, ALU.mult))
                    link(nc.vector.reduce_max(small[0:1, 12:13], lg, axis=AX))
                    link(nc.vector.tensor_scalar(oh, lg, small[0:1, 12:13], None, ALU.is_equal))
                    link(nc.vector.tensor_tensor(small[0:1, 54:55], oh[:, 0:1], oh[:, 1:2], ALU.mult))
                    link(nc.vector.tensor_tensor(oh[:, 1:2], oh[:, 1:2], small[0:1, 54:55], ALU.subtract))
                    link(nc.vector.tensor_tensor(small[0:1, 55:56], oh[:, 0:1], oh[:, 1:2], ALU.add))
                    nc.vector.tensor_scalar(oh[:, 2:3], small[0:1, 55:56], -1.0, 1.0, ALU.mult,
                                            ALU.add).then_inc(onehot, 1)
                    dve.wait_ge(onehot_ps, 1)
                    link(nc.vector.tensor_copy(small[:, 57:60], ps[:, 6 * BANK:6 * BANK + 3]))

                    def choose(dst, parts):
                        link(nc.vector.tensor_scalar(dst, parts[0], small[:, 57:58], None, ALU.mult))
                        for i in (1, 2):
                            link(nc.vector.scalar_tensor_tensor(dst, parts[i], small[:, 57 + i:58 + i], dst,
                                                                ALU.mult, ALU.add))

                    choose(w_sel[:], [w_all[:, i, :] for i in range(3)])
                    for n, scale in enumerate((1.0 / math.sqrt(K1), 1.0)):
                        src = w_sel[:, D * n:D * (n + 1)].rearrange("p (h a c) -> p h a c", h=H1, a=1)
                        last = nc.vector.tensor_scalar(w_thrice[:, n, :, 0:3, :], src.broadcast_to([D, H1, 3, K1]),
                                                       scale, None, ALU.mult)
                    last.then_inc(wsel_ready, 1)
                    choose(wo_sel[:].rearrange("p g n -> p (g n)"),
                           [wo_all[:, i, :, :].rearrange("p g n -> p (g n)") for i in range(3)])
                    for i in range(8):
                        dve.wait_ge(q2_act, i + 1)
                        dst = (q4 if i % 2 == 0 else k4)[:, i // 2, :].rearrange("p (c w) -> p c w", c=NC)
                        nc.vector.scalar_tensor_tensor(
                            dst, qk_high[:, i % 2, :].bitcast(FP32).rearrange("p (c w) -> p c w", c=NC),
                            (q_sign if i % 2 == 0 else k_sign)[:], banks(3 * (i % 2), 3, D, CH),
                            ALU.mult, ALU.add).then_inc(q2_dve, 1)
                    dve.wait_ge(pads_zero, 2)
                    dve.wait_ge(q2_ps, 9)
                    for c in range(NC):
                        last = nc.vector.tensor_copy(
                            v2[:, 3 * c:3 * c + 3, :, 0:K1],
                            ps[0:T, c * BANK:c * BANK + 3 * D].rearrange("p (t h c) -> p t h c", t=3, h=H1))
                    last.then_inc(q2_dve, 1)
                    for n in range(PASS1):
                        dve.wait_ge(s2_ps, n + 1)
                        row_max(4 * BANK * (n % 2), rowmax[:, n:n + 1]).then_inc(s2_max, 1)
                    dve.wait_ge(s2_max, PASS1)
                    link(nc.vector.tensor_copy(max_high[:], rowmax[:]))
                    heads = mpad[:].rearrange("p g t (j m) -> p (g t j) m", j=2)
                    nc.vector.tensor_copy(heads[:, :, 3 * K1], max_high[:].bitcast(FP32))
                    nc.vector.tensor_tensor(heads[:, :, 3 * K1 + 1], rowmax[:], max_high[:].bitcast(FP32),
                                            ALU.subtract).then_inc(m_ready, 1)
                    for g in range(4):
                        dve.wait_ge(mT_ps, g + 1)
                        nc.vector.tensor_tensor(q4[:, g, :].rearrange("p (c w) -> p c w", c=NC),
                                                banks(3 * (g % 2), 3, D, CH),
                                                q4[:, g, :].bitcast(FP32).rearrange("p (c w) -> p c w", c=NC),
                                                ALU.add).then_inc(q2_shift, 1)

                def best_of_sides(t):
                    dve.wait_ge(sim_ps, t + 1)
                    sims = ps[0:T, 6 * BANK:8 * BANK].rearrange("p (g k) -> p g k", k=NKEYS)
                    tt = top[:, t % 2, :, :, :].rearrange("p s h k -> p (s h) k")
                    for g in range(2 * NE_HEADS):
                        last = nc.vector.max(tt[:, g, 0:8], sims[:, g, :])
                    link(last)
                    for g in range(2 * NE_HEADS):
                        last = nc.vector.match_replace(simw[:, g, :], tt[:, g, 0:8], sims[:, g, :], REMOVED)
                    last.then_inc(sim_read, 1)
                    dve.wait_ge(sim_read, t + 1)
                    for g in range(2 * NE_HEADS):
                        last = nc.vector.max(tt[:, g, 8:16], simw[:, g, :])
                    last.then_inc(top_ready, 1)

                def mark_best(t):
                    dve.wait_ge(cand_ready, t + 1)
                    for half in range(2):
                        src = (cand if half == 0 else left)[:, t % 2, :, :]
                        places = slice(8 * half, 8 * half + 8)
                        for g in range(NE_HEADS):
                            last = nc.vector.max(best[:, t % 2, g, places], src[:, g, :])
                        link(last)
                        for g in range(NE_HEADS):
                            last = nc.vector.match_replace(left[:, t % 2, g, :], best[:, t % 2, g, places],
                                                           src[:, g, :], REMOVED)
                        if half == 0:
                            link(last)
                    last.then_inc(marked, 1)

                def weight_sums(t):
                    g = slice(NE_HEADS * t, NE_HEADS * (t + 1))
                    dve.wait_ge(weighed, t + 1)
                    link(nc.vector.reduce_sum(rowsum[:, g], prob[:, t % 4, :, :], axis=AX))
                    nc.vector.reciprocal(rrec[:, g], rowsum[:, g]).then_inc(wsum_ready, 1)

                def over_heads(t):
                    dve.wait_ge(wnorm_ready, t + 1)
                    return nc.vector.reduce_sum(wexp[:, t, :], prob[:, t % 4, :, :].rearrange("p h c -> p c h"),
                                                axis=AX)

                def normalise_chunk(n):
                    g, c = n // NC, n % NC
                    dve.wait_ge(sum_ps, n + 1)
                    recip = stage[:, SP:SP + CH]
                    link(nc.vector.reciprocal(recip, ps[:, 5 * BANK:5 * BANK + CH]))
                    nc.vector.tensor_tensor(o2T[:, g, CH * c:CH * (c + 1)], o2T[:, g, CH * c:CH * (c + 1)],
                                            recip, ALU.mult).then_inc(o3_norm, 1)

                if new:
                    first_half()
                else:
                    y_free()
                if old:
                    second_half()
                else:
                    for part in result_parts:
                        part()
                chunks = 0
                for t in range(NT + 3):
                    if new:
                        if t < NT:
                            best_of_sides(t)
                        if 0 <= t - 1 < NT:
                            mark_best(t - 1)
                        if 0 <= t - 2 < NT:
                            weight_sums(t - 2)
                        if t - 3 >= 0:
                            last = over_heads(t - 3)
                    while old and chunks < 2 * NC and (NT * (chunks + 1) + LOOK_STEP - 1) // LOOK_STEP <= t:
                        normalise_chunk(chunks)
                        chunks += 1
                if new:
                    link(last)
                    dve.wait_ge(gelu_done, 1)
                    nc.vector.tensor_tensor(wexp[:], wexp[:], hexp[:], ALU.mult).then_inc(wexp_ready, 1)
                    dve.wait_ge(tok_ready, 1 if old else 2)
                    dve.wait_ge(xnT_ps[3 if old else 1], 1)
                    link(nc.vector.tensor_tensor(wide(xn), banks(0, 3, T, 3 * D), wide(base), ALU.add))
                    stats_of(xn)
                if old:
                    dve.wait_ge(y2_ps, 1)
                    nc.vector.tensor_tensor(wide(y), banks(3, 3, T, 3 * D), wide(h), ALU.add).then_inc(round_done, 1)
                if new:
                    rstd(LN_EPS)
                    normalise(xn, xn)
                    dve.wait_ge(eout_ps, 1)
                    nc.vector.tensor_tensor(wide(h), banks(3, 3, T, 3 * D), wide(h_new), ALU.add)
                end_round(dve, go_dve)

            one_round(True, False)
            with dve.Fori(1, B) as b:
                one_round(True, True)
            one_round(False, True)

        @block.tensor
        def _(pe_):
            def mm(out_, lhsT, rhs, start=True, stop=True):
                return nc.tensor.matmul(out_, lhsT, rhs, start=start, stop=stop)

            pe_.wait_ge(pool_setup, 2)
            pe_.wait_ge(loaded, NL)
            for hh in range(NE_HEADS):
                nc.tensor.transpose(ps[:, hh * 128:(hh + 1) * 128], big[:, hh * 128:(hh + 1) * 128], ident[:])
                nc.tensor.transpose(ps[:, 1024 + hh * 64:1024 + (hh + 1) * 64],
                                    stage[0:NKEYS, hh * 128:(hh + 1) * 128], ident[0:NKEYS, 0:NKEYS])
            nc.tensor.transpose(ps[:, 1536:1536 + NCAND], stage[0:NCAND, 1024:1152],
                                ident[0:NCAND, 0:NCAND]).then_inc(setup_T, 1)
            pe_.wait_ge(setup_copied, 1)
            for hh in range(NE_HEADS):
                for s in range(2):
                    r = slice(64 * s, 64 * s + 64)
                    last = mm(ps[:, (4 + s) * BANK + hh * 64:(4 + s) * BANK + (hh + 1) * 64],
                              big[r, 2048 + hh * 128:2048 + (hh + 1) * 128], big[r, 3072 + hh * 64:3072 + (hh + 1) * 64])
            last.then_inc(setup_sim, 1)
            pe_.wait_ge(setup_done, 1)

            def one_round(new, old):
                def three_chunks(first, lhsT, rhs):
                    for c in range(NC):
                        last = mm(ps[0:lhsT.shape[1], (first + c) * BANK:(first + c) * BANK + CH], lhsT,
                                  rhs[:, CH * c:CH * (c + 1)])
                    return last

                def tokens_T(src, width, first=0):
                    for t in range(NT):
                        at = (first + t // 3) * BANK + (t % 3) * T
                        last = nc.tensor.transpose(ps[0:width, at:at + T], src[:, t, :], ident[0:T, 0:T])
                    return last

                def by_token(first, xT_, rhs):
                    for t in range(NT):
                        at = (first + t // 3) * BANK + (t % 3) * D
                        last = mm(ps[0:T, at:at + D], xT_[:, T * t:T * (t + 1)], rhs)
                    return last

                def normed_T(k):
                    if k or not old:
                        pe_.wait_ge(xn_ready[k], 1)
                    tokens_T(xn, D, 0 if k else 3).then_inc(xnT_ps[k], 1)
                    pe_.wait_ge(xnT_ready[k], 1)

                def patches(n):
                    pe_.wait_ge(x_loaded, 48)
                    pe_.sem_clear(x_loaded)
                    tokens_T(xin, F).then_inc(xT_ps, 1)
                    pe_.wait_ge(xT_ready, n)
                    by_token(0, xinT, w_tok[:]).then_inc(tok_ready, 1)

                def first_half():
                    if not old:
                        patches(1)
                    normed_T(0)
                    pe_.wait_ge(tok_read, 1)

                    def job(i):
                        _, _, kind, head, c = JOBS[i]
                        if kind == "o":
                            pe_.wait_ge(oT_ready, c + 1)
                        before = i - 1
                        if before >= 2 * NC:
                            if JOBS[before][2] == "o":
                                pe_.wait_ge(y_added, JOBS[before][4] + 1)
                            else:
                                pe_.wait_ge(rest_done, splits_before(before) + 1)
                        bank = ps[:, job_bank(i) * BANK:(job_bank(i) + 1) * BANK]
                        for j in range(3 if kind in "ov" else 0):
                            dst = bank[0:T, j * D:(j + 1) * D]
                            if kind == "v":
                                t = 3 * c + j
                                last = mm(dst, xnT[:, T * t:T * (t + 1)], w_v0[:, D * head:D * (head + 1)])
                            else:
                                last = mm(dst, oT[:, c % 2, T * j:T * (j + 1)], w_o0[:, head, :])
                        if kind in "qk":
                            w = w_q0 if kind == "q" else w_k0
                            last = mm(bank[:, 0:CH], w[:, head, :], xnT[:, CH * c:CH * (c + 1)])
                        last.then_inc(oproj_done if kind == "o" else job_ps, 1)

                    for i in jobs_at(-1, 0):
                        job(i)
                    pe_.wait_ge(rest_done, 2 * NC)
                    for s in range(UNITS + 10):
                        if s < UNITS:
                            head, t = s // NT, s % NT
                            if s >= 1:
                                pe_.wait_ge(score_sb, s)
                            if t == 0 and head:
                                pe_.wait_ge(rest_done, splits_through("k", head))
                            for n, k_part in enumerate((k_high, k_rest)):
                                for c in range(NC):
                                    last = mm(ps[0:T, c * BANK:c * BANK + CH], q_parts[:, head % 2, T * t:T * (t + 1)],
                                              k_part[:, head % 2, CH * c:CH * (c + 1)], start=(n == 0), stop=(n == 1))
                            last.then_inc(score_ps, 1)
                        for i in jobs_at(s, 0):
                            job(i)
                        c, j = (s - 6) // 3, (s - 6) % 3
                        if 0 <= c < CHUNKS:
                            if j == 0:
                                pe_.wait_ge(probT_sb, 3 * c + 3)
                                if c >= 1:
                                    pe_.wait_ge(oT_ready, c)
                                if c % NC == 0:
                                    pe_.wait_ge(rest_done, splits_through("v", c // NC))
                            par = (c // NC) % 2
                            for kt in range(3 * j, 3 * j + 3):
                                for n, (vp, pp) in enumerate(((v_high, pt_high), (v_high, pt_rest), (v_rest, pt_high))):
                                    last = mm(ps[:, 6 * BANK:6 * BANK + CH], vp[:, par, kt, :],
                                              pp[:, c % 2, CH * kt:CH * (kt + 1)], start=(kt == 0 and n == 0),
                                              stop=(kt == NT - 1 and n == 2))
                            if j == 2:
                                last.then_inc(pv_done, 1)
                        for i in jobs_at(s, 1):
                            job(i)
                        u = s - 2
                        if 0 <= u < UNITS:
                            pe_.wait_ge(prob_ready, u + 1)
                            if u >= 1:
                                pe_.wait_ge(probT_sb, u)
                            for kt in range(NT):
                                at = (3 + kt // 3) * BANK + (kt % 3) * T
                                last = nc.tensor.transpose(ps[0:T, at:at + T], mring[:, u % 3, T * kt:T * (kt + 1)],
                                                           ident[0:T, 0:T])
                            last.then_inc(probT_ps, 1)

                def second_half():
                    normed_T(2)
                    three_chunks(0, w_a1[:, 0, :], xnT).then_inc(q1_ps, 1)
                    three_chunks(3, w_a1[:, 1, :], xnT).then_inc(q1_ps, 1)
                    pe_.wait_ge(q1_act, 1)
                    by_token(0, xnT, w_a1[:, 2, :]).then_inc(q1_ps, 1)
                    if new:
                        pe_.wait_ge(y_added, CHUNKS)
                    pe_.wait_ge(q1_act, 2)
                    pe_.wait_ge(q1_dve, 1)
                    for s in range(NT + 2):
                        if s < NT:
                            if s >= 1:
                                pe_.wait_ge(p1_ready, s)
                            for c0, c1 in ((0, 512), (512, 1024), (1024, SEQ)):
                                last = mm(ps[0:T, c0:c1], q1T[:, T * s:T * (s + 1)], k1T[:, c0:c1])
                            last.then_inc(s1_ps, 1)
                        if s == 0:
                            pe_.wait_ge(ksum_ready, 1)
                            for t in range(NT):
                                last = mm(ps[0:T, 6 * BANK + t:6 * BANK + t + 1], q1T[:, T * t:T * (t + 1)], small[:, 6:7])
                            last.then_inc(rs_ps, 1)
                        u = s - 1
                        if 0 <= u < NT:
                            pe_.wait_ge(p1_ready, u + 1)
                            if u >= 1:
                                pe_.wait_ge(p1T_sb, u)
                            for kt in range(NT):
                                at = (3 + kt // 3) * BANK + (kt % 3) * T
                                last = nc.tensor.transpose(ps[0:T, at:at + T], mring[:, u % 2, T * kt:T * (kt + 1)],
                                                           ident[0:T, 0:T])
                            last.then_inc(p1T_ps, 1)
                        u = s - 2
                        if 0 <= u < NT:
                            pe_.wait_ge(p1T_sb, u + 1)
                            if u == 0:
                                pe_.wait_ge(rs_part, 1)
                            if u >= 2:
                                pe_.wait_ge(o1_read, u - 1)
                            for kt in range(NT):
                                at = (6 + u % 2) * BANK
                                last = mm(ps[0:T, at:at + D], pt1[:, u % 2, kt, :], v1[:, kt, :],
                                          start=(kt == 0), stop=(kt == NT - 1))
                            last.then_inc(o1_ps, 1)
                    if new:
                        normed_T(1)
                    normed_T(3)
                    pe_.wait_ge(mean_ready, 1)
                    mm(ps[0:RH, 6 * BANK:6 * BANK + 1], rw1[:], small[:, 9:10]).then_inc(r1_ps, 1)
                    pe_.wait_ge(r1_ready, 1)
                    mm(ps[0:1, 7 * BANK:7 * BANK + 3], small[0:RH, 10:11], rw2[:]).then_inc(r2_ps, 1)
                    pe_.wait_ge(onehot, 1)
                    mm(ps[:, 6 * BANK:6 * BANK + 3], ones1[:], small[0:1, 50:53]).then_inc(onehot_ps, 1)
                    if new:
                        look_hidden()
                    pe_.wait_ge(wsel_ready, 1)
                    for i in range(8):
                        if i >= 2:
                            pe_.wait_ge(q2_dve, i - 1)
                        w = w_thrice[:, i % 2, i // 2 * 2:i // 2 * 2 + 2, :, :].rearrange("p h r c -> p (h r c)")
                        three_chunks(3 * (i % 2), w, xnT).then_inc(q2_ps, 1)
                    pe_.wait_ge(q2_dve, 7)
                    by_token(0, xnT, w_sel[:, 2 * D:3 * D]).then_inc(q2_ps, 1)
                    pe_.wait_ge(q2_dve, 9)
                    for n in range(PASS1):
                        g, t, j = n // (2 * NT), n // 2 % NT, n % 2
                        r = slice(64 * j, 64 * j + 64)
                        side = 4 * BANK * (n % 2)
                        if n >= 2:
                            pe_.wait_ge(s2_max, n - 1)
                        for c0, w in ((0, BANK), (BANK, BANK), (2 * BANK, SP - 2 * BANK)):
                            last = mm(ps[0:T, side + c0:side + c0 + w], q4[r, g, T * t:T * (t + 1)],
                                      k4[r, g, c0:c0 + w])
                        last.then_inc(s2_ps, 1)
                    pe_.wait_ge(s2_max, PASS1)
                    if new:
                        similarities(0)
                    pe_.wait_ge(m_ready, 1)
                    for g in range(4):
                        if g >= 2:
                            pe_.wait_ge(q2_shift, g - 1)
                        for t in range(NT):
                            at = (3 * (g % 2) + t // 3) * BANK + (t % 3) * T
                            last = nc.tensor.transpose(ps[:, at:at + T], mpad[:, g, t, :], ident[0:T, 0:T])
                        last.then_inc(mT_ps, 1)
                    pe_.wait_ge(q2_shift, 4)


                def values(m):
                    gc, kt = m // NT, m % NT
                    kk = LAST if kt == NT - 1 else T
                    pe_.wait_ge(p3_ready, 2 * m + 2)
                    if kt == 0 and gc >= 1:
                        pe_.wait_ge(o3_sb, gc)
                    for j in range(4):
                        last = mm(ps[32 * j:32 * j + 32, 4 * BANK:4 * BANK + CH],
                                  v2[0:kk, kt, 4 * (gc // NC) + j, :], p2[0:kk, 2 * (m % 2) + j // 2, j % 2, :],
                                  start=(kt == 0), stop=(kt == NT - 1))
                    last.then_inc(pv3_quad, 1)

                def sums(gc):
                    g, c = gc // NC, gc % NC
                    pe_.wait_ge(o3_sb, gc + 1)
                    if gc >= 1:
                        pe_.wait_ge(o3_norm, gc)
                    mm(ps[:, 5 * BANK:5 * BANK + CH], sum_row[:], o2T[:, g, CH * c:CH * (c + 1)]).then_inc(sum_ps, 1)

                def look_hidden():
                    for t in range(NT):
                        at = 7 * BANK + t * NCAND
                        last = mm(ps[0:T, at:at + NCAND], xnT_look[:, T * t:T * (t + 1)], w_down[:])
                    last.then_inc(hexp_ps, 1)

                def similarities(t):
                    if t >= 1:
                        pe_.wait_ge(sim_read, t)
                    else:
                        pe_.wait_ge(gelu_done, 1)
                    for n in range(2):
                        at = (6 + n) * BANK
                        last = mm(ps[0:T, at:at + BANK], xnT_look[:, T * t:T * (t + 1)],
                                  w_sim[:, n * BANK:(n + 1) * BANK])
                    last.then_inc(sim_ps, 1)

                if new:
                    first_half()
                if old:
                    second_half()
                else:
                    pe_.wait_ge(y_added, CHUNKS)
                    normed_T(1)
                    look_hidden()
                if new and not old:
                    similarities(0)
                for m in range(QUADS + 1):
                    if new and m % LOOK_STEP == 2 and m // LOOK_STEP + 1 < NT:
                        similarities(m // LOOK_STEP + 1)
                    if old and m < QUADS:
                        gc, kt = m // NT, m % NT
                        c = gc % NC
                        kk = LAST if kt == NT - 1 else T
                        for n in (2 * m, 2 * m + 1):
                            if n >= 2:
                                pe_.wait_ge(p3_ready, n - 1)
                            for j in range(2):
                                r = slice(64 * j, 64 * j + 64)
                                g = 2 * (gc // NC) + n % 2
                                at = (2 * (n % 2) + j) * BANK
                                last = mm(ps[0:kk, at:at + CH], k4[r, g, T * kt:T * kt + kk],
                                          q4[r, g, CH * c:CH * (c + 1)])
                            last.then_inc(s3_ps, 1)
                    if old and m >= 1:
                        values(m - 1)
                    if old and m > NT and (m - 1) % NT == 1:
                        sums((m - 1) // NT - 1)
                if old:
                    sums(2 * NC - 1)
                if new:
                    patches(1 if old else 2)
                if old:
                    pe_.wait_ge(o3_norm, 2 * NC)
                    for t in range(NT):
                        at = (3 + t // 3) * BANK + (t % 3) * D
                        for g in range(2):
                            last = mm(ps[0:T, at:at + D], o2T[:, g, T * t:T * (t + 1)], wo_sel[:, g, :],
                                      start=(g == 0), stop=(g == 1))
                    last.then_inc(y2_ps, 1)
                if new:
                    pe_.wait_ge(wexp_ready, 1)
                    if old:
                        pe_.wait_ge(round_done, 1)
                    tokens_T(wexp, NCAND, 3).then_inc(wexpT_ps, 1)
                    pe_.wait_ge(wexpT_sb, 1)
                    by_token(3, wexpT, w_up[:]).then_inc(eout_ps, 1)
                end_round(pe_, go_pe)

            one_round(True, False)
            with pe_.Fori(1, B) as b:
                one_round(True, True)
            one_round(False, True)


_INS = ['x', 'cls_tok', 'L0_tok_W', 'L0_attn_Wq', 'L0_attn_Wk', 'L0_attn_Wv', 'L0_attn_Wo', 'L0_attn_bo',
        'L0_attn_gamma', 'L0_attn_beta', 'L0_ffn_W_q', 'L0_ffn_keys', 'L0_ffn_down_embed', 'L0_ffn_up_embed',
        'L1_attn_kernel', 'L1_ffn_r_w1', 'L1_ffn_r_b1', 'L1_ffn_r_w2', 'L1_ffn_r_b2', 'L1_ffn_wq0', 'L1_ffn_wk0',
        'L1_ffn_wv0', 'L1_ffn_wo0', 'L1_ffn_wq1', 'L1_ffn_wk1', 'L1_ffn_wv1', 'L1_ffn_wo1', 'L1_ffn_wq2',
        'L1_ffn_wk2', 'L1_ffn_wv2', 'L1_ffn_wo2']


def position_table():
    position = np.arange(2 * (SEQ - 1), dtype=np.float32)[:, None]
    div_term = np.exp(np.arange(0, D, 2, dtype=np.float32) * (-math.log(10000.0) / D))
    pe = np.zeros((2 * (SEQ - 1), D), dtype=np.float32)
    pe[:, 0::2] = np.sin(position * div_term)
    pe[:, 1::2] = np.cos(position * div_term)
    table = np.zeros((SP, D), np.float32)
    table[1:SEQ] = pe[:SEQ - 1]
    return table


def kernel(**inputs):
    import concourse.bacc as bacc
    from concourse.bass_utils import run_bass_kernel_spmd

    nc = bacc.Bacc("TRN2", target_bir_lowering=False, num_devices=1)
    arrays, aps = {}, {}
    for name in _INS + ['position_table']:
        a = position_table() if name == 'position_table' else np.ascontiguousarray(inputs[name])
        arrays[f"in_{name}"] = a
        aps[name] = nc.dram_tensor(f"in_{name}", a.shape, mybir.dt.from_np(a.dtype), kind="ExternalInput").ap()
    out = nc.dram_tensor("out", (B, SEQ, D), FP32, kind="ExternalOutput").ap()
    a = [aps[n] for n in _INS]
    last = a[19:]
    vit_kernel(nc, *a[:19], [last[0], last[4], last[8]], [last[1], last[5], last[9]],
               [last[2], last[6], last[10]], [last[3], last[7], last[11]], aps['position_table'], out)
    r = run_bass_kernel_spmd(nc, [arrays], core_ids=[0])
    return r.results[0]["out"]
```
